# Optimizing a Trainium2 kernel written in Bass

```python
import numpy as np
import jax
import jax.numpy as jnp

def _softmax(x, axis=-1):
    return jax.nn.softmax(x, axis=axis)

def _gelu(x):
    return jax.nn.gelu(x, approximate=True)

def _silu(x):
    return jax.nn.silu(x)

def _sigmoid(x):
    return jax.nn.sigmoid(x)

def _layernorm(x, axis=-1, eps=1e-05):
    m = jnp.mean(x, axis=axis, keepdims=True)
    v = jnp.var(x, axis=axis, keepdims=True)
    return (x - m) / jnp.sqrt(v + eps)

def _scatter_add(tgt, idx, src, axis=0):
    return tgt.at[idx].add(src)

def _segment_sum(src, seg, n):
    return jax.ops.segment_sum(src, seg, n)
kernel_name = 'mk_vit_tower_d1_tok_img768_r4_505d01'

def setup_inputs(seed: int=0):
    np.random.seed(seed)
    _w = jnp.asarray

    def _rec_inputs():
        import jax
        import jax.numpy as jnp
        _rk = jax.random.key(seed)
        x = 7.57192e-06 + 1.00007 * jax.random.normal(jax.random.fold_in(_rk, 1), (32, 3, 96, 96), jnp.float32)
        return x
    x = _rec_inputs()

    def _L0_tok_setup():
        import jax, jax.numpy as jnp
        import numpy as np
        K = 4
        STRIDE = 4
        EPS = 1e-05
        SLOPE = 0.01

        def conv2d(x, w, b, stride):
            out = jax.lax.conv_general_dilated(x, w, (stride, stride), 'VALID', dimension_numbers=('NCHW', 'OIHW', 'NCHW'))
            return out + b[None, :, None, None]

        def batchnorm(x, g, b, m, v):
            inv = g / jnp.sqrt(v + EPS)
            return x * inv[None, :, None, None] + (b - m * inv)[None, :, None, None]

        def leaky_relu(x):
            return jnp.where(x >= 0, x, SLOPE * x)

        def deform_conv(x, offset, w, b):
            B, C, H, W = x.shape
            Ho, Wo = (offset.shape[2], offset.shape[3])
            KK = K * K
            off = offset.reshape(B, KK, 2, Ho, Wo)
            kh = jnp.repeat(jnp.arange(K), K).astype(x.dtype)
            kw = jnp.tile(jnp.arange(K), K).astype(x.dtype)
            base_y = (jnp.arange(Ho) * STRIDE).astype(x.dtype)
            base_x = (jnp.arange(Wo) * STRIDE).astype(x.dtype)
            py = base_y[None, None, :, None] + kh[None, :, None, None] + off[:, :, 0]
            px = base_x[None, None, None, :] + kw[None, :, None, None] + off[:, :, 1]
            y0 = jnp.floor(py)
            x0 = jnp.floor(px)
            wy = py - y0
            wx = px - x0

            def corner(yc, xc):
                yi = yc.astype(jnp.int32)
                xi = xc.astype(jnp.int32)
                valid = (yi >= 0) & (yi < H) & (xi >= 0) & (xi < W)
                yi = jnp.clip(yi, 0, H - 1)
                xi = jnp.clip(xi, 0, W - 1)
                v = jax.vmap(lambda img, a, c: img[:, a, c])(x, yi, xi)
                return v * valid[:, None].astype(x.dtype)
            v00 = corner(y0, x0)
            v01 = corner(y0, x0 + 1)
            v10 = corner(y0 + 1, x0)
            v11 = corner(y0 + 1, x0 + 1)
            wy_ = wy[:, None]
            wx_ = wx[:, None]
            sampled = v00 * (1 - wy_) * (1 - wx_) + v01 * (1 - wy_) * wx_ + v10 * wy_ * (1 - wx_) + v11 * wy_ * wx_
            out = jnp.einsum('bckhw,ock->bohw', sampled, w.reshape(w.shape[0], C, KK))
            return out + b[None, :, None, None]
        key = jax.random.key(seed)
        ks = jax.random.split(key, 16)
        f32 = jnp.float32
        inp = {'x': jax.random.normal(ks[0], (64, 3, 224, 224), f32), 'stem_w': jax.random.normal(ks[1], (96, 3, 4, 4), f32) * 0.1, 'stem_b': jax.random.normal(ks[2], (96,), f32) * 0.05, 'bn1_g': jax.random.uniform(ks[3], (96,), f32, 0.5, 1.5), 'bn1_b': jax.random.normal(ks[4], (96,), f32) * 0.05, 'bn1_m': jax.random.normal(ks[5], (96,), f32) * 0.05, 'bn1_v': jax.random.uniform(ks[6], (96,), f32, 0.5, 1.5), 'off_w': jax.random.normal(ks[7], (32, 96, 4, 4), f32) * 0.02, 'off_b': jax.random.normal(ks[8], (32,), f32) * 0.02, 'dcn_w': jax.random.normal(ks[9], (192, 96, 4, 4), f32) * 0.05, 'dcn_b': jax.random.normal(ks[10], (192,), f32) * 0.05, 'bn2_g': jax.random.uniform(ks[11], (192,), f32, 0.5, 1.5), 'bn2_b': jax.random.normal(ks[12], (192,), f32) * 0.05, 'bn2_m': jax.random.normal(ks[13], (192,), f32) * 0.05, 'bn2_v': jax.random.uniform(ks[14], (192,), f32, 0.5, 1.5)}
        return inp
    _L0_tok_all = _L0_tok_setup()
    _L0_tok_in = {k: v for k, v in _L0_tok_all.items() if k in ('stem_w', 'stem_b', 'bn1_g', 'bn1_b', 'bn1_m', 'bn1_v', 'off_w', 'off_b', 'dcn_w', 'dcn_b', 'bn2_g', 'bn2_b', 'bn2_m', 'bn2_v')}
    del _L0_tok_all

    def _L0_attn_setup():
        import jax, jax.numpy as jnp
        import numpy as np
        import math
        B, N, C = (8, 1024, 192)
        H = 12
        DH = C // H
        M = 64
        LN_EPS = 1e-05

        def _phi(t, random_features):
            norm_sq = 0.5 * jnp.sum(t * t, axis=-1, keepdims=True)
            proj = jnp.einsum('bhnd,md->bhnm', t, random_features)
            return jnp.exp(proj - norm_sq) * (1.0 / math.sqrt(M))
        key = jax.random.key(seed)
        ks = jax.random.split(key, 7)
        x = jax.random.normal(ks[0], (B, N, C), dtype=jnp.float32)
        W_qkv = jax.random.normal(ks[1], (C, 3 * C), dtype=jnp.float32) * (1.0 / math.sqrt(C))
        W_proj = jax.random.normal(ks[2], (C, C), dtype=jnp.float32) * (1.0 / math.sqrt(C))
        b_proj = jnp.zeros((C,), dtype=jnp.float32)
        gamma = jnp.ones((C,), dtype=jnp.float32)
        beta = jnp.zeros((C,), dtype=jnp.float32)
        random_features = jax.random.normal(ks[3], (M, DH), dtype=jnp.float32) / math.sqrt(DH)
        return {'x': x, 'W_qkv': W_qkv, 'W_proj': W_proj, 'b_proj': b_proj, 'gamma': gamma, 'beta': beta, 'random_features': random_features}
    _L0_attn_all = _L0_attn_setup()
    _L0_attn_in = {k: v for k, v in _L0_attn_all.items() if k in ('W_qkv', 'W_proj', 'b_proj', 'gamma', 'beta', 'random_features')}
    del _L0_attn_all

    def _L0_ffn_setup():
        import jax, jax.numpy as jnp
        import numpy as np
        B, T, H, F, E = (128, 32, 192, 768, 3)
        key = jax.random.key(seed)
        ks = jax.random.split(key, 4)
        s = 0.02
        return {'x': jax.random.normal(ks[0], (B, T, H), jnp.float32), 'Wg': jax.random.normal(ks[1], (E, H), jnp.float32) * s, 'W1': jax.random.normal(ks[2], (E, H, F), jnp.float32) * s, 'b1': jnp.zeros((E, F), jnp.float32), 'W2': jax.random.normal(ks[3], (E, F, H), jnp.float32) * s, 'b2': jnp.zeros((E, H), jnp.float32)}
    _L0_ffn_all = _L0_ffn_setup()
    _L0_ffn_in = {k: v for k, v in _L0_ffn_all.items() if k in ('Wg', 'W1', 'b1', 'W2', 'b2')}
    del _L0_ffn_all
    return {'x': x, 'L0_tok_stem_w': _L0_tok_in['stem_w'], 'L0_tok_stem_b': _L0_tok_in['stem_b'], 'L0_tok_bn1_g': _L0_tok_in['bn1_g'], 'L0_tok_bn1_b': _L0_tok_in['bn1_b'], 'L0_tok_bn1_m': _L0_tok_in['bn1_m'], 'L0_tok_bn1_v': _L0_tok_in['bn1_v'], 'L0_tok_off_w': _L0_tok_in['off_w'], 'L0_tok_off_b': _L0_tok_in['off_b'], 'L0_tok_dcn_w': _L0_tok_in['dcn_w'], 'L0_tok_dcn_b': _L0_tok_in['dcn_b'], 'L0_tok_bn2_g': _L0_tok_in['bn2_g'], 'L0_tok_bn2_b': _L0_tok_in['bn2_b'], 'L0_tok_bn2_m': _L0_tok_in['bn2_m'], 'L0_tok_bn2_v': _L0_tok_in['bn2_v'], 'L0_attn_W_qkv': _L0_attn_in['W_qkv'], 'L0_attn_W_proj': _L0_attn_in['W_proj'], 'L0_attn_b_proj': _L0_attn_in['b_proj'], 'L0_attn_gamma': _L0_attn_in['gamma'], 'L0_attn_beta': _L0_attn_in['beta'], 'L0_attn_random_features': _L0_attn_in['random_features'], 'L0_ffn_Wg': _L0_ffn_in['Wg'], 'L0_ffn_W1': _L0_ffn_in['W1'], 'L0_ffn_b1': _L0_ffn_in['b1'], 'L0_ffn_W2': _L0_ffn_in['W2'], 'L0_ffn_b2': _L0_ffn_in['b2']}

def reference(x, L0_tok_stem_w, L0_tok_stem_b, L0_tok_bn1_g, L0_tok_bn1_b, L0_tok_bn1_m, L0_tok_bn1_v, L0_tok_off_w, L0_tok_off_b, L0_tok_dcn_w, L0_tok_dcn_b, L0_tok_bn2_g, L0_tok_bn2_b, L0_tok_bn2_m, L0_tok_bn2_v, L0_attn_W_qkv, L0_attn_W_proj, L0_attn_b_proj, L0_attn_gamma, L0_attn_beta, L0_attn_random_features, L0_ffn_Wg, L0_ffn_W1, L0_ffn_b1, L0_ffn_W2, L0_ffn_b2):
    import jax
    import jax.numpy as jnp

    def _L0_tok_ref(x, stem_w, stem_b, bn1_g, bn1_b, bn1_m, bn1_v, off_w, off_b, dcn_w, dcn_b, bn2_g, bn2_b, bn2_m, bn2_v):
        import jax, jax.numpy as jnp
        import numpy as np
        K = 4
        STRIDE = 4
        EPS = 1e-05
        SLOPE = 0.01

        def conv2d(x, w, b, stride):
            out = jax.lax.conv_general_dilated(x, w, (stride, stride), 'VALID', dimension_numbers=('NCHW', 'OIHW', 'NCHW'))
            return out + b[None, :, None, None]

        def batchnorm(x, g, b, m, v):
            inv = g / jnp.sqrt(v + EPS)
            return x * inv[None, :, None, None] + (b - m * inv)[None, :, None, None]

        def leaky_relu(x):
            return jnp.where(x >= 0, x, SLOPE * x)

        def deform_conv(x, offset, w, b):
            B, C, H, W = x.shape
            Ho, Wo = (offset.shape[2], offset.shape[3])
            KK = K * K
            off = offset.reshape(B, KK, 2, Ho, Wo)
            kh = jnp.repeat(jnp.arange(K), K).astype(x.dtype)
            kw = jnp.tile(jnp.arange(K), K).astype(x.dtype)
            base_y = (jnp.arange(Ho) * STRIDE).astype(x.dtype)
            base_x = (jnp.arange(Wo) * STRIDE).astype(x.dtype)
            py = base_y[None, None, :, None] + kh[None, :, None, None] + off[:, :, 0]
            px = base_x[None, None, None, :] + kw[None, :, None, None] + off[:, :, 1]
            y0 = jnp.floor(py)
            x0 = jnp.floor(px)
            wy = py - y0
            wx = px - x0

            def corner(yc, xc):
                yi = yc.astype(jnp.int32)
                xi = xc.astype(jnp.int32)
                valid = (yi >= 0) & (yi < H) & (xi >= 0) & (xi < W)
                yi = jnp.clip(yi, 0, H - 1)
                xi = jnp.clip(xi, 0, W - 1)
                v = jax.vmap(lambda img, a, c: img[:, a, c])(x, yi, xi)
                return v * valid[:, None].astype(x.dtype)
            v00 = corner(y0, x0)
            v01 = corner(y0, x0 + 1)
            v10 = corner(y0 + 1, x0)
            v11 = corner(y0 + 1, x0 + 1)
            wy_ = wy[:, None]
            wx_ = wx[:, None]
            sampled = v00 * (1 - wy_) * (1 - wx_) + v01 * (1 - wy_) * wx_ + v10 * wy_ * (1 - wx_) + v11 * wy_ * wx_
            out = jnp.einsum('bckhw,ock->bohw', sampled, w.reshape(w.shape[0], C, KK))
            return out + b[None, :, None, None]
        h = conv2d(x, stem_w, stem_b, 4)
        h = leaky_relu(batchnorm(h, bn1_g, bn1_b, bn1_m, bn1_v))
        offset = conv2d(h, off_w, off_b, 4)
        h = deform_conv(h, offset, dcn_w, dcn_b)
        h = leaky_relu(batchnorm(h, bn2_g, bn2_b, bn2_m, bn2_v))
        B, C, Ho, Wo = h.shape
        return h.reshape(B, C, Ho * Wo).transpose(0, 2, 1)

    def _L0_attn_ref(x, W_qkv, W_proj, b_proj, gamma, beta, random_features):
        import jax, jax.numpy as jnp
        import numpy as np
        import math
        B, N, C = (8, 1024, 192)
        H = 12
        DH = C // H
        M = 64
        LN_EPS = 1e-05

        def _phi(t, random_features):
            norm_sq = 0.5 * jnp.sum(t * t, axis=-1, keepdims=True)
            proj = jnp.einsum('bhnd,md->bhnm', t, random_features)
            return jnp.exp(proj - norm_sq) * (1.0 / math.sqrt(M))
        b, n, c = x.shape
        qkv = (x @ W_qkv).reshape(b, n, 3, H, DH)
        qkv = jnp.transpose(qkv, (2, 0, 3, 1, 4))
        q, k, v = (qkv[0], qkv[1], qkv[2])
        q_p = _phi(q, random_features)
        k_p = _phi(k, random_features)
        kv = jnp.einsum('bhnm,bhnd->bhmd', k_p, v)
        out = jnp.einsum('bhnm,bhmd->bhnd', q_p, kv)
        k_sum = jnp.sum(k_p, axis=2)
        normalizer = jnp.einsum('bhnm,bhm->bhn', q_p, k_sum)[..., None]
        out = out / (normalizer + 1e-06)
        x_attn = jnp.transpose(out, (0, 2, 1, 3)).reshape(b, n, c)
        x_attn = x_attn @ W_proj + b_proj
        y = x + x_attn
        mu = jnp.mean(y, axis=-1, keepdims=True)
        var = jnp.mean(jnp.square(y - mu), axis=-1, keepdims=True)
        return (y - mu) * jax.lax.rsqrt(var + LN_EPS) * gamma + beta

    def _L0_ffn_ref(x, Wg, W1, b1, W2, b2):
        import jax, jax.numpy as jnp
        import numpy as np
        B, T, H, F, E = (128, 32, 192, 768, 3)
        scores = jax.nn.softmax(jnp.mean(x, axis=1) @ Wg.T, axis=-1)
        _, idx = jax.lax.top_k(scores, 1)
        sel = idx[:, 0]
        h = jax.nn.gelu(jnp.einsum('bth,ehf->betf', x, W1) + b1[None, :, None, :], approximate=False)
        y = jnp.einsum('betf,efh->beth', h, W2) + b2[None, :, None, :]
        w = scores * jax.nn.one_hot(sel, E, dtype=scores.dtype)
        out = jnp.einsum('beth,be->bth', y, w)
        return out
    h = _L0_tok_ref(x, L0_tok_stem_w, L0_tok_stem_b, L0_tok_bn1_g, L0_tok_bn1_b, L0_tok_bn1_m, L0_tok_bn1_v, L0_tok_off_w, L0_tok_off_b, L0_tok_dcn_w, L0_tok_dcn_b, L0_tok_bn2_g, L0_tok_bn2_b, L0_tok_bn2_m, L0_tok_bn2_v)
    h = h + _L0_attn_ref(_layernorm(h, axis=-1), L0_attn_W_qkv, L0_attn_W_proj, L0_attn_b_proj, L0_attn_gamma, L0_attn_beta, L0_attn_random_features)
    h = h + _L0_ffn_ref(_layernorm(h, axis=-1), L0_ffn_Wg, L0_ffn_W1, L0_ffn_b1, L0_ffn_W2, L0_ffn_b2)
    return h

_drawn_inputs = setup_inputs


def setup_inputs(seed=0):
    import zlib

    import numpy as np

    out = dict(_drawn_inputs(seed))
    spreads = {'L0_attn_b_proj': (0.0, 0.1),
     'L0_attn_gamma': (1.0, 0.2),
     'L0_attn_beta': (0.0, 0.1),
     'L0_ffn_b1': (0.0, 0.8),
     'L0_ffn_b2': (0.0, 0.375)}
    factors = {'L0_attn_random_features': 3.378, 'L0_ffn_W1': 3.221, 'L0_ffn_W2': 2.885}
    for name, (base, spread) in spreads.items():
        noise = np.random.default_rng([zlib.crc32(name.encode()), seed]).standard_normal(out[name].shape)
        drawn = base * np.exp(spread * noise) if base else spread * noise
        out[name] = jnp.asarray(drawn.astype(out[name].dtype))
    for name, factor in factors.items():
        out[name] = (out[name] * factor).astype(out[name].dtype)
    return out
```

```python
from contextlib import ExitStack

import numpy as np

import concourse.bass as bass
from concourse import mybir

F32 = mybir.dt.float32
I32 = mybir.dt.int32
ALU = mybir.AluOpType
ACT = mybir.ActivationFunctionType
AX = mybir.AxisListType

IMAGES, CIN, SIDE = 32, 3, 96
STRIDE = 4
C1, C2 = 96, 192
GRID = SIDE // STRIDE
OUT_SIDE = GRID // STRIDE
TOK_IMG = OUT_SIDE * OUT_SIDE
TAPS = STRIDE * STRIDE
GROUP = 8
GROUPS = IMAGES // GROUP
SUB = GROUP // 2
ROWS = SUB * GRID
TOK = GROUP * TOK_IMG
SUBTOK = TOK // 2
COLS = TOK * TAPS // 128
FULL = TOK // 128
REST = TOK - 128 * FULL
BATCH = 3
BATCHES = COLS // BATCH
SLOTS = 6
CELL = 4 * C1
PAD = GRID
HEADS, DH, M = 12, 16, 64
PAIRS = HEADS // 2
VW = DH + 1
EXPERTS, FF = 3, 768
FCH = FF // 128
TILES = ((0, 108), (108, 108), (216, 72))
TT = 108
SLOPE = 0.01
EPS = 1e-5


def tables():
    p = np.arange(128)[:, None]
    col = np.arange(COLS)[None, :]
    full = col < FULL * TAPS
    tok = np.where(full, 128 * (col // TAPS) + p, 128 * FULL + p % 32)
    tap = np.where(full, col % TAPS, 4 * (col - FULL * TAPS) + p // 32)
    py, px = tok % TOK_IMG // OUT_SIDE, tok % OUT_SIDE
    point = np.stack([STRIDE * py + tap // STRIDE, STRIDE * px + tap % STRIDE], 2)
    row = PAD + tok // TOK_IMG * GRID * GRID
    r = np.arange(128)[:, None]
    c = np.arange(4 * M)[None, :]
    same_head = (r % 64) // DH == c // M
    head = np.where(r < 64, 1.0, -0.5) * same_head
    t = np.arange(TT)
    same_img = t[:, None] // TOK_IMG == t[None, :] // TOK_IMG
    f = np.float32
    return {
        "ident": np.eye(128, dtype=f),
        "point": point.reshape(128, 2 * COLS).astype(f),
        "row": row.astype(f),
        "head": head.astype(f),
        "own": (t[:, None] // TOK_IMG == np.arange(3)[None, :]).astype(f),
        "mean": (same_img / TOK_IMG).astype(f),
        "fold": (p % 32 == np.arange(32)[None, :]).astype(f),
    }


def build(nc, a, out):
    a = dict(a)
    w = {n.split("_", 2)[2] if n.startswith("L0_") else n: ap for n, ap in a.items()}
    table = nc.dram_tensor("cells", (PAD + GROUP * GRID * GRID, CELL), F32, kind="Internal").ap()
    out_rows = out.rearrange("b t c -> (b t) c")

    with ExitStack() as ctx:
        def sb(name, shape, dt=F32):
            return ctx.enter_context(nc.sbuf_tensor(name, shape, dt))

        def sem(name):
            return ctx.enter_context(nc.semaphore(name))

        ident = sb("ident_sb", [128, 128])
        point = sb("point_sb", [128, 2 * COLS])
        offb = sb("offb_sb", [128, 2 * COLS])
        rowbase = sb("row_sb", [128, COLS])
        own = sb("own_sb", [TT, 3])
        mean = sb("mean_sb", [TT, TT])
        fold = sb("fold_sb", [128, 32])
        headmask = sb("headmask", [64, 4 * M])
        w_stem = sb("w_stem", [96, 2, C1])
        w_off = sb("w_off", [C1, TAPS, 32])
        w_dcn = sb("w_dcn", [C1, TAPS, C2])
        w_qk = sb("w_qk", [96, 2, 6, 2, 64])
        w_v = sb("w_v", [96, 2, C2])
        w_proj = sb("w_proj", [96, 2, C2])
        w_feat = sb("w_feat", [128, 4 * M])
        w_gate = sb("w_gate", [96, 2, EXPERTS])
        w_up = sb("w_up", [96, 2, EXPERTS, FF])
        w_down = sb("w_down", [128, EXPERTS, FCH, C2])
        b_up = sb("b_up", [128, EXPERTS * FCH])
        b_down = sb("b_down", [TT, EXPERTS, C2])
        gamma = sb("gamma_sb", [TT, C2])
        beta = sb("beta_sb", [TT, C2])
        b_proj = sb("b_proj_sb", [TT, C2])
        bn = sb("bn", [96, 5, 3])
        bn_scale = sb("bn_scale", [96, 3])
        bn_bias = sb("bn_bias", [96, 3])
        bn_tmp = sb("bn_tmp", [96, 2, 3])
        bn_nat = sb("bn_nat", [15, 96])
        gate_nat = sb("gate_nat", [EXPERTS, C2])
        bup_nat = sb("bup_nat", [EXPERTS * FCH, 128])
        feat_nat = sb("feat_nat", [M, 4, DH])

        xs = sb("xs", [ROWS, CIN * STRIDE, SIDE])
        xt = sb("xt", [96, GRID // 2, ROWS])
        h = sb("h", [C1, 2, GRID, ROWS])
        ht = sb("ht", [ROWS, GRID + 1, C1])
        xr = ht[:, 0:GRID // 2, :].rearrange("p r c -> p (r c)")
        part = sb("part", [128, TOK])
        pos = sb("pos", [128, 2 * COLS])
        clipped = sb("clipped", [128, 2 * COLS])
        whole_i = sb("whole_i", [128, 2 * COLS], I32)
        whole = sb("whole", [128, 2 * COLS])
        hat = sb("hat", [128, 2 * COLS, 2])
        above = hat[:, :, 0]
        corner = sb("corner", [128, COLS, 2, 2])
        cell_f = sb("cell_f", [128, COLS])
        cell = sb("cell", [128, COLS], I32)
        ring = sb("ring", [128, SLOTS, BATCH, CELL])
        acc = sb("acc", [128, 3, BATCH, C1])
        shared = sb("shared", [128, TAPS * TOK])
        samp = shared[0:C1, :].rearrange("c (k t) -> c k t", k=TAPS)
        QP_END = 3 * HEADS * M + PAIRS * TOK
        kp = shared[0:TT, 0:3 * HEADS * M].rearrange("t (a f) -> t a f", a=3)
        qp = shared[:, 3 * HEADS * M:3 * HEADS * M + PAIRS * TOK].rearrange("f (p t) -> f p t", p=PAIRS)
        h2t = sb("h2t", [96, 2, TOK])
        h2 = sb("h2", [TT, 3, C2])
        xn = sb("xn", [TT, 3, C2])
        lnT = sb("lnT", [96, 2, TOK])
        qk = sb("qk", [128, 6, TOK])
        mv = sb("mv", [TT, 3, 3, HEADS * VW])
        kv = sb("kv", [128, 3, PAIRS, 3, 2 * VW])
        o = sb("o", [TT, 3, PAIRS, 2 * VW])
        den = sb("den", [TT, 3, HEADS])
        xa = shared[0:TT, QP_END:QP_END + 3 * C2].rearrange("t (a c) -> t a c", a=3)
        h3 = sb("h3", [TT, 3, C2])
        xfT = sb("xfT", [96, 2, TOK])
        stats = sb("stats", [TT, 3, 6])
        mvar = sb("mvar", [TT, 3, 2])
        rs_x = sb("rs_x", [TT, 3])
        rs_i = sb("rs_i", [TT, 3], I32)
        rs_t = sb("rs_t", [TT, 3])
        rstd = sb("rstd", [TT, 3])
        rt = sb("rt", [TT, 3, EXPERTS])
        logit = sb("logit", [TT, 3, EXPERTS])
        rmax = sb("rmax", [TT, 3])
        rsum = sb("rsum", [TT, 3])
        prob = sb("prob", [TT, 3, EXPERTS])
        hot = sb("hot", [TT, 3, EXPERTS])
        gates = sb("gates", [TT, 3, EXPERTS])
        hid = sb("hid", [128, 2, FCH, TOK])
        y = sb("y", [TT, 3, C2])

        flat = ring[:, :, :, :].rearrange("p s b c -> p (s b c)")
        dcn_nat = flat[0:96, 0:2 * C1 * TAPS].rearrange("o (m k) -> o m k", m=2)
        off_nat = flat[0:32, 2 * C1 * TAPS:3 * C1 * TAPS]
        stem_nat = flat[0:96, 3 * C1 * TAPS:3 * C1 * TAPS + 192].rearrange("o (x k) -> o x k", x=2)

        ps = [ctx.enter_context(nc.psum_tensor(f"bank{i}", [128, 512], F32)) for i in range(8)]

        ld_stem, ld_small, ld_dcn, ld_attn, ld_ffn = (sem(n) for n in ("ld_stem", "ld_small", "ld_dcn", "ld_attn", "ld_ffn"))
        ld_bn, ld_offb, ld_nat, point_ready = sem("ld_bn"), sem("ld_offb"), sem("ld_nat"), sem("point_ready")
        xn_biased = sem("xn_biased")
        zeroed = sem("zeroed")
        nat_mm, nat_evac = sem("nat_mm"), sem("nat_evac")
        bn_ready, bn_chain, feat_ready = sem("bn_ready"), sem("bn_chain"), sem("feat_ready")
        x_in, x_ready = sem("x_in"), sem("x_ready")
        xt_mm, xh_evac = sem("xt_mm"), sem("xh_evac")
        stem_mm, bn_evac, h_ready = sem("stem_mm"), sem("bn_evac"), sem("h_ready")
        ht_mm, h_stored = sem("ht_mm"), sem("h_stored")
        off_mm, part_ready, off_tok = sem("off_mm"), sem("part_ready"), sem("off_tok")
        idx_chain, idx_ready = sem("idx_chain"), sem("idx_ready")
        gathered = [sem(f"gathered{i}") for i in range(SLOTS)]
        first_corner, comb_chain, combined = sem("first_corner"), sem("comb_chain"), sem("combined")
        samp_mm, samp_evac = sem("samp_mm"), sem("samp_evac")
        dcn_mm, bn2_evac, h2_ready = sem("dcn_mm"), sem("bn2_evac"), sem("h2_ready")
        t1_mm, t1_evac, ln_chain, xn_ready = sem("t1_mm"), sem("t1_evac"), sem("ln_chain"), sem("xn_ready")
        t2_mm, t2_evac = sem("t2_mm"), sem("t2_evac")
        qk_mm, q_copied, q_squared = sem("qk_mm"), sem("q_copied"), sem("q_squared")
        v_mm, v_evac = sem("v_mm"), sem("v_evac")
        feat_mm, exp_done = sem("feat_mm"), sem("exp_done")
        kv_mm, kv_lo, kv_hi = sem("kv_mm"), sem("kv_lo"), sem("kv_hi")
        out_mm, o_chain, o_evac, xa_ready = sem("out_mm"), sem("o_chain"), sem("o_evac"), sem("xa_ready")
        t3_mm, t3_evac = sem("t3_mm"), sem("t3_evac")
        proj_mm, ln2_chain, xf_ready = sem("proj_mm"), sem("ln2_chain"), sem("xf_ready")
        t4_mm, t4_evac = sem("t4_mm"), sem("t4_evac")
        rt_mm, rt_copied, logit_mm = sem("rt_mm"), sem("rt_copied"), sem("logit_mm")
        gate_chain, logit_ready, prob_exp = sem("gate_chain"), sem("logit_ready"), sem("prob_exp")
        up_mm, gelu_done, down_mm, y_added = sem("up_mm"), sem("gelu_done"), sem("down_mm"), sem("y_added")
        stored = sem("stored")
        edges = sem("edges")
        pool_turns, dve_turns = sem("pool_turns"), sem("dve_turns")

        def later(g):
            return not isinstance(g, int) or g > 0

        class Chain:

            def __init__(self, eng, s, g, per):
                self.eng, self.s, self.g, self.per, self.n = eng, s, g, per, 0

            def add(self, ins):
                self.n += 1
                ins.then_inc(self.s, 1)
                return self.n

            def wait(self, n=None):
                self.eng.wait_ge(self.s, self.g * self.per + (self.n if n is None else n))

            def link(self, ins):
                self.add(ins)
                self.wait()

            def end(self):
                assert self.n == self.per, (self.n, self.per)

        def steps(eng, step):
            step(0, False, True)
            with eng.Fori(1, GROUPS - 1) as g:
                step(g, True, True)
            step(GROUPS - 1, True, False)

        block = ctx.enter_context(nc.Block())

        @block.sync
        def _(sp):
            def load_images(g):
                for s in range(2):
                    if s == 1 or later(g):
                        sp.wait_ge(x_ready, 2 * g + s)
                    for b in range(SUB):
                        img = w["x"][bass.ds(g * GROUP + (SUB * s + b), 1)]
                        sp.dma_start(xs[GRID * b:GRID * (b + 1), :, :].rearrange("y (c k) x -> y c (k x)", c=CIN),
                                     img.rearrange("n c (y k) x -> (n y) c (k x)", k=STRIDE)).then_inc(x_in, 16)

            def store_cells(g):
                if later(g):
                    for i in range(SLOTS):
                        sp.wait_ge(gathered[i], 96 * g)
                for s in range(2):
                    sp.wait_ge(xh_evac, 18 * g + 12 + 6 * s)
                    for slot in range(2):
                        first = PAD + s * SUB * GRID * GRID - slot * GRID
                        dst = table[first:first + ROWS * GRID, slot * 2 * C1:(slot + 1) * 2 * C1]
                        src = bass.AP(ht, 0, [[(GRID + 1) * C1, ROWS], [C1, GRID], [1, 2 * C1]])
                        sp.dma_start(dst.rearrange("(p x) c -> p x c", p=ROWS), src).then_inc(h_stored, 16)

            def store_out(g):
                sp.wait_ge(y_added, 9 * (g + 1))
                for t, (t0, n) in enumerate(TILES):
                    sp.dma_start(out_rows[bass.ds(g * TOK + t0, n), :], y[0:n, t, :]).then_inc(stored, 16)

            sp.dma_start(stem_nat[:, 0, 0:48], w["stem_w"].rearrange("o c k l -> o (c k l)")).then_inc(ld_stem, 16)
            sp.dma_start(stem_nat[:, 1, 48:96], w["stem_w"].rearrange("o c k l -> o (c k l)")).then_inc(ld_stem, 16)
            sp.dma_start(ident[:, :], w["ident"]).then_inc(ld_stem, 16)
            load_images(0)
            sp.dma_start(off_nat, w["off_w"].rearrange("o c k l -> o (c k l)")).then_inc(ld_small, 16)
            sp.dma_start(point[:, :], w["point"]).then_inc(ld_small, 16)
            sp.dma_start(rowbase[:, :], w["row"]).then_inc(ld_small, 16)
            sp.dma_start(fold[:, :], w["fold"]).then_inc(ld_small, 16)
            sp.dma_start(headmask[:, :], w["head"][0:64, :]).then_inc(ld_small, 16)
            sp.dma_start(w_feat[64:128, :], w["head"][64:128, :]).then_inc(ld_small, 16)
            sp.dma_start(own[:, :], w["own"]).then_inc(ld_small, 16)
            sp.dma_start(mean[:, :], w["mean"]).then_inc(ld_small, 16)
            sp.wait_ge(zeroed, 4)
            zeros = kv[0:PAD, :, :, :, :].rearrange("p t q i c -> p (t q i c)")[:, 0:2 * C1]
            sp.dma_start(table[0:PAD, 0:2 * C1], zeros).then_inc(edges, 16)
            sp.dma_start(table[GROUP * GRID * GRID:, 2 * C1:], zeros).then_inc(edges, 16)
            sp.dma_start(dcn_nat, w["dcn_w"].rearrange("(m o) c k l -> o m (c k l)", m=2)).then_inc(ld_dcn, 16)
            store_cells(0)
            for n, kt in ((n, kt) for n in range(6) for kt in range(2)):
                for d in range(2):
                    sp.dma_start(w_qk[:, kt, n, d, :], w["W_qkv"][96 * kt:96 * kt + 96, 64 * n:64 * n + 64]).then_inc(ld_attn, 16)
            sp.dma_start(w_v[:, :, :], w["W_qkv"][:, 2 * C2:].rearrange("(t p) n -> p t n", t=2)).then_inc(ld_attn, 16)
            sp.dma_start(w_proj[:, :, :], w["W_proj"].rearrange("(t p) n -> p t n", t=2)).then_inc(ld_attn, 16)
            for dst, name in ((gamma, "gamma"), (beta, "beta"), (b_proj, "b_proj")):
                sp.dma_start(dst[:, :], w[name].partition_broadcast(TT)).then_inc(ld_attn, 16)
            for kt in range(2):
                sp.dma_start(w_up[:, kt, :, :], w["W1"][:, 96 * kt:96 * kt + 96, :].rearrange("e p f -> p e f")).then_inc(ld_ffn, 16)
            for e in range(EXPERTS):
                sp.dma_start(w_down[:, e, :, :], w["W2"][e].rearrange("(f p) n -> p f n", p=128)).then_inc(ld_ffn, 16)
            sp.dma_start(b_down[:, :, :], w["b2"].rearrange("e n -> (e n)").partition_broadcast(TT)).then_inc(ld_ffn, 16)

            def step(g, has_last, has_next):
                if has_next:
                    load_images(g + 1)
                    store_cells(g + 1)
                if has_last:
                    store_out(g - 1)

            steps(sp, step)
            store_out(GROUPS - 1)
            sp.wait_ge(stored, 16 * 3 * GROUPS)

        @block.gpsimd
        def _(pool):
            pool.memset(stem_nat[:, 0, 48:96], 0.0).then_inc(zeroed, 1)
            pool.memset(stem_nat[:, 1, 0:48], 0.0).then_inc(zeroed, 1)
            pool.memset(ht[:, GRID, :], 0.0).then_inc(zeroed, 1)
            pool.memset(kv[:, :, :, :, :], 0.0).then_inc(zeroed, 1)
            pool.memset(mvar[:, :, :], 1.0).then_inc(zeroed, 1)
            pool.memset(logit[:, :, :], 0.0).then_inc(zeroed, 1)

            for i, name in enumerate(("stem_b", "bn1_g", "bn1_b", "bn1_m", "bn1_v")):
                pool.dma_start(bn_nat[3 * i:3 * i + 1, :], w[name].rearrange("(m p) -> m p", m=1)).then_inc(ld_bn, 16)
            for i, name in enumerate(("dcn_b", "bn2_g", "bn2_b", "bn2_m", "bn2_v")):
                pool.dma_start(bn_nat[3 * i + 1:3 * i + 3, :], w[name].rearrange("(m p) -> m p", m=2)).then_inc(ld_bn, 16)
            for t in range(FULL):
                pool.dma_start(offb[:, 32 * t:32 * t + 32], w["off_b"].partition_broadcast(128)).then_inc(ld_offb, 16)
            for q in range(4):
                taps = w["off_b"].rearrange("(j q x) -> j q x", j=4, q=4)[:, q, :]
                pool.dma_start(offb[32 * q:32 * q + 32, 64:72].rearrange("p (j x) -> p j x", j=4),
                               taps.partition_broadcast(32)).then_inc(ld_offb, 16)
            pool.dma_start(gate_nat[:, :], w["Wg"]).then_inc(ld_nat, 16)
            pool.dma_start(bup_nat[:, :], w["b1"].rearrange("e (f p) -> (e f) p", p=128)).then_inc(ld_nat, 16)
            for i in range(4):
                pool.dma_start(feat_nat[:, i, :], w["random_features"]).then_inc(ld_nat, 16)

            def rearrange_rows(g):
                for s in range(2):
                    pool.wait_ge(x_in, 128 * g + 64 * (s + 1))
                    if s == 1:
                        pool.wait_ge(xt_mm, 6 * g + 3)
                    elif later(g):
                        pool.wait_ge(h_stored, 64 * g)
                    pool.sem_inc(pool_turns, 1)
                    pool.tensor_copy(xr.rearrange("p (x r k) -> p x r k", x=GRID, k=STRIDE),
                                     xs[:, :, :].rearrange("p r (x k) -> p x r k", k=STRIDE)).then_inc(x_ready, 1)

            def gather(g):
                pool.wait_ge(idx_ready, 2 * g + 2)
                pool.wait_ge(h_stored, 64 * (g + 1))
                for k in range(BATCHES):
                    if k >= SLOTS:
                        pool.wait_ge(combined, BATCH * (BATCHES * g + (k - SLOTS + 1)))
                    elif later(g):
                        pool.wait_ge(combined, BATCH * (BATCHES * (g - 1) + (k + SLOTS + 1)))
                    pool.sem_inc(pool_turns, 1)
                    for j in range(BATCH):
                        col = BATCH * k + j
                        pool.indirect_dma_start(
                            ring[:, k % SLOTS, j, :], None, table,
                            bass.IndirectOffsetOnAxis(ap=cell[:, col:col + 1], axis=0)).then_inc(gathered[k % SLOTS], 16)

            rearrange_rows(0)
            pool.wait_ge(edges, 32)
            pool.wait_ge(nat_mm, 11)
            gather(0)

            def step(g, has_last, has_next):
                if has_next:
                    rearrange_rows(g + 1)
                    gather(g + 1)

            steps(pool, step)

        @block.tensor
        def _(pe):
            def stem_x(g, s):
                pe.wait_ge(x_ready, 2 * g + s + 1)
                for j in range(3):
                    u = 3 * s + j
                    if u >= 2:
                        pe.wait_ge(xh_evac, 18 * g + (u - 1))
                    elif later(g):
                        pe.wait_ge(bn2_evac, 2 * g)
                    for i in range(4):
                        mm = pe.transpose(ps[u % 2][0:96, ROWS * i:ROWS * (i + 1)], xr[:, 96 * (4 * j + i):96 * (4 * j + i + 1)],
                                          ident[0:ROWS, 0:ROWS])
                    mm.then_inc(xt_mm, 1)

            def stem_products(g, s):
                for i in range(6):
                    n = 6 * s + i
                    pe.wait_ge(xh_evac, 18 * g + (3 * s + i // 2 + 1))
                    if n >= 2:
                        pe.wait_ge(bn_evac, 12 * g + (n - 1))
                    elif later(g):
                        pe.wait_ge(t1_evac, 3 * g)
                    pe.matmul(ps[2 + n % 2][0:C1, 0:4 * ROWS], w_stem[:, i % 2, :],
                              xt[:, 4 * (i // 2):4 * (i // 2) + 4, :], start=True, stop=True).then_inc(stem_mm, 1)

            def stem_rows(g):
                for s in range(2):
                    for j in range(6):
                        u = 6 + 6 * s + j
                        pe.wait_ge(h_ready, 6 * g + (3 * s + j // 2 + 1))
                        pe.wait_ge(xh_evac, 18 * g + (u - 1))
                        for i in range(4):
                            mm = pe.transpose(ps[u % 2][0:ROWS, C1 * i:C1 * (i + 1)], h[:, s, 4 * j + i, :],
                                              ident[0:C1, 0:C1])
                        mm.then_inc(ht_mm, 1)
                    if s == 0 and later(g):
                        pe.wait_ge(t1_evac, 3 * g)
                    for kw in range(STRIDE):
                        for kh in range(STRIDE):
                            rhs = bass.AP(h, s * GRID * ROWS + kw * ROWS + kh,
                                          [[2 * GRID * ROWS, C1], [STRIDE, SUB * OUT_SIDE], [STRIDE * ROWS, OUT_SIDE]])
                            mm = pe.matmul(ps[4][32 * kh:32 * kh + 32, SUBTOK * s:SUBTOK * (s + 1)],
                                           w_off[:, STRIDE * kh + kw, :], rhs,
                                           start=(kw == 0), stop=(kw == STRIDE - 1), skip_group_check=True)
                    mm.then_inc(off_mm, 1)

            def offsets_by_token(g):
                pe.wait_ge(part_ready, g + 1)
                for t in range(FULL):
                    pe.matmul(ps[4][:, TOK + 32 * t:TOK + 32 * t + 32], part[:, 128 * t:128 * t + 128], fold[:, :],
                              start=True, stop=True, skip_group_check=True)
                for q in range(4):
                    mm = pe.matmul(ps[4][32 * q:32 * q + 32, TOK + 64:TOK + 72], part[:, 128 * FULL:TOK],
                                   fold[:, :].rearrange("p (j q x) -> p j q x", j=4, q=4)[:, :, q, :],
                                   start=True, stop=True, skip_group_check=True)
                mm.then_inc(off_tok, 1)

            def dcn(g):
                for k in range(BATCHES):
                    pe.wait_ge(combined, BATCH * (BATCHES * g + k + 1))
                    if k >= 2:
                        pe.wait_ge(samp_evac, BATCHES * g + (k - 1))
                    elif later(g):
                        pe.wait_ge(o_evac, 6 * g)
                        pe.wait_ge(logit_ready, g)
                    for j in range(BATCH):
                        mm = pe.transpose(ps[2 + k % 2][0:C1, 128 * j:128 * (j + 1)], acc[:, k % 3, j, :], ident[:, :])
                    mm.then_inc(samp_mm, 1)
                pe.wait_ge(samp_evac, BATCHES * (g + 1))
                if later(g):
                    pe.wait_ge(t4_evac, 2 * g)
                else:
                    pe.wait_ge(xh_evac, 18)
                for m in range(2):
                    for k in range(TAPS):
                        mm = pe.matmul(ps[m][0:96, 0:TOK], w_dcn[:, k, 96 * m:96 * m + 96], samp[:, k, :],
                                       start=(k == 0), stop=(k == TAPS - 1))
                    mm.then_inc(dcn_mm, 1)

            def tokens(g):
                pe.wait_ge(h2_ready, 2 * (g + 1))
                pe.wait_ge(idx_ready, 2 * g + 2)
                for t, (t0, n) in enumerate(TILES):
                    for m in range(2):
                        mm = pe.transpose(ps[2 + t][0:n, 96 * m:96 * m + 96], h2t[:, m, t0:t0 + n], ident[0:96, 0:96])
                    mm.then_inc(t1_mm, 1)

            def channels(g, src, ready, s):
                for t, (t0, n) in enumerate(TILES):
                    pe.wait_ge(ready, 3 * g + t + 1)
                    for m in range(2):
                        mm = pe.transpose(ps[m][0:96, t0:t0 + n], src[0:n, t, 96 * m:96 * m + 96], ident[0:n, 0:n])
                mm.then_inc(s, 1)

            def qkv(g, has_next):
                pe.wait_ge(t2_evac, 2 * (g + 1))
                for n in range(6):
                    if n >= 3:
                        pe.wait_ge(q_copied, 6 * g + (n - 2))
                        pe.wait_ge(q_squared, 6 * g + (n - 2))
                    elif has_next:
                        pe.wait_ge(idx_ready, 2 * g + 4)
                    else:
                        pe.wait_ge(t1_evac, 3 * (g + 1))
                    for kt in range(2):
                        mm = pe.matmul(ps[2 + n % 3][:, 0:TOK], w_qk[:, kt, n, :, :].rearrange("p d c -> p (d c)"),
                                       lnT[:, kt, :], start=(kt == 0), stop=(kt == 1))
                    mm.then_inc(qk_mm, 1)
                for t, (t0, n) in enumerate(TILES):
                    if t == 2:
                        pe.wait_ge(v_evac, 3 * g + 1)
                    for kt in range(2):
                        mm = pe.matmul(ps[t % 2][0:n, 0:C2], lnT[:, kt, t0:t0 + n], w_v[:, kt, :],
                                       start=(kt == 0), stop=(kt == 1))
                    mm.then_inc(v_mm, 1)

            def features(g):
                pe.wait_ge(q_copied, 6 * (g + 1))
                pe.wait_ge(q_squared, 6 * (g + 1))
                pe.wait_ge(v_evac, 3 * (g + 1))
                for u in range(12):
                    if u >= 4:
                        pe.wait_ge(exp_done, 12 * g + (u - 3))
                    bank = ps[u % 4]
                    if u < 6:
                        t0, n = TILES[u // 2]
                        for j in ((0, 1) if u % 2 == 0 else (2,)):
                            mm = pe.matmul(bank[0:n, 256 * (j % 2):256 * (j % 2) + 256], qk[:, 3 + j, t0:t0 + n],
                                           w_feat[:, :], start=True, stop=True)
                    else:
                        p = u - 6
                        mm = pe.matmul(bank[:, 0:TOK], w_feat[:, 128 * (p % 2):128 * (p % 2) + 128], qk[:, p // 2, :],
                                       start=True, stop=True)
                    mm.then_inc(feat_mm, 1)

            def kv_sums(g):
                pe.wait_ge(exp_done, 12 * g + 10)
                for u in range(6):
                    t, b = u // 2, u % 2
                    n = TILES[t][1]
                    ni = n // TOK_IMG
                    if u >= 3:
                        pe.wait_ge(kv_lo, 6 * g + (u - 2))
                        pe.wait_ge(kv_hi, 6 * g + (u - 2))
                    for i in range(3):
                        p = 3 * b + i
                        mm = pe.matmul(ps[(4, 0, 1)[u % 3]][:, 102 * i:102 * i + 34 * ni], kp[0:n, t, 128 * p:128 * p + 128],
                                       mv[0:n, t, 0:ni, 34 * p:34 * p + 34], start=True, stop=True)
                    mm.then_inc(kv_mm, 1)

            def attend(g):
                pe.wait_ge(exp_done, 12 * (g + 1))
                for u in range(6):
                    t, b = u // 2, u % 2
                    t0, n = TILES[t]
                    ni = n // TOK_IMG
                    pe.wait_ge(kv_lo, 6 * g + (u + 1))
                    pe.wait_ge(kv_hi, 6 * g + (u + 1))
                    if u >= 2:
                        pe.wait_ge(o_evac, 6 * g + (u - 1))
                    for i in range(3):
                        p = 3 * b + i
                        mm = pe.matmul(ps[2 + b][0:n, 102 * i:102 * i + 34 * ni], qp[:, p, t0:t0 + n],
                                       kv[:, t, p, 0:ni, :], start=True, stop=True)
                    mm.then_inc(out_mm, 1)

            def project(g):
                pe.wait_ge(t3_evac, 2 * (g + 1))
                for t, (t0, n) in enumerate(TILES):
                    for kt in range(2):
                        mm = pe.matmul(ps[2 + t][0:n, 0:C2], lnT[:, kt, t0:t0 + n], w_proj[:, kt, :],
                                       start=(kt == 0), stop=(kt == 1))
                    mm.then_inc(proj_mm, 1)

            def route(g):
                pe.wait_ge(t4_evac, 2 * (g + 1))
                for t, (t0, n) in enumerate(TILES):
                    for kt in range(2):
                        mm = pe.matmul(ps[2][0:n, 4 * t:4 * t + 3], xfT[:, kt, t0:t0 + n], w_gate[:, kt, :],
                                       start=(kt == 0), stop=(kt == 1))
                mm.then_inc(rt_mm, 1)
                pe.wait_ge(rt_copied, g + 1)
                for t, (t0, n) in enumerate(TILES):
                    mm = pe.matmul(ps[3][0:n, 4 * t:4 * t + 3], mean[0:n, 0:n], rt[0:n, t, :], start=True, stop=True)
                mm.then_inc(logit_mm, 1)

            def up(g, e):
                if e == 0:
                    pe.wait_ge(t4_evac, 2 * (g + 1))
                for f in range(FCH):
                    n = FCH * e + f
                    if f >= 2:
                        pe.wait_ge(gelu_done, 18 * g + (n - 1))
                    elif f == 0 and (e > 0 or later(g)):
                        pe.wait_ge(y_added, 9 * g + 3 * e)
                    for kt in range(2):
                        mm = pe.matmul(ps[5 + n % 2][:, 0:TOK], w_up[:, kt, e, 128 * f:128 * f + 128], xfT[:, kt, :],
                                       start=(kt == 0), stop=(kt == 1))
                    mm.then_inc(up_mm, 1)

            def down(g, e):
                pe.wait_ge(gelu_done, 18 * g + 6 * (e + 1))
                for t, (t0, n) in enumerate(TILES):
                    for f in range(FCH):
                        mm = pe.matmul(ps[(7, 5, 6)[t]][0:n, 0:C2], hid[:, e % 2, f, t0:t0 + n],
                                       w_down[:, e, f, :], start=(f == 0), stop=(f == FCH - 1))
                    mm.then_inc(down_mm, 1)

            pe.wait_ge(ld_stem, 48)
            pe.wait_ge(zeroed, 2)
            pe.wait_ge(ld_bn, 16 * 10)
            pe.transpose(ps[5][0:96, 192:207], bn_nat[:, :], ident[0:15, 0:15])
            for i in range(2):
                mm = pe.transpose(ps[5][0:96, 96 * i:96 * i + 96], stem_nat[:, i, :], ident[0:96, 0:96])
            mm.then_inc(nat_mm, 1)
            pe.wait_ge(ld_small, 16 * 8)
            for k in range(TAPS):
                mm = pe.transpose(ps[6][0:C1, 32 * k:32 * k + 32],
                                  off_nat.rearrange("o (c k) -> o c k", k=TAPS)[:, :, k], ident[0:32, 0:32])
            mm.then_inc(nat_mm, 1)
            pe.wait_ge(ld_nat, 16 * 6)
            for kt in range(2):
                pe.transpose(ps[7][0:96, 4 * kt:4 * kt + 3], gate_nat[:, 96 * kt:96 * kt + 96], ident[0:3, 0:3])
            pe.transpose(ps[7][:, 32:32 + EXPERTS * FCH], bup_nat[:, :], ident[0:18, 0:18])
            pe.transpose(ps[7][0:64, 64:128], feat_nat[:, :, :].rearrange("m h d -> m (h d)"),
                         ident[0:64, 0:64]).then_inc(nat_mm, 1)
            pe.wait_ge(nat_evac, 1)
            for s in range(2):
                stem_x(0, s)
                stem_products(0, s)
            pe.wait_ge(nat_evac, 2)
            stem_rows(0)
            offsets_by_token(0)
            pe.wait_ge(ld_dcn, 16)
            for u in range(8):
                m, k0 = u // 4, 4 * (u % 4)
                pe.wait_ge(nat_evac, u + 3 if u < 2 else u + 2)
                if u == 0:
                    pe.wait_ge(nat_evac, 3)
                for i in range(4):
                    mm = pe.transpose(ps[5 + u % 3][0:C1, 96 * i:96 * i + 96],
                                      dcn_nat[:, m, :].rearrange("o (c k) -> o c k", k=TAPS)[:, :, k0 + i], ident[0:96, 0:96])
                mm.then_inc(nat_mm, 1)
            pe.wait_ge(nat_evac, 11)
            pe.wait_ge(ld_attn, 16 * 29)
            pe.wait_ge(ld_ffn, 16 * 6)
            pe.wait_ge(feat_ready, 1)

            def step(g, has_last, has_next):
                dcn(g)
                if has_next:
                    stem_x(g + 1, 0)
                tokens(g)
                if has_next:
                    stem_products(g + 1, 0)
                    stem_x(g + 1, 1)
                    stem_products(g + 1, 1)
                    stem_rows(g + 1)
                if has_next:
                    pe.wait_ge(xh_evac, 18 * (g + 2))
                channels(g, xn, xn_ready, t2_mm)
                if has_next:
                    offsets_by_token(g + 1)
                if has_last:
                    up(g - 1, 0)
                qkv(g, has_next)
                if has_last:
                    down(g - 1, 0)
                features(g)
                if has_last:
                    up(g - 1, 1)
                kv_sums(g)
                attend(g)
                if has_last:
                    down(g - 1, 1)
                channels(g, xa, xa_ready, t3_mm)
                project(g)
                if has_last:
                    up(g - 1, 2)
                    down(g - 1, 2)
                channels(g, xa, xf_ready, t4_mm)
                route(g)

            steps(pe, step)
            for e in range(EXPERTS):
                up(GROUPS - 1, e)
                down(GROUPS - 1, e)

        @block.scalar
        def _(act):
            def stem_bn(g):
                for s in range(2):
                    if later(g):
                        act.wait_ge(off_mm, 2 * (g - 1) + (s + 1))
                    for i in range(6):
                        n = 6 * s + i
                        act.wait_ge(stem_mm, 12 * g + n + 1)
                        first = 8 * (i // 2) + i % 2
                        act.activation(h[:, s, first:first + 7:2, :], ps[2 + n % 2][0:C1, 0:4 * ROWS], ACT.Identity,
                                       bias=bn_bias[:, 0:1], scale=bn_scale[:, 0:1]).then_inc(bn_evac, 1)

            def first_corners(g, k):
                act.wait_ge(gathered[k % SLOTS], 96 * g + 48 * (k // SLOTS + 1))
                if k >= 3:
                    act.wait_ge(samp_mm, BATCHES * g + (k - 2))
                elif later(g):
                    act.wait_ge(samp_mm, BATCHES * g)
                for j in range(BATCH):
                    ins = act.activation(acc[:, k % 3, j, :], ring[:, k % SLOTS, j, 0:C1], ACT.Copy,
                                         scale=corner[:, BATCH * k + j, 0, 0:1])
                ins.then_inc(first_corner, 1)

            def samp_copy(g, k):
                act.wait_ge(samp_mm, BATCHES * g + k + 1)
                bank = ps[2 + k % 2]
                col, pieces = BATCH * k, []
                while col < BATCH * (k + 1):
                    t = col // TAPS
                    run = min(BATCH * (k + 1), TAPS * (t + 1)) - col
                    src = bank[0:C1, 128 * (col - BATCH * k):128 * (col - BATCH * k + run)]
                    if t < FULL:
                        pieces.append((samp[:, col - TAPS * t:col - TAPS * t + run, 128 * t:128 * t + 128],
                                       src.rearrange("c (r t) -> c r t", r=run)))
                    else:
                        k0 = 4 * (col - TAPS * FULL)
                        pieces.append((samp[:, k0:k0 + 4 * run, 128 * FULL:TOK], src.rearrange("c (r t) -> c r t", r=4 * run)))
                    col += run
                for dst, src in pieces:
                    ins = act.activation(dst, src, ACT.Copy)
                ins.then_inc(samp_evac, 1)

            def combine(g):
                act.wait_ge(idx_ready, 2 * g + 2)
                if later(g):
                    act.wait_ge(out_mm, 6 * g)
                first_corners(g, 0)
                for k in range(BATCHES):
                    if k + 1 < BATCHES:
                        first_corners(g, k + 1)
                    samp_copy(g, k)

            def dcn_bn(g):
                if later(g):
                    act.wait_ge(t1_mm, 3 * g)
                for m in range(2):
                    act.wait_ge(dcn_mm, 2 * g + m + 1)
                    act.activation(h2t[:, m, :], ps[m][0:96, 0:TOK], ACT.Identity,
                                   bias=bn_bias[:, 1 + m:2 + m], scale=bn_scale[:, 1 + m:2 + m]).then_inc(bn2_evac, 1)

            def copy_banks(g, s, dst, done):
                act.wait_ge(s, g + 1)
                for m in range(2):
                    act.activation(dst[:, m, :], ps[m][0:96, 0:TOK], ACT.Copy).then_inc(done, 1)

            def squares(g):
                for n in range(6):
                    act.wait_ge(qk_mm, 6 * g + n + 1)
                    act.activation(qk[64:128, n, :], ps[2 + n % 3][64:128, 0:TOK], ACT.Square).then_inc(q_squared, 1)

            def exps(g):
                for u in range(12):
                    act.wait_ge(feat_mm, 12 * g + u + 1)
                    bank = ps[u % 4]
                    if u < 6:
                        n = TILES[u // 2][1]
                        w0, w1 = (0, 512) if u % 2 == 0 else (512, 768)
                        act.activation(kp[0:n, u // 2, w0:w1], bank[0:n, 0:w1 - w0], ACT.Exp).then_inc(exp_done, 1)
                    else:
                        act.activation(qp[:, u - 6, :], bank[:, 0:TOK], ACT.Exp).then_inc(exp_done, 1)

            def kv_high(g):
                for u in range(6):
                    t, b = u // 2, u % 2
                    ni = TILES[t][1] // TOK_IMG
                    act.wait_ge(kv_mm, 6 * g + u + 1)
                    src = ps[(4, 0, 1)[u % 3]][64:128, 0:306].rearrange("f (p i c) -> f p i c", p=3, i=3)
                    act.activation(kv[64:128, t, 3 * b:3 * b + 3, 0:ni, VW:2 * VW], src[:, :, 0:ni, VW:2 * VW],
                                   ACT.Copy).then_inc(kv_hi, 1)

            def gelus(g, e):
                if e >= 2:
                    act.wait_ge(down_mm, 9 * g + 3 * (e - 1))
                elif later(g):
                    act.wait_ge(down_mm, 9 * g)
                for f in range(FCH):
                    n = FCH * e + f
                    act.wait_ge(up_mm, 18 * g + n + 1)
                    act.activation(hid[:, e % 2, f, :], ps[5 + n % 2][:, 0:TOK], ACT.Gelu,
                                   bias=b_up[:, n:n + 1]).then_inc(gelu_done, 1)

            def prob_exps(g):
                act.wait_ge(logit_ready, g + 1)
                act.activation(prob[:, :, :], logit[:, :, :], ACT.Exp).then_inc(prob_exp, 1)

            act.wait_ge(bn_ready, 1)
            stem_bn(0)
            act.wait_ge(zeroed, 6)
            act.wait_ge(feat_ready, 1)

            def step(g, has_last, has_next):
                combine(g)
                dcn_bn(g)
                if has_next:
                    stem_bn(g + 1)
                copy_banks(g, t2_mm, lnT, t2_evac)
                if has_last:
                    gelus(g - 1, 0)
                squares(g)
                exps(g)
                if has_last:
                    gelus(g - 1, 1)
                kv_high(g)
                copy_banks(g, t3_mm, lnT, t3_evac)
                if has_last:
                    gelus(g - 1, 2)
                copy_banks(g, t4_mm, xfT, t4_evac)
                prob_exps(g)

            steps(act, step)
            for e in range(EXPERTS):
                gelus(GROUPS - 1, e)

        @block.vector
        def _(dve):
            def rsqrt(chain, dst, x, ti, tt):
                chain.link(dve.tensor_scalar(ti.bitcast(I32) if ti.dtype != I32 else ti, x.bitcast(I32), 1, None, ALU.logical_shift_right))
                chain.link(dve.tensor_scalar(dst.bitcast(I32), ti, -1.0, float(0x5F3759DF), ALU.mult, ALU.add))
                for _ in range(3):
                    chain.link(dve.tensor_tensor(tt, dst, dst, ALU.mult))
                    chain.link(dve.scalar_tensor_tensor(tt, tt, -0.5, x, ALU.mult, ALU.mult))
                    chain.link(dve.scalar_tensor_tensor(dst, tt, 1.5, dst, ALU.add, ALU.mult))

            RSQRT = 11

            def stem_xt(g, s):
                if s == 1 or later(g):
                    dve.wait_ge(stem_mm, 12 * g + 6 * s)
                for j in range(3):
                    u = 3 * s + j
                    dve.wait_ge(xt_mm, 6 * g + u + 1)
                    dve.tensor_copy(xt[:, 4 * j:4 * j + 4, :], ps[u % 2][0:96, 0:4 * ROWS]).then_inc(xh_evac, 1)

            def leaky(g, s):
                for j in range(3):
                    dve.wait_ge(bn_evac, 12 * g + 6 * s + 2 * (j + 1))
                    part_h = h[:, s, 8 * j:8 * j + 8, :]
                    dve.scalar_tensor_tensor(part_h, part_h, SLOPE, part_h, ALU.mult, ALU.max).then_inc(h_ready, 1)

            def stem_ht(g, s):
                if s == 1:
                    dve.wait_ge(h_stored, 64 * g + 32)
                elif later(g):
                    dve.wait_ge(h_stored, 64 * g)
                for j in range(6):
                    u = 6 + 6 * s + j
                    dve.wait_ge(ht_mm, 12 * g + 6 * s + j + 1)
                    dve.tensor_copy(ht[:, 4 * j:4 * j + 4, :], ps[u % 2][0:ROWS, 0:4 * C1]).then_inc(xh_evac, 1)

            def part_copy(g):
                dve.wait_ge(off_mm, 2 * (g + 1))
                dve.tensor_copy(part[:, :], ps[4][:, 0:TOK]).then_inc(part_ready, 1)

            def sample_points(g):
                dve.wait_ge(off_tok, g + 1)
                chain = Chain(dve, idx_chain, g, 11)
                chain.link(dve.tensor_tensor(pos[:, :], ps[4][:, TOK:TOK + 2 * COLS], point[:, :], ALU.add))
                chain.link(dve.tensor_scalar(clipped[:, :], pos[:, :], 0.0, float(GRID - 2), ALU.max, ALU.min))
                chain.link(dve.tensor_copy(whole_i[:, :], clipped[:, :]))
                chain.link(dve.tensor_copy(whole[:, :], whole_i[:, :]))
                chain.link(dve.tensor_tensor(above, whole[:, :], clipped[:, :], ALU.is_gt))
                chain.link(dve.tensor_tensor(whole[:, :], whole[:, :], above, ALU.subtract))
                wh = whole[:, :].rearrange("p (c x) -> p c x", x=2)
                chain.add(dve.scalar_tensor_tensor(cell_f[:, :], wh[:, :, 0], float(GRID), wh[:, :, 1], ALU.mult, ALU.add))
                chain.link(dve.tensor_tensor(hat[:, :, 0], pos[:, :], whole[:, :], ALU.subtract))
                chain.link(dve.tensor_scalar(hat[:, :, 1], hat[:, :, 0], -1.0, None, ALU.add))
                chain.link(dve.scalar_tensor_tensor(hat[:, :, :], hat[:, :, :], -1.0, hat[:, :, :], ALU.mult, ALU.min))
                chain.link(dve.tensor_scalar(hat[:, :, :], hat[:, :, :], 1.0, 0.0, ALU.add, ALU.max))
                hv = hat[:, :, :].rearrange("p (c x) k -> p c x k", x=2)
                hy = hv[:, :, 0, :].unsqueeze(3).to_broadcast([128, COLS, 2, 2])
                hx = hv[:, :, 1, :].unsqueeze(2).to_broadcast([128, COLS, 2, 2])
                dve.tensor_tensor(cell[:, :], cell_f[:, :], rowbase[:, :], ALU.add).then_inc(idx_ready, 1)
                dve.tensor_tensor(corner[:, :, :, :], hy, hx, ALU.mult).then_inc(idx_ready, 1)
                chain.end()

            def combine(g):
                chain = Chain(dve, comb_chain, g, 2 * BATCH * BATCHES)
                for k in range(BATCHES):
                    dve.wait_ge(first_corner, BATCHES * g + k + 1)
                    for c in range(1, 4):
                        for j in range(BATCH):
                            if c > 1:
                                chain.wait(2 * BATCH * k + BATCH * (c - 2) + j + 1)
                            dst = acc[:, k % 3, j, :]
                            ins = dve.scalar_tensor_tensor(dst, ring[:, k % SLOTS, j, C1 * c:C1 * (c + 1)],
                                                           corner[:, BATCH * k + j, c // 2, c % 2:c % 2 + 1], dst,
                                                           ALU.mult, ALU.add)
                            if c < 3:
                                chain.add(ins)
                            else:
                                ins.then_inc(combined, 1)
                chain.end()

            def dcn_leaky(g):
                for m in range(2):
                    dve.wait_ge(bn2_evac, 2 * g + m + 1)
                    part_h = h2t[:, m, :]
                    dve.scalar_tensor_tensor(part_h, part_h, SLOPE, part_h, ALU.mult, ALU.max).then_inc(h2_ready, 1)

            def moments(chain, src):
                for t, (t0, n) in enumerate(TILES):
                    chain.add(dve.bn_stats(stats[0:n, t, :], src[0:n, t, :]))
                chain.wait()
                dve.sem_inc(dve_turns, 1)
                for t, (t0, n) in enumerate(TILES):
                    chain.add(dve.bn_aggr(mvar[0:n, t, :], stats[0:n, t, :]))
                chain.wait()
                chain.link(dve.tensor_scalar(rs_x[:, :], mvar[:, :, 1], EPS, None, ALU.add))
                rsqrt(chain, rstd[:, :], rs_x[:, :], rs_i[:, :], rs_t[:, :])

            MOMENTS = 7 + RSQRT

            def norm(t, n, dst, src):
                return dve.tensor_scalar(dst[0:n, t, :], src[0:n, t, :], mvar[0:n, t, 0:1], rstd[0:n, t:t + 1],
                                         ALU.subtract, ALU.mult)

            def norm_in(g):
                chain = Chain(dve, ln_chain, g, MOMENTS + 3)
                for t, (t0, n) in enumerate(TILES):
                    dve.wait_ge(t1_mm, 3 * g + t + 1)
                    dve.tensor_copy(h2[0:n, t, :], ps[2 + t][0:n, 0:C2]).then_inc(t1_evac, 1)
                dve.wait_ge(t1_evac, 3 * (g + 1))
                moments(chain, h2)
                for t, (t0, n) in enumerate(TILES):
                    norm(t, n, xn, h2).then_inc(xn_ready, 1)
                dve.wait_ge(xn_ready, 3 * (g + 1))
                for t, (t0, n) in enumerate(TILES):
                    chain.link(dve.tensor_tensor(h2[0:n, t, :], h2[0:n, t, :], beta[0:n, :], ALU.add))
                chain.end()

            def q_copies(g):
                for n in range(6):
                    dve.wait_ge(qk_mm, 6 * g + n + 1)
                    dve.tensor_copy(qk[0:64, n, :], ps[2 + n % 3][0:64, 0:TOK]).then_inc(q_copied, 1)

            def values(g):
                for t, (t0, n) in enumerate(TILES):
                    dve.wait_ge(v_mm, 3 * g + t + 1)
                    for i in range(n // TOK_IMG):
                        dst = mv[0:n, t, i, :].rearrange("t (h c) -> t h c", c=VW)[:, :, 0:DH]
                        ins = dve.tensor_scalar(dst, ps[t % 2][0:n, 0:C2].rearrange("t (h c) -> t h c", c=DH),
                                                own[0:n, i:i + 1], None, ALU.mult)
                    ins.then_inc(v_evac, 1)

            def add_proj_bias(g):
                dve.wait_ge(t2_mm, g + 1)
                for t, (t0, n) in enumerate(TILES):
                    ins = dve.tensor_tensor(xn[0:n, t, :], xn[0:n, t, :], b_proj[0:n, :], ALU.add)
                ins.then_inc(xn_biased, 1)

            def kv_low(g):
                for u in range(6):
                    t, b = u // 2, u % 2
                    ni = TILES[t][1] // TOK_IMG
                    dve.wait_ge(kv_mm, 6 * g + u + 1)
                    src = ps[(4, 0, 1)[u % 3]][0:64, 0:306].rearrange("f (p i c) -> f p i c", p=3, i=3)
                    dve.tensor_copy(kv[0:64, t, 3 * b:3 * b + 3, 0:ni, 0:VW], src[:, :, 0:ni, 0:VW]).then_inc(kv_lo, 1)

            def outputs(g):
                chain = Chain(dve, o_chain, g, 10 + 6)
                for u in range(6):
                    t, b = u // 2, u % 2
                    n = TILES[t][1]
                    dve.wait_ge(out_mm, 6 * g + u + 1)
                    src = ps[2 + b][0:n, 0:306].rearrange("t (p i c) -> t p i c", p=3, i=3)
                    dst = o[0:n, t, 3 * b:3 * b + 3, :]
                    chain.link(dve.tensor_scalar(dst, src[:, :, 0, :], own[0:n, 0:1], None, ALU.mult))
                    images = n // TOK_IMG
                    for i in range(1, images):
                        ins = dve.scalar_tensor_tensor(dst, src[:, :, i, :], own[0:n, i:i + 1], dst, ALU.mult, ALU.add)
                        if i < images - 1:
                            chain.link(ins)
                    ins.then_inc(o_evac, 1)
                    if b == 1:
                        dve.wait_ge(o_evac, 6 * g + (u + 1))
                        ov = o[0:n, t, :, :].rearrange("t p (h c) -> t (p h) c", c=VW)
                        chain.link(dve.tensor_scalar(den[0:n, t, :], ov[:, :, DH], M * 1e-6, None, ALU.add))
                        chain.link(dve.reciprocal(den[0:n, t, :], den[0:n, t, :]))
                        dve.tensor_tensor(xa[0:n, t, :].rearrange("t (h c) -> t h c", c=DH), ov[:, :, 0:DH],
                                          den[0:n, t, :].unsqueeze(2).to_broadcast([n, HEADS, DH]),
                                          ALU.mult).then_inc(xa_ready, 1)
                chain.end()

            def norms_out(g):
                chain = Chain(dve, ln2_chain, g, 2 * MOMENTS + 12)
                dve.wait_ge(xn_biased, g + 1)
                for t, (t0, n) in enumerate(TILES):
                    dve.wait_ge(proj_mm, 3 * g + t + 1)
                    chain.link(dve.tensor_tensor(xn[0:n, t, :], ps[2 + t][0:n, 0:C2], xn[0:n, t, :], ALU.add))
                moments(chain, xn)
                for t, (t0, n) in enumerate(TILES):
                    chain.link(norm(t, n, h3, xn))
                    chain.link(dve.tensor_tensor(h3[0:n, t, :], h3[0:n, t, :], gamma[0:n, :], ALU.mult))
                    chain.link(dve.tensor_tensor(h3[0:n, t, :], h3[0:n, t, :], h2[0:n, t, :], ALU.add))
                moments(chain, h3)
                for t, (t0, n) in enumerate(TILES):
                    norm(t, n, xa, h3).then_inc(xf_ready, 1)
                chain.end()

            def gate(g):
                dve.wait_ge(rt_mm, g + 1)
                for t, (t0, n) in enumerate(TILES):
                    ins = dve.tensor_copy(rt[0:n, t, :], ps[2][0:n, 4 * t:4 * t + 3])
                ins.then_inc(rt_copied, 1)
                chain = Chain(dve, gate_chain, g, 3 + 1 + 9 + 9)
                dve.wait_ge(logit_mm, g + 1)
                for t, (t0, n) in enumerate(TILES):
                    chain.add(dve.tensor_copy(logit[0:n, t, :], ps[3][0:n, 4 * t:4 * t + 3]))
                chain.wait()
                chain.link(dve.tensor_reduce(rmax[:, :], logit[:, :, :], AX.X, ALU.max))
                dve.tensor_tensor(logit[:, :, :], logit[:, :, :], rmax[:, :].unsqueeze(2).to_broadcast([TT, 3, EXPERTS]),
                                  ALU.subtract).then_inc(logit_ready, 1)
                dve.wait_ge(prob_exp, g + 1)
                chain.link(dve.tensor_reduce(rsum[:, :], prob[:, :, :], AX.X, ALU.add))
                chain.link(dve.reciprocal(rsum[:, :], rsum[:, :]))
                chain.link(dve.tensor_tensor(prob[:, :, :], prob[:, :, :], rsum[:, :].unsqueeze(2).to_broadcast([TT, 3, EXPERTS]), ALU.mult))
                chain.link(dve.tensor_reduce(rmax[:, :], prob[:, :, :], AX.X, ALU.max))
                chain.link(dve.tensor_tensor(hot[:, :, :], prob[:, :, :], rmax[:, :].unsqueeze(2).to_broadcast([TT, 3, EXPERTS]), ALU.is_ge))
                chain.link(dve.tensor_tensor(hot[:, :, 1], hot[:, :, 1], hot[:, :, 0], ALU.is_gt))
                chain.link(dve.tensor_tensor(rmax[:, :], hot[:, :, 0], hot[:, :, 1], ALU.add))
                chain.link(dve.tensor_tensor(hot[:, :, 2], hot[:, :, 2], rmax[:, :], ALU.is_gt))
                chain.link(dve.tensor_tensor(gates[:, :, :], prob[:, :, :], hot[:, :, :], ALU.mult))
                for e in range(EXPERTS):
                    for t, (t0, n) in enumerate(TILES):
                        chain.link(dve.scalar_tensor_tensor(h3[0:n, t, :], b_down[0:n, e, :], gates[0:n, t, e:e + 1],
                                                            h3[0:n, t, :], ALU.mult, ALU.add))
                chain.end()

            def add_expert(g, e):
                if e == 0 and later(g):
                    dve.wait_ge(stored, 48 * g)
                for t, (t0, n) in enumerate(TILES):
                    u = 3 * e + t
                    dve.wait_ge(down_mm, 9 * g + u + 1)
                    if e > 0:
                        dve.wait_ge(y_added, 9 * g + (u - 2))
                    dve.scalar_tensor_tensor(y[0:n, t, :], ps[(7, 5, 6)[t]][0:n, 0:C2], gates[0:n, t, e:e + 1],
                                             (h3 if e == 0 else y)[0:n, t, :], ALU.mult, ALU.add).then_inc(y_added, 1)

            dve.wait_ge(nat_mm, 1)
            dve.tensor_copy(w_stem[:, :, :], ps[5][0:96, 0:192]).then_inc(nat_evac, 1)
            chain = Chain(dve, bn_chain, 0, 2 + RSQRT + 3)
            chain.link(dve.tensor_copy(bn[:, :, :], ps[5][0:96, 192:207]))
            chain.link(dve.tensor_scalar(bn_tmp[:, 0, :], bn[:, 4, :], EPS, None, ALU.add))
            rsqrt(chain, bn_scale[:, :], bn_tmp[:, 0, :], bn_tmp[:, 1, :].bitcast(I32), bn_bias[:, :])
            chain.link(dve.tensor_tensor(bn_scale[:, :], bn_scale[:, :], bn[:, 1, :], ALU.mult))
            chain.link(dve.tensor_tensor(bn_bias[:, :], bn[:, 0, :], bn[:, 3, :], ALU.subtract))
            chain.link(dve.tensor_tensor(bn_bias[:, :], bn_bias[:, :], bn_scale[:, :], ALU.mult))
            dve.tensor_tensor(bn_bias[:, :], bn_bias[:, :], bn[:, 2, :], ALU.add).then_inc(bn_ready, 1)
            chain.end()
            dve.wait_ge(nat_mm, 2)
            dve.tensor_copy(w_off[:, :, :], ps[6][0:C1, 0:512]).then_inc(nat_evac, 1)
            dve.wait_ge(nat_mm, 3)
            dve.wait_ge(ld_small, 16 * 8)
            dve.tensor_copy(w_gate[:, :, :], ps[7][0:96, 0:8].rearrange("p (t e) -> p t e", t=2)[:, :, 0:3])
            dve.tensor_copy(b_up[:, :], ps[7][:, 32:32 + EXPERTS * FCH])
            dve.tensor_tensor(w_feat[0:64, :].rearrange("p (h m) -> p h m", h=4),
                              ps[7][0:64, 64:128].unsqueeze(1).to_broadcast([64, 4, M]),
                              headmask[:, :].rearrange("p (h m) -> p h m", h=4), ALU.mult).then_inc(nat_evac, 1)
            stem_xt(0, 0)
            stem_xt(0, 1)
            dve.wait_ge(zeroed, 6)
            for s in range(2):
                leaky(0, s)
                stem_ht(0, s)
            part_copy(0)
            dve.wait_ge(ld_offb, 16 * 6)
            dve.tensor_tensor(point[:, :], point[:, :], offb[:, :], ALU.add).then_inc(point_ready, 1)
            dve.wait_ge(point_ready, 1)
            sample_points(0)
            for t in range(3):
                ones = mv[:, t, :, :].rearrange("t i (h c) -> t i h c", c=VW)[:, :, :, DH]
                ins = dve.tensor_copy(ones, own[:, :].unsqueeze(2).to_broadcast([TT, 3, HEADS]))
            ins.then_inc(feat_ready, 1)
            for u in range(8):
                m, k0 = u // 4, 4 * (u % 4)
                dve.wait_ge(nat_mm, u + 4)
                dve.tensor_copy(w_dcn[:, k0:k0 + 4, 96 * m:96 * m + 96],
                                ps[5 + u % 3][0:C1, 0:384].rearrange("c (k o) -> c k o", k=4)).then_inc(nat_evac, 1)
            dve.wait_ge(ld_attn, 16 * 29)
            dve.wait_ge(ld_ffn, 16 * 6)

            def step(g, has_last, has_next):
                combine(g)
                dcn_leaky(g)
                if has_next:
                    stem_xt(g + 1, 0)
                norm_in(g)
                if has_next:
                    stem_xt(g + 1, 1)
                    for s in range(2):
                        leaky(g + 1, s)
                        stem_ht(g + 1, s)
                    part_copy(g + 1)
                    sample_points(g + 1)
                add_proj_bias(g)
                q_copies(g)
                values(g)
                if has_last:
                    add_expert(g - 1, 0)
                kv_low(g)
                outputs(g)
                if has_last:
                    add_expert(g - 1, 1)
                norms_out(g)
                if has_last:
                    add_expert(g - 1, 2)
                gate(g)

            steps(dve, step)
            for e in range(EXPERTS):
                add_expert(GROUPS - 1, e)


_INS = ["x", "L0_tok_stem_w", "L0_tok_stem_b", "L0_tok_bn1_g", "L0_tok_bn1_b", "L0_tok_bn1_m", "L0_tok_bn1_v",
        "L0_tok_off_w", "L0_tok_off_b", "L0_tok_dcn_w", "L0_tok_dcn_b", "L0_tok_bn2_g", "L0_tok_bn2_b", "L0_tok_bn2_m",
        "L0_tok_bn2_v", "L0_attn_W_qkv", "L0_attn_W_proj", "L0_attn_b_proj", "L0_attn_gamma", "L0_attn_beta",
        "L0_attn_random_features", "L0_ffn_Wg", "L0_ffn_W1", "L0_ffn_b1", "L0_ffn_W2", "L0_ffn_b2"]


def kernel(**inputs):
    import numpy as _np
    import concourse.bacc as _bacc
    from concourse import mybir as _mybir
    from concourse.bass_utils import run_bass_kernel_spmd as _run

    nc = _bacc.Bacc("TRN2", target_bir_lowering=False, num_devices=1)
    arrays, aps = {}, {}
    for name in _INS:
        x = _np.ascontiguousarray(inputs[name])
        arrays[f"in_{name}_dram"] = x
        aps[name] = nc.dram_tensor(f"in_{name}_dram", x.shape, _mybir.dt.from_np(x.dtype), kind="ExternalInput").ap()
    for name, x in tables().items():
        arrays[f"table_{name}_dram"] = x
        aps[name] = nc.dram_tensor(f"table_{name}_dram", x.shape, _mybir.dt.from_np(x.dtype), kind="ExternalInput").ap()
    out = nc.dram_tensor("out_0_dram", (IMAGES, TOK_IMG, C2), _mybir.dt.float32, kind="ExternalOutput").ap()
    build(nc, aps, out)
    r = _run(nc, [arrays], core_ids=[0])
    return r.results[0]["out_0_dram"]
```

```python
from contextlib import ExitStack

import numpy as np

import concourse.bass as bass
from concourse import mybir

F32 = mybir.dt.float32
I32 = mybir.dt.int32
ALU = mybir.AluOpType
ACT = mybir.ActivationFunctionType
AX = mybir.AxisListType

IMAGES, CIN, SIDE = 32, 3, 96
STRIDE = 4
C1, C2 = 96, 192
GRID = SIDE // STRIDE
OUT_SIDE = GRID // STRIDE
TOK_IMG = OUT_SIDE * OUT_SIDE
TAPS = STRIDE * STRIDE
GROUP = 8
GROUPS = IMAGES // GROUP
SUB = GROUP // 2
ROWS = SUB * GRID
TOK = GROUP * TOK_IMG
SUBTOK = TOK // 2
COLS = TOK * TAPS // 128
FULL = TOK // 128
REST = TOK - 128 * FULL
BATCH = 3
BATCHES = COLS // BATCH
SLOTS = 6
CELL = 4 * C1
PAD = GRID
HEADS, DH, M = 12, 16, 64
PAIRS = HEADS // 2
VW = DH + 1
EXPERTS, FF = 3, 768
FCH = FF // 128
TILES = ((0, 108), (108, 108), (216, 72))
TT = 108
SLOPE = 0.01
EPS = 1e-5


def tables():
    p = np.arange(128)[:, None]
    col = np.arange(COLS)[None, :]
    full = col < FULL * TAPS
    tok = np.where(full, 128 * (col // TAPS) + p, 128 * FULL + p % 32)
    tap = np.where(full, col % TAPS, 4 * (col - FULL * TAPS) + p // 32)
    py, px = tok % TOK_IMG // OUT_SIDE, tok % OUT_SIDE
    point = np.stack([STRIDE * py + tap // STRIDE, STRIDE * px + tap % STRIDE], 2)
    row = PAD + tok // TOK_IMG * GRID * GRID
    r = np.arange(128)[:, None]
    c = np.arange(4 * M)[None, :]
    same_head = (r % 64) // DH == c // M
    head = np.where(r < 64, 1.0, -0.5) * same_head
    t = np.arange(TT)
    same_img = t[:, None] // TOK_IMG == t[None, :] // TOK_IMG
    f = np.float32
    return {
        "ident": np.eye(128, dtype=f),
        "point": point.reshape(128, 2 * COLS).astype(f),
        "row": row.astype(f),
        "head": head.astype(f),
        "own": (t[:, None] // TOK_IMG == np.arange(3)[None, :]).astype(f),
        "mean": (same_img / TOK_IMG).astype(f),
        "fold": (p % 32 == np.arange(32)[None, :]).astype(f),
    }


def build(nc, a, out):
    a = dict(a)
    w = {n.split("_", 2)[2] if n.startswith("L0_") else n: ap for n, ap in a.items()}
    table = nc.dram_tensor("cells", (PAD + GROUP * GRID * GRID, CELL), F32, kind="Internal").ap()
    out_rows = out.rearrange("b t c -> (b t) c")

    with ExitStack() as ctx:
        def sb(name, shape, dt=F32):
            return ctx.enter_context(nc.sbuf_tensor(name, shape, dt))

        def sem(name):
            return ctx.enter_context(nc.semaphore(name))

        ident = sb("ident_sb", [128, 128])
        point = sb("point_sb", [128, 2 * COLS])
        offb = sb("offb_sb", [128, 2 * COLS])
        rowbase = sb("row_sb", [128, COLS])
        own = sb("own_sb", [TT, 3])
        mean = sb("mean_sb", [TT, TT])
        fold = sb("fold_sb", [128, 32])
        headmask = sb("headmask", [64, 4 * M])
        w_stem = sb("w_stem", [96, 2, C1])
        w_off = sb("w_off", [C1, TAPS, 32])
        w_dcn = sb("w_dcn", [C1, TAPS, C2])
        w_qk = sb("w_qk", [96, 2, 6, 2, 64])
        w_v = sb("w_v", [96, 2, C2])
        w_proj = sb("w_proj", [96, 2, C2])
        w_feat = sb("w_feat", [128, 4 * M])
        w_gate = sb("w_gate", [96, 2, EXPERTS])
        w_up = sb("w_up", [96, 2, EXPERTS, FF])
        w_down = sb("w_down", [128, EXPERTS, FCH, C2])
        b_up = sb("b_up", [128, EXPERTS * FCH])
        b_down = sb("b_down", [TT, EXPERTS, C2])
        gamma = sb("gamma_sb", [TT, C2])
        beta = sb("beta_sb", [TT, C2])
        b_proj = sb("b_proj_sb", [TT, C2])
        bn = sb("bn", [96, 5, 3])
        bn_scale = sb("bn_scale", [96, 3])
        bn_bias = sb("bn_bias", [96, 3])
        bn_tmp = sb("bn_tmp", [96, 2, 3])
        bn_nat = sb("bn_nat", [15, 96])
        gate_nat = sb("gate_nat", [EXPERTS, C2])
        bup_nat = sb("bup_nat", [EXPERTS * FCH, 128])
        feat_nat = sb("feat_nat", [M, 4, DH])

        xs = sb("xs", [ROWS, CIN * STRIDE, SIDE])
        xt = sb("xt", [96, GRID // 2, ROWS])
        h = sb("h", [C1, 2, GRID, ROWS])
        xr = sb("xr", [ROWS, 2, SIDE * CIN * STRIDE])
        part = sb("part", [128, TOK])
        pos = sb("pos", [128, 2 * COLS])
        clipped = sb("clipped", [128, 2 * COLS])
        whole_i = sb("whole_i", [128, 2 * COLS], I32)
        whole = sb("whole", [128, 2 * COLS])
        hat = sb("hat", [128, 2 * COLS, 2])
        above = hat[:, :, 0]
        corner = sb("corner", [128, COLS, 2, 2])
        cell_f = sb("cell_f", [128, COLS])
        cell = sb("cell", [128, COLS], I32)
        ring = sb("ring", [128, SLOTS, BATCH, CELL])
        acc = sb("acc", [128, 3, BATCH, C1])
        shared = sb("shared", [128, TAPS * TOK])
        samp = shared[0:C1, :].rearrange("c (k t) -> c k t", k=TAPS)
        QP_END = 3 * HEADS * M + PAIRS * TOK
        kp = shared[0:TT, 0:3 * HEADS * M].rearrange("t (a f) -> t a f", a=3)
        qp = shared[:, 3 * HEADS * M:3 * HEADS * M + PAIRS * TOK].rearrange("f (p t) -> f p t", p=PAIRS)
        h2t = sb("h2t", [96, 2, TOK])
        h2 = sb("h2", [TT, 3, C2])
        xn = sb("xn", [TT, 3, C2])
        lnT = sb("lnT", [96, 2, TOK])
        qk = sb("qk", [128, 6, TOK])
        mv = sb("mv", [TT, 3, 3, HEADS * VW])
        kv = sb("kv", [128, 3, PAIRS, 3, 2 * VW])
        o = sb("o", [TT, 3, PAIRS, 2 * VW])
        den = sb("den", [TT, 3, HEADS])
        xa = shared[0:TT, QP_END:QP_END + 3 * C2].rearrange("t (a c) -> t a c", a=3)
        h3 = sb("h3", [TT, 3, C2])
        xfT = sb("xfT", [96, 2, TOK])
        stats = sb("stats", [TT, 3, 6])
        mvar = sb("mvar", [TT, 3, 2])
        rs_x = sb("rs_x", [TT, 3])
        rs_i = sb("rs_i", [TT, 3], I32)
        rs_t = sb("rs_t", [TT, 3])
        rstd = sb("rstd", [TT, 3])
        rt = sb("rt", [TT, 3, EXPERTS])
        logit = sb("logit", [TT, 3, EXPERTS])
        rmax = sb("rmax", [TT, 3])
        rsum = sb("rsum", [TT, 3])
        prob = sb("prob", [TT, 3, EXPERTS])
        hot = sb("hot", [TT, 3, EXPERTS])
        gates = sb("gates", [TT, 3, EXPERTS])
        hid = sb("hid", [128, 2, FCH, TOK])
        y = sb("y", [TT, 3, C2])

        flat = ring[:, :, :, :].rearrange("p s b c -> p (s b c)")
        HALF = GRID * C1
        ht = flat[0:ROWS, 0:2 * HALF].rearrange("r (s x c) -> r s x c", s=2, c=C1)
        dcn_nat = shared[0:96, 0:2 * C1 * TAPS].rearrange("o (m k) -> o m k", m=2)
        off_nat = shared[0:32, 2 * C1 * TAPS:3 * C1 * TAPS]
        stem_nat = flat[0:96, 2 * HALF:2 * HALF + 192].rearrange("o (x k) -> o x k", x=2)

        ps = [ctx.enter_context(nc.psum_tensor(f"bank{i}", [128, 512], F32)) for i in range(8)]

        ld_stem, ld_small, ld_dcn, ld_attn, ld_ffn = (sem(n) for n in ("ld_stem", "ld_small", "ld_dcn", "ld_attn", "ld_ffn"))
        ld_bn, ld_offb, ld_nat, point_ready = sem("ld_bn"), sem("ld_offb"), sem("ld_nat"), sem("point_ready")
        xn_biased = sem("xn_biased")
        zeroed = sem("zeroed")
        nat_mm, nat_evac = sem("nat_mm"), sem("nat_evac")
        bn_ready, bn_chain, feat_ready = sem("bn_ready"), sem("bn_chain"), sem("feat_ready")
        x_in, x_ready = sem("x_in"), sem("x_ready")
        xt_mm, xt_evac = sem("xt_mm"), sem("xt_evac")
        stem_mm, bn_evac, h_ready = sem("stem_mm"), sem("bn_evac"), sem("h_ready")
        ht_mm, ht_even, ht_odd, h_stored = sem("ht_mm"), sem("ht_even"), sem("ht_odd"), sem("h_stored")
        off_mm, part_ready, off_tok = sem("off_mm"), sem("part_ready"), sem("off_tok")
        idx_chain, idx_ready = sem("idx_chain"), sem("idx_ready")
        gathered = [sem(f"gathered{i}") for i in range(SLOTS)]
        first_corner, comb_chain, combined = sem("first_corner"), sem("comb_chain"), sem("combined")
        samp_mm, samp_evac = sem("samp_mm"), sem("samp_evac")
        dcn_mm, bn2_evac, h2_ready = sem("dcn_mm"), sem("bn2_evac"), sem("h2_ready")
        t1_mm, t1_evac, ln_chain, xn_ready = sem("t1_mm"), sem("t1_evac"), sem("ln_chain"), sem("xn_ready")
        t2_mm, t2_evac = sem("t2_mm"), sem("t2_evac")
        qk_mm, q_copied, q_squared = sem("qk_mm"), sem("q_copied"), sem("q_squared")
        v_mm, v_evac = sem("v_mm"), sem("v_evac")
        feat_mm, exp_done = sem("feat_mm"), sem("exp_done")
        kv_mm, kv_lo, kv_hi = sem("kv_mm"), sem("kv_lo"), sem("kv_hi")
        o_first = sem("o_first")
        out_mm, o_chain, o_evac, xa_ready = sem("out_mm"), sem("o_chain"), sem("o_evac"), sem("xa_ready")
        t3_mm, t3_evac = sem("t3_mm"), sem("t3_evac")
        proj_mm, ln2_chain, xf_ready = sem("proj_mm"), sem("ln2_chain"), sem("xf_ready")
        t4_mm, t4_evac = sem("t4_mm"), sem("t4_evac")
        rt_mm, rt_copied, logit_mm = sem("rt_mm"), sem("rt_copied"), sem("logit_mm")
        gate_chain, logit_chain, logit_ready, prob_exp = sem("gate_chain"), sem("logit_chain"), sem("logit_ready"), sem("prob_exp")
        up_mm, gelu_done, down_mm, y_added = sem("up_mm"), sem("gelu_done"), sem("down_mm"), sem("y_added")
        y_biased, stored = sem("y_biased"), sem("stored")
        edges = sem("edges")
        pool_turns, dve_turns = sem("pool_turns"), sem("dve_turns")

        FIRST_UPS = ((2, 1), (3, 1), (4, 2))
        DOWN_BANKS = ((7, 4, 1), (7, 4, 1), (7, 5, 6))

        def later(g):
            return not isinstance(g, int) or g > 0

        class Chain:

            def __init__(self, eng, s, g, per, n=0):
                self.eng, self.s, self.g, self.per, self.n = eng, s, g, per, n

            def add(self, ins):
                self.n += 1
                ins.then_inc(self.s, 1)
                return self.n

            def wait(self, n=None):
                self.eng.wait_ge(self.s, self.g * self.per + (self.n if n is None else n))

            def link(self, ins):
                self.add(ins)
                self.wait()

            def end(self):
                assert self.n == self.per, (self.n, self.per)

        def steps(eng, step):
            step(0, False, True)
            with eng.Fori(1, GROUPS - 1) as g:
                step(g, True, True)
            step(GROUPS - 1, True, False)

        block = ctx.enter_context(nc.Block())

        @block.sync
        def _(sp):
            def load_images(g):
                for s in range(2):
                    if s == 1 or later(g):
                        sp.wait_ge(x_ready, 2 * g + s)
                    for b in range(SUB):
                        img = w["x"][bass.ds(g * GROUP + (SUB * s + b), 1)]
                        sp.dma_start(xs[GRID * b:GRID * (b + 1), :, :].rearrange("y (c k) x -> y c (k x)", c=CIN),
                                     img.rearrange("n c (y k) x -> (n y) c (k x)", k=STRIDE)).then_inc(x_in, 16)

            def store_cells(g):
                if later(g):
                    for i in range(SLOTS):
                        sp.wait_ge(gathered[i], 96 * g)
                for s in range(2):
                    sp.wait_ge(ht_even, 6 * g + 3 * (s + 1))
                    sp.wait_ge(ht_odd, 6 * g + 3 * (s + 1))
                    for slot in range(2):
                        first = PAD + s * SUB * GRID * GRID - slot * GRID
                        dst = table[first:first + ROWS * GRID, slot * 2 * C1:(slot + 1) * 2 * C1]
                        src = bass.AP(ring, s * HALF, [[SLOTS * BATCH * CELL, ROWS], [C1, GRID - 1], [1, 2 * C1]])
                        sp.dma_start(dst.rearrange("(p x) c -> p x c", p=ROWS)[:, 0:GRID - 1, :], src).then_inc(h_stored, 16)

            def store_out(g):
                sp.wait_ge(y_added, 9 * (g + 1))
                for t, (t0, n) in enumerate(TILES):
                    sp.dma_start(out_rows[bass.ds(g * TOK + t0, n), :], y[0:n, t, :]).then_inc(stored, 16)

            sp.sem_inc(stored, 1)
            sp.dma_start(stem_nat[:, 0, 0:48], w["stem_w"].rearrange("o c k l -> o (c k l)")).then_inc(ld_stem, 16)
            sp.dma_start(stem_nat[:, 1, 48:96], w["stem_w"].rearrange("o c k l -> o (c k l)")).then_inc(ld_stem, 16)
            sp.dma_start(ident[:, :], w["ident"]).then_inc(ld_stem, 16)
            load_images(0)
            sp.dma_start(off_nat, w["off_w"].rearrange("o c k l -> o (c k l)")).then_inc(ld_small, 16)
            sp.dma_start(point[:, :], w["point"]).then_inc(ld_small, 16)
            sp.dma_start(rowbase[:, :], w["row"]).then_inc(ld_small, 16)
            sp.dma_start(fold[:, :], w["fold"]).then_inc(ld_small, 16)
            sp.dma_start(headmask[:, :], w["head"][0:64, :]).then_inc(ld_small, 16)
            sp.dma_start(w_feat[64:128, :], w["head"][64:128, :]).then_inc(ld_small, 16)
            sp.dma_start(own[:, :], w["own"]).then_inc(ld_small, 16)
            sp.dma_start(mean[:, :], w["mean"]).then_inc(ld_small, 16)
            sp.dma_start(dcn_nat, w["dcn_w"].rearrange("(m o) c k l -> o m (c k l)", m=2)).then_inc(ld_dcn, 16)
            sp.wait_ge(zeroed, 3)
            zeros = kv[:, :, :, :, :].rearrange("p t q i c -> p (t q i c)")
            last = GROUP * GRID * GRID
            sp.dma_start(table[0:PAD - 1, 0:2 * C1], zeros[0:PAD - 1, 0:2 * C1]).then_inc(edges, 16)
            sp.dma_start(table[last:last + GRID - 1, 2 * C1:], zeros[0:GRID - 1, 0:2 * C1]).then_inc(edges, 16)
            sp.dma_start(table[PAD - 1:PAD, :], zeros[0:1, 0:CELL]).then_inc(edges, 16)
            sp.dma_start(table[PAD:, :].rearrange("(p a x) c -> p a x c", a=2, x=GRID)[:, :, GRID - 1, :],
                         zeros[0:GROUP * GRID // 2, 0:2 * CELL].rearrange("p (a c) -> p a c", a=2)).then_inc(edges, 16)
            store_cells(0)
            for i in range(SLOTS):
                sp.wait_ge(gathered[i], 96)
            for n, kt in ((n, kt) for n in range(6) for kt in range(2)):
                for d in range(2):
                    sp.dma_start(w_qk[:, kt, n, d, :], w["W_qkv"][96 * kt:96 * kt + 96, 64 * n:64 * n + 64]).then_inc(ld_attn, 16)
            sp.dma_start(w_v[:, :, :], w["W_qkv"][:, 2 * C2:].rearrange("(t p) n -> p t n", t=2)).then_inc(ld_attn, 16)
            sp.dma_start(w_proj[:, :, :], w["W_proj"].rearrange("(t p) n -> p t n", t=2)).then_inc(ld_attn, 16)
            for dst, name in ((gamma, "gamma"), (beta, "beta"), (b_proj, "b_proj")):
                sp.dma_start(dst[:, :], w[name].partition_broadcast(TT)).then_inc(ld_attn, 16)
            for kt in range(2):
                sp.dma_start(w_up[:, kt, :, :], w["W1"][:, 96 * kt:96 * kt + 96, :].rearrange("e p f -> p e f")).then_inc(ld_ffn, 16)
            for e in range(EXPERTS):
                sp.dma_start(w_down[:, e, :, :], w["W2"][e].rearrange("(f p) n -> p f n", p=128)).then_inc(ld_ffn, 16)
            sp.dma_start(b_down[:, :, :], w["b2"].rearrange("e n -> (e n)").partition_broadcast(TT)).then_inc(ld_ffn, 16)

            def step(g, has_last, has_next):
                if has_next:
                    load_images(g + 1)
                    store_cells(g + 1)
                if has_last:
                    store_out(g - 1)

            steps(sp, step)
            store_out(GROUPS - 1)
            sp.wait_ge(stored, 16 * 3 * GROUPS + 1)

        @block.gpsimd
        def _(pool):
            pool.memset(stem_nat[:, 0, 48:96], 0.0).then_inc(zeroed, 1)
            pool.memset(stem_nat[:, 1, 0:48], 0.0).then_inc(zeroed, 1)
            pool.memset(kv[:, :, :, :, :], 0.0).then_inc(zeroed, 1)
            pool.memset(mvar[:, :, :], 1.0).then_inc(zeroed, 1)
            pool.memset(logit[:, :, :], 0.0).then_inc(zeroed, 1)

            def rearrange_rows(g):
                for s in range(2):
                    if later(g):
                        pool.wait_ge(xt_mm, 6 * g + 3 * s - 3)
                    pool.wait_ge(x_in, 128 * g + 64 * (s + 1))
                    pool.sem_inc(pool_turns, 1)
                    pool.tensor_copy(xr[:, s, :].rearrange("p (x r k) -> p x r k", x=GRID, k=STRIDE),
                                     xs[:, :, :].rearrange("p r (x k) -> p x r k", k=STRIDE)).then_inc(x_ready, 1)

            def gather(g):
                pool.wait_ge(idx_ready, 2 * g + 2)
                pool.wait_ge(h_stored, 64 * (g + 1))
                for k in range(BATCHES):
                    if k >= SLOTS:
                        pool.wait_ge(combined, BATCH * (BATCHES * g + (k - SLOTS + 1)))
                    elif later(g):
                        pool.wait_ge(combined, BATCH * (BATCHES * (g - 1) + (k + SLOTS + 1)))
                    pool.sem_inc(pool_turns, 1)
                    for j in range(BATCH):
                        col = BATCH * k + j
                        pool.indirect_dma_start(
                            ring[:, k % SLOTS, j, :], None, table,
                            bass.IndirectOffsetOnAxis(ap=cell[:, col:col + 1], axis=0)).then_inc(gathered[k % SLOTS], 16)

            rearrange_rows(0)
            pool.wait_ge(edges, 64)
            pool.wait_ge(nat_mm, 1)
            gather(0)

            def step(g, has_last, has_next):
                if has_next:
                    rearrange_rows(g + 1)
                    gather(g + 1)

            steps(pool, step)

        @block.tensor
        def _(pe):
            def stem_x(g, s):
                pe.wait_ge(x_ready, 2 * g + s + 1)
                for j in range(3):
                    u = 3 * s + j
                    if u >= 2:
                        pe.wait_ge(xt_evac, 6 * g + (u - 1))
                    elif later(g):
                        pe.wait_ge(bn2_evac, 2 * g)
                    for i in range(4):
                        mm = pe.transpose(ps[u % 2][0:96, ROWS * i:ROWS * (i + 1)], xr[:, s, 96 * (4 * j + i):96 * (4 * j + i + 1)],
                                          ident[0:ROWS, 0:ROWS])
                    mm.then_inc(xt_mm, 1)

            def stem_products(g, s):
                for i in range(6):
                    n = 6 * s + i
                    pe.wait_ge(xt_evac, 6 * g + (3 * s + i // 2 + 1))
                    if n >= 2:
                        pe.wait_ge(bn_evac, 12 * g + (n - 1))
                    elif later(g):
                        pe.wait_ge(t1_evac, 3 * g)
                    pe.matmul(ps[2 + n % 2][0:C1, 0:4 * ROWS], w_stem[:, i % 2, :],
                              xt[:, 4 * (i // 2):4 * (i // 2) + 4, :], start=True, stop=True).then_inc(stem_mm, 1)

            def stem_rows(g):
                for s in range(2):
                    for j in range(6):
                        u = 6 * s + j
                        pe.wait_ge(h_ready, 6 * g + (3 * s + j // 2 + 1))
                        if u < 2:
                            pe.wait_ge(xt_evac, 6 * (g + 1))
                        else:
                            pe.wait_ge((ht_even, ht_odd)[u % 2], 6 * g + u // 2)
                        for i in range(4):
                            mm = pe.transpose(ps[u % 2][0:ROWS, C1 * i:C1 * (i + 1)], h[:, s, 4 * j + i, :],
                                              ident[0:C1, 0:C1])
                        mm.then_inc(ht_mm, 1)
                    if s == 0 and later(g):
                        pe.wait_ge(t1_evac, 3 * g)
                    for kw in range(STRIDE):
                        for kh in range(STRIDE):
                            rhs = bass.AP(h, s * GRID * ROWS + kw * ROWS + kh,
                                          [[2 * GRID * ROWS, C1], [STRIDE, SUB * OUT_SIDE], [STRIDE * ROWS, OUT_SIDE]])
                            mm = pe.matmul(ps[4][32 * kh:32 * kh + 32, SUBTOK * s:SUBTOK * (s + 1)],
                                           w_off[:, STRIDE * kh + kw, :], rhs,
                                           start=(kw == 0), stop=(kw == STRIDE - 1), skip_group_check=True)
                    mm.then_inc(off_mm, 1)

            def offsets_by_token(g):
                pe.wait_ge(part_ready, g + 1)
                for t in range(FULL):
                    pe.matmul(ps[4][:, TOK + 32 * t:TOK + 32 * t + 32], part[:, 128 * t:128 * t + 128], fold[:, :],
                              start=True, stop=True, skip_group_check=True)
                for q in range(4):
                    mm = pe.matmul(ps[4][32 * q:32 * q + 32, TOK + 64:TOK + 72], part[:, 128 * FULL:TOK],
                                   fold[:, :].rearrange("p (j q x) -> p j q x", j=4, q=4)[:, :, q, :],
                                   start=True, stop=True, skip_group_check=True)
                mm.then_inc(off_tok, 1)

            def dcn(g, has_last):
                for k in range(BATCHES):
                    pe.wait_ge(combined, BATCH * (BATCHES * g + k + 1))
                    if k >= 2:
                        pe.wait_ge(samp_evac, BATCHES * g + (k - 1))
                    elif later(g):
                        pe.wait_ge(o_evac, 6 * g)
                        pe.wait_ge(logit_ready, g)
                    for j in range(BATCH):
                        mm = pe.transpose(ps[2 + k % 2][0:C1, 128 * j:128 * (j + 1)], acc[:, k % 3, j, :], ident[:, :])
                    mm.then_inc(samp_mm, 1)
                    if has_last:
                        if k < 3:
                            up(g - 1, 0, *FIRST_UPS[k])
                        elif k < 6:
                            down(g - 1, 0, k - 3)
                        elif k < 9:
                            up(g - 1, 1, 2 * (k - 6), 2)
                        else:
                            down(g - 1, 1, k - 9)
                pe.wait_ge(samp_evac, BATCHES * (g + 1))
                if later(g):
                    pe.wait_ge(t4_evac, 2 * g)
                else:
                    pe.wait_ge(ht_even, 6)
                    pe.wait_ge(ht_odd, 6)
                for m in range(2):
                    if m == 1 and has_last:
                        pe.wait_ge(y_added, 9 * g - 3)
                    for k in range(TAPS):
                        mm = pe.matmul(ps[m][0:96, 0:TOK], w_dcn[:, k, 96 * m:96 * m + 96], samp[:, k, :],
                                       start=(k == 0), stop=(k == TAPS - 1))
                    mm.then_inc(dcn_mm, 1)

            def tokens(g):
                pe.wait_ge(h2_ready, 2 * (g + 1))
                pe.wait_ge(idx_ready, 2 * g + 2)
                for t, (t0, n) in enumerate(TILES):
                    for m in range(2):
                        mm = pe.transpose(ps[2 + t][0:n, 96 * m:96 * m + 96], h2t[:, m, t0:t0 + n], ident[0:96, 0:96])
                    mm.then_inc(t1_mm, 1)

            def channels(g, src, ready, s):
                for t, (t0, n) in enumerate(TILES):
                    pe.wait_ge(ready, 3 * g + t + 1)
                    for m in range(2):
                        mm = pe.transpose(ps[m][0:96, t0:t0 + n], src[0:n, t, 96 * m:96 * m + 96], ident[0:n, 0:n])
                mm.then_inc(s, 1)

            def qkv(g, has_next):
                pe.wait_ge(t2_evac, 2 * (g + 1))
                for n in range(6):
                    if n >= 3:
                        pe.wait_ge(q_copied, 6 * g + (n - 2))
                        pe.wait_ge(q_squared, 6 * g + (n - 2))
                    elif has_next and n < 2:
                        pe.wait_ge(bn_evac, 12 * (g + 2))
                    elif has_next:
                        pe.wait_ge(idx_ready, 2 * g + 4)
                    else:
                        pe.wait_ge(t1_evac, 3 * (g + 1))
                    for kt in range(2):
                        mm = pe.matmul(ps[2 + n % 3][:, 0:TOK], w_qk[:, kt, n, :, :].rearrange("p d c -> p (d c)"),
                                       lnT[:, kt, :], start=(kt == 0), stop=(kt == 1))
                    mm.then_inc(qk_mm, 1)
                for t, (t0, n) in enumerate(TILES):
                    if t == 2:
                        pe.wait_ge(v_evac, 3 * g + 1)
                    for kt in range(2):
                        mm = pe.matmul(ps[t % 2][0:n, 0:C2], lnT[:, kt, t0:t0 + n], w_v[:, kt, :],
                                       start=(kt == 0), stop=(kt == 1))
                    mm.then_inc(v_mm, 1)

            def features(g):
                pe.wait_ge(q_copied, 6 * (g + 1))
                pe.wait_ge(q_squared, 6 * (g + 1))
                pe.wait_ge(v_evac, 3 * (g + 1))
                for u in range(12):
                    if u >= 4:
                        pe.wait_ge(exp_done, 12 * g + (u - 3))
                    bank = ps[u % 4]
                    if u < 6:
                        t0, n = TILES[u // 2]
                        for j in ((0, 1) if u % 2 == 0 else (2,)):
                            mm = pe.matmul(bank[0:n, 256 * (j % 2):256 * (j % 2) + 256], qk[:, 3 + j, t0:t0 + n],
                                           w_feat[:, :], start=True, stop=True)
                    else:
                        p = u - 6
                        mm = pe.matmul(bank[:, 0:TOK], w_feat[:, 128 * (p % 2):128 * (p % 2) + 128], qk[:, p // 2, :],
                                       start=True, stop=True)
                    mm.then_inc(feat_mm, 1)

            def kv_sums(g):
                pe.wait_ge(exp_done, 12 * g + 10)
                for u in range(6):
                    t, b = u // 2, u % 2
                    n = TILES[t][1]
                    ni = n // TOK_IMG
                    if u >= 3:
                        pe.wait_ge(kv_lo, 6 * g + (u - 2))
                        pe.wait_ge(kv_hi, 6 * g + (u - 2))
                    for i in range(3):
                        p = 3 * b + i
                        mm = pe.matmul(ps[(4, 0, 1)[u % 3]][:, 102 * i:102 * i + 34 * ni], kp[0:n, t, 128 * p:128 * p + 128],
                                       mv[0:n, t, 0:ni, 34 * p:34 * p + 34], start=True, stop=True)
                    mm.then_inc(kv_mm, 1)

            def attend(g):
                pe.wait_ge(exp_done, 12 * (g + 1))
                for u in range(6):
                    t, b = u // 2, u % 2
                    t0, n = TILES[t]
                    ni = n // TOK_IMG
                    pe.wait_ge(kv_lo, 6 * g + (u + 1))
                    pe.wait_ge(kv_hi, 6 * g + (u + 1))
                    if u >= 2:
                        pe.wait_ge(o_evac, 6 * g + (u - 1))
                    for i in range(3):
                        p = 3 * b + i
                        mm = pe.matmul(ps[2 + b][0:n, 102 * i:102 * i + 34 * ni], qp[:, p, t0:t0 + n],
                                       kv[:, t, p, 0:ni, :], start=True, stop=True)
                    mm.then_inc(out_mm, 1)

            def project(g):
                pe.wait_ge(t3_evac, 2 * (g + 1))
                for t, (t0, n) in enumerate(TILES):
                    for kt in range(2):
                        mm = pe.matmul(ps[2 + t][0:n, 0:C2], lnT[:, kt, t0:t0 + n], w_proj[:, kt, :],
                                       start=(kt == 0), stop=(kt == 1))
                    mm.then_inc(proj_mm, 1)

            def route(g):
                pe.wait_ge(t4_evac, 2 * (g + 1))
                for t, (t0, n) in enumerate(TILES):
                    for kt in range(2):
                        mm = pe.matmul(ps[2][0:n, 4 * t:4 * t + 3], xfT[:, kt, t0:t0 + n], w_gate[:, kt, :],
                                       start=(kt == 0), stop=(kt == 1))
                mm.then_inc(rt_mm, 1)

            def logits(g):
                pe.wait_ge(rt_copied, g + 1)
                for t, (t0, n) in enumerate(TILES):
                    mm = pe.matmul(ps[3][0:n, 4 * t:4 * t + 3], mean[0:n, 0:n], rt[0:n, t, :], start=True, stop=True)
                mm.then_inc(logit_mm, 1)

            def up(g, e, first=0, count=FCH):
                if e == 0 and first == 0:
                    pe.wait_ge(t4_evac, 2 * (g + 1))
                for f in range(first, first + count):
                    n = FCH * e + f
                    if n >= 2:
                        pe.wait_ge(gelu_done, 18 * g + (n - 1))
                    for kt in range(2):
                        mm = pe.matmul(ps[5 + n % 2][:, 0:TOK], w_up[:, kt, e, 128 * f:128 * f + 128], xfT[:, kt, :],
                                       start=(kt == 0), stop=(kt == 1))
                    mm.then_inc(up_mm, 1)

            def down(g, e, t):
                t0, n = TILES[t]
                pe.wait_ge(gelu_done, 18 * g + 6 * (e + 1))
                if e > 0:
                    pe.wait_ge(y_added, 9 * g + 3 * e)
                for f in range(FCH):
                    mm = pe.matmul(ps[DOWN_BANKS[e][t]][0:n, 0:C2], hid[:, e % 2, f, t0:t0 + n],
                                   w_down[:, e, f, :], start=(f == 0), stop=(f == FCH - 1))
                mm.then_inc(down_mm, 1)

            pe.wait_ge(ld_stem, 48)
            pe.wait_ge(zeroed, 2)
            pe.wait_ge(ld_bn, 16 * 10)
            pe.transpose(ps[5][0:96, 192:207], bn_nat[:, :], ident[0:15, 0:15])
            for i in range(2):
                mm = pe.transpose(ps[5][0:96, 96 * i:96 * i + 96], stem_nat[:, i, :], ident[0:96, 0:96])
            mm.then_inc(nat_mm, 1)
            pe.wait_ge(nat_evac, 1)
            for s in range(2):
                stem_x(0, s)
                stem_products(0, s)
            pe.wait_ge(ld_small, 16 * 8)
            for k in range(TAPS):
                mm = pe.transpose(ps[6][0:C1, 32 * k:32 * k + 32],
                                  off_nat.rearrange("o (c k) -> o c k", k=TAPS)[:, :, k], ident[0:32, 0:32])
            mm.then_inc(nat_mm, 1)
            pe.wait_ge(ld_nat, 16 * 6)
            for kt in range(2):
                pe.transpose(ps[7][0:96, 4 * kt:4 * kt + 3], gate_nat[:, 96 * kt:96 * kt + 96], ident[0:3, 0:3])
            pe.transpose(ps[7][:, 32:32 + EXPERTS * FCH], bup_nat[:, :], ident[0:18, 0:18])
            pe.transpose(ps[7][0:64, 64:128], feat_nat[:, :, :].rearrange("m h d -> m (h d)"),
                         ident[0:64, 0:64]).then_inc(nat_mm, 1)
            pe.wait_ge(nat_evac, 2)
            stem_rows(0)
            offsets_by_token(0)
            pe.wait_ge(ld_dcn, 16)
            for u in range(8):
                m, k0 = u // 4, 4 * (u % 4)
                pe.wait_ge(nat_evac, u + 3 if u < 2 else u + 2)
                if u == 0:
                    pe.wait_ge(nat_evac, 3)
                for i in range(4):
                    mm = pe.transpose(ps[5 + u % 3][0:C1, 96 * i:96 * i + 96],
                                      dcn_nat[:, m, :].rearrange("o (c k) -> o c k", k=TAPS)[:, :, k0 + i], ident[0:96, 0:96])
                mm.then_inc(nat_mm, 1)
            pe.wait_ge(nat_evac, 11)

            def step(g, has_last, has_next):
                if has_last:
                    up(g - 1, 0, 0, 2)
                    logits(g - 1)
                dcn(g, has_last)
                if has_next:
                    stem_x(g + 1, 0)
                tokens(g)
                if not has_last:
                    pe.wait_ge(ld_attn, 16 * 29)
                    pe.wait_ge(feat_ready, 1)
                if has_next:
                    stem_products(g + 1, 0)
                    stem_x(g + 1, 1)
                    stem_products(g + 1, 1)
                    stem_rows(g + 1)
                    pe.wait_ge(ht_even, 6 * (g + 2))
                    pe.wait_ge(ht_odd, 6 * (g + 2))
                channels(g, xn, xn_ready, t2_mm)
                if has_next:
                    offsets_by_token(g + 1)
                qkv(g, has_next)
                features(g)
                kv_sums(g)
                attend(g)
                channels(g, xa, xa_ready, t3_mm)
                project(g)
                if has_last:
                    up(g - 1, 2)
                    for t in range(3):
                        down(g - 1, 2, t)
                channels(g, xa, xf_ready, t4_mm)
                if has_last:
                    pe.wait_ge(y_added, 9 * g)
                route(g)
                if not has_last:
                    pe.wait_ge(ld_ffn, 16 * 6)

            steps(pe, step)
            g = GROUPS - 1
            up(g, 0, 0, 2)
            logits(g)
            up(g, 0, 2, 4)
            for e in range(EXPERTS):
                if e + 1 < EXPERTS:
                    up(g, e + 1, 0, 2)
                for t in range(3):
                    down(g, e, t)
                if e + 1 < EXPERTS:
                    up(g, e + 1, 2, 4)

        @block.scalar
        def _(act):
            def stem_bn(g):
                for s in range(2):
                    if later(g):
                        act.wait_ge(off_mm, 2 * (g - 1) + (s + 1))
                    for i in range(6):
                        n = 6 * s + i
                        act.wait_ge(stem_mm, 12 * g + n + 1)
                        first = 8 * (i // 2) + i % 2
                        act.activation(h[:, s, first:first + 7:2, :], ps[2 + n % 2][0:C1, 0:4 * ROWS], ACT.Identity,
                                       bias=bn_bias[:, 0:1], scale=bn_scale[:, 0:1]).then_inc(bn_evac, 1)

            def stem_ht(g):
                for s in range(2):
                    for j in range(0, 6, 2):
                        act.wait_ge(ht_mm, 12 * g + 6 * s + j + 1)
                        act.activation(ht[:, s, 4 * j:4 * j + 4, :], ps[0][0:ROWS, 0:4 * C1], ACT.Copy).then_inc(ht_even, 1)

            def first_corners(g, k):
                act.wait_ge(gathered[k % SLOTS], 96 * g + 48 * (k // SLOTS + 1))
                if k >= 3:
                    act.wait_ge(samp_mm, BATCHES * g + (k - 2))
                elif later(g):
                    act.wait_ge(samp_mm, BATCHES * g)
                for j in range(BATCH):
                    ins = act.activation(acc[:, k % 3, j, :], ring[:, k % SLOTS, j, 0:C1], ACT.Copy,
                                         scale=corner[:, BATCH * k + j, 0, 0:1])
                ins.then_inc(first_corner, 1)

            def samp_copy(g, k):
                act.wait_ge(samp_mm, BATCHES * g + k + 1)
                bank = ps[2 + k % 2]
                col, pieces = BATCH * k, []
                while col < BATCH * (k + 1):
                    t = col // TAPS
                    run = min(BATCH * (k + 1), TAPS * (t + 1)) - col
                    src = bank[0:C1, 128 * (col - BATCH * k):128 * (col - BATCH * k + run)]
                    if t < FULL:
                        pieces.append((samp[:, col - TAPS * t:col - TAPS * t + run, 128 * t:128 * t + 128],
                                       src.rearrange("c (r t) -> c r t", r=run)))
                    else:
                        k0 = 4 * (col - TAPS * FULL)
                        pieces.append((samp[:, k0:k0 + 4 * run, 128 * FULL:TOK], src.rearrange("c (r t) -> c r t", r=4 * run)))
                    col += run
                for dst, src in pieces:
                    ins = act.activation(dst, src, ACT.Copy)
                ins.then_inc(samp_evac, 1)

            def combine_start(g):
                act.wait_ge(idx_ready, 2 * g + 2)
                for k in range(3):
                    first_corners(g, k)

            def combine(g, has_last):
                if later(g):
                    act.wait_ge(out_mm, 6 * g)
                for k in range(BATCHES):
                    if has_last and 1 <= k < 4:
                        gelus(g - 1, 0, *FIRST_UPS[k - 1])
                    if has_last and k == 3:
                        prob_exps(g - 1)
                    if has_last and 7 <= k < 10:
                        gelus(g - 1, 1, 2 * (k - 7), 2)
                    samp_copy(g, k)
                    if k + 3 < BATCHES:
                        first_corners(g, k + 3)

            def dcn_bn(g):
                if later(g):
                    act.wait_ge(t1_mm, 3 * g)
                for m in range(2):
                    act.wait_ge(dcn_mm, 2 * g + m + 1)
                    act.activation(h2t[:, m, :], ps[m][0:96, 0:TOK], ACT.Identity,
                                   bias=bn_bias[:, 1 + m:2 + m], scale=bn_scale[:, 1 + m:2 + m]).then_inc(bn2_evac, 1)

            def copy_banks(g, s, dst, done):
                act.wait_ge(s, g + 1)
                for m in range(2):
                    act.activation(dst[:, m, :], ps[m][0:96, 0:TOK], ACT.Copy).then_inc(done, 1)

            def squares(g):
                for n in range(6):
                    act.wait_ge(qk_mm, 6 * g + n + 1)
                    act.activation(qk[64:128, n, :], ps[2 + n % 3][64:128, 0:TOK], ACT.Square).then_inc(q_squared, 1)

            def exps(g):
                for u in range(12):
                    act.wait_ge(feat_mm, 12 * g + u + 1)
                    bank = ps[u % 4]
                    if u < 6:
                        n = TILES[u // 2][1]
                        w0, w1 = (0, 512) if u % 2 == 0 else (512, 768)
                        act.activation(kp[0:n, u // 2, w0:w1], bank[0:n, 0:w1 - w0], ACT.Exp).then_inc(exp_done, 1)
                    else:
                        act.activation(qp[:, u - 6, :], bank[:, 0:TOK], ACT.Exp).then_inc(exp_done, 1)

            def kv_high(g):
                for u in range(6):
                    t, b = u // 2, u % 2
                    ni = TILES[t][1] // TOK_IMG
                    act.wait_ge(kv_mm, 6 * g + u + 1)
                    src = ps[(4, 0, 1)[u % 3]][64:128, 0:306].rearrange("f (p i c) -> f p i c", p=3, i=3)
                    act.activation(kv[64:128, t, 3 * b:3 * b + 3, 0:ni, VW:2 * VW], src[:, :, 0:ni, VW:2 * VW],
                                   ACT.Copy).then_inc(kv_hi, 1)

            def outputs_first(g):
                for u in range(6):
                    t, b = u // 2, u % 2
                    n = TILES[t][1]
                    act.wait_ge(out_mm, 6 * g + u + 1)
                    src = ps[2 + b][0:n, 0:306].rearrange("t (p i c) -> t p i c", p=3, i=3)
                    act.activation(o[0:n, t, 3 * b:3 * b + 3, :], src[:, :, 0, :], ACT.Copy,
                                   scale=own[0:n, 0:1]).then_inc(o_first, 1)

            def gelus(g, e, start=0, count=FCH):
                if e >= 2:
                    act.wait_ge(down_mm, 9 * g + 3 * (e - 1))
                for f in range(start, start + count):
                    n = FCH * e + f
                    act.wait_ge(up_mm, 18 * g + n + 1)
                    act.activation(hid[:, e % 2, f, :], ps[5 + n % 2][:, 0:TOK], ACT.Gelu,
                                   bias=b_up[:, n:n + 1]).then_inc(gelu_done, 1)

            def prob_exps(g):
                act.wait_ge(logit_ready, g + 1)
                act.activation(prob[:, :, :], logit[:, :, :], ACT.Exp).then_inc(prob_exp, 1)

            for i, name in enumerate(("stem_b", "bn1_g", "bn1_b", "bn1_m", "bn1_v")):
                act.dma_start(bn_nat[3 * i:3 * i + 1, :], w[name].rearrange("(m p) -> m p", m=1)).then_inc(ld_bn, 16)
            for i, name in enumerate(("dcn_b", "bn2_g", "bn2_b", "bn2_m", "bn2_v")):
                act.dma_start(bn_nat[3 * i + 1:3 * i + 3, :], w[name].rearrange("(m p) -> m p", m=2)).then_inc(ld_bn, 16)
            for t in range(FULL):
                act.dma_start(offb[:, 32 * t:32 * t + 32], w["off_b"].partition_broadcast(128)).then_inc(ld_offb, 16)
            for q in range(4):
                taps = w["off_b"].rearrange("(j q x) -> j q x", j=4, q=4)[:, q, :]
                act.dma_start(offb[32 * q:32 * q + 32, 64:72].rearrange("p (j x) -> p j x", j=4),
                               taps.partition_broadcast(32)).then_inc(ld_offb, 16)
            act.dma_start(gate_nat[:, :], w["Wg"]).then_inc(ld_nat, 16)
            act.dma_start(bup_nat[:, :], w["b1"].rearrange("e (f p) -> (e f) p", p=128)).then_inc(ld_nat, 16)
            for i in range(4):
                act.dma_start(feat_nat[:, i, :], w["random_features"]).then_inc(ld_nat, 16)

            act.wait_ge(bn_ready, 1)
            stem_bn(0)
            stem_ht(0)
            act.wait_ge(zeroed, 5)
            act.wait_ge(feat_ready, 1)
            combine_start(0)

            def step(g, has_last, has_next):
                if has_last:
                    gelus(g - 1, 0, 0, 2)
                combine(g, has_last)
                dcn_bn(g)
                if has_next:
                    stem_bn(g + 1)
                    stem_ht(g + 1)
                copy_banks(g, t2_mm, lnT, t2_evac)
                squares(g)
                exps(g)
                kv_high(g)
                outputs_first(g)
                copy_banks(g, t3_mm, lnT, t3_evac)
                if has_last:
                    gelus(g - 1, 2)
                if has_next:
                    combine_start(g + 1)
                copy_banks(g, t4_mm, xfT, t4_evac)

            steps(act, step)
            gelus(GROUPS - 1, 0)
            prob_exps(GROUPS - 1)
            for e in range(1, EXPERTS):
                gelus(GROUPS - 1, e)

        @block.vector
        def _(dve):
            def rsqrt(chain, dst, x, ti, tt):
                chain.link(dve.tensor_scalar(ti.bitcast(I32) if ti.dtype != I32 else ti, x.bitcast(I32), 1, None, ALU.logical_shift_right))
                chain.link(dve.tensor_scalar(dst.bitcast(I32), ti, -1.0, float(0x5F3759DF), ALU.mult, ALU.add))
                for _ in range(3):
                    chain.link(dve.tensor_tensor(tt, dst, dst, ALU.mult))
                    chain.link(dve.scalar_tensor_tensor(tt, tt, -0.5, x, ALU.mult, ALU.mult))
                    chain.link(dve.scalar_tensor_tensor(dst, tt, 1.5, dst, ALU.add, ALU.mult))

            RSQRT = 11

            def stem_xt(g, s):
                if s == 1 or later(g):
                    dve.wait_ge(stem_mm, 12 * g + 6 * s)
                for j in range(3):
                    u = 3 * s + j
                    dve.wait_ge(xt_mm, 6 * g + u + 1)
                    dve.tensor_copy(xt[:, 4 * j:4 * j + 4, :], ps[u % 2][0:96, 0:4 * ROWS]).then_inc(xt_evac, 1)

            def leaky(g, s):
                for j in range(3):
                    dve.wait_ge(bn_evac, 12 * g + 6 * s + 2 * (j + 1))
                    part_h = h[:, s, 8 * j:8 * j + 8, :]
                    dve.scalar_tensor_tensor(part_h, part_h, SLOPE, part_h, ALU.mult, ALU.max).then_inc(h_ready, 1)

            def stem_ht(g, s):
                for j in range(1, 6, 2):
                    dve.wait_ge(ht_mm, 12 * g + 6 * s + j + 1)
                    dve.tensor_copy(ht[:, s, 4 * j:4 * j + 4, :], ps[1][0:ROWS, 0:4 * C1]).then_inc(ht_odd, 1)

            def part_copy(g):
                dve.wait_ge(off_mm, 2 * (g + 1))
                dve.tensor_copy(part[:, :], ps[4][:, 0:TOK]).then_inc(part_ready, 1)

            def sample_points(g):
                dve.wait_ge(off_tok, g + 1)
                chain = Chain(dve, idx_chain, g, 11)
                chain.link(dve.tensor_tensor(pos[:, :], ps[4][:, TOK:TOK + 2 * COLS], point[:, :], ALU.add))
                chain.link(dve.tensor_scalar(clipped[:, :], pos[:, :], 0.0, float(GRID - 2), ALU.max, ALU.min))
                chain.link(dve.tensor_copy(whole_i[:, :], clipped[:, :]))
                chain.link(dve.tensor_copy(whole[:, :], whole_i[:, :]))
                chain.link(dve.tensor_tensor(above, whole[:, :], clipped[:, :], ALU.is_gt))
                chain.link(dve.tensor_tensor(whole[:, :], whole[:, :], above, ALU.subtract))
                wh = whole[:, :].rearrange("p (c x) -> p c x", x=2)
                chain.add(dve.scalar_tensor_tensor(cell_f[:, :], wh[:, :, 0], float(GRID), wh[:, :, 1], ALU.mult, ALU.add))
                chain.link(dve.tensor_tensor(hat[:, :, 0], pos[:, :], whole[:, :], ALU.subtract))
                chain.link(dve.tensor_scalar(hat[:, :, 1], hat[:, :, 0], -1.0, None, ALU.add))
                chain.link(dve.scalar_tensor_tensor(hat[:, :, :], hat[:, :, :], -1.0, hat[:, :, :], ALU.mult, ALU.min))
                chain.link(dve.tensor_scalar(hat[:, :, :], hat[:, :, :], 1.0, 0.0, ALU.add, ALU.max))
                hv = hat[:, :, :].rearrange("p (c x) k -> p c x k", x=2)
                hy = hv[:, :, 0, :].unsqueeze(3).to_broadcast([128, COLS, 2, 2])
                hx = hv[:, :, 1, :].unsqueeze(2).to_broadcast([128, COLS, 2, 2])
                dve.tensor_tensor(cell[:, :], cell_f[:, :], rowbase[:, :], ALU.add).then_inc(idx_ready, 1)
                dve.tensor_tensor(corner[:, :, :, :], hy, hx, ALU.mult).then_inc(idx_ready, 1)
                chain.end()

            def combine(g, first, last):
                chain = Chain(dve, comb_chain, g, 2 * BATCH * BATCHES, 2 * BATCH * first)
                for k in range(first, last):
                    dve.wait_ge(first_corner, BATCHES * g + k + 1)
                    for c in range(1, 4):
                        for j in range(BATCH):
                            if c > 1:
                                chain.wait(2 * BATCH * k + BATCH * (c - 2) + j + 1)
                            dst = acc[:, k % 3, j, :]
                            ins = dve.scalar_tensor_tensor(dst, ring[:, k % SLOTS, j, C1 * c:C1 * (c + 1)],
                                                           corner[:, BATCH * k + j, c // 2, c % 2:c % 2 + 1], dst,
                                                           ALU.mult, ALU.add)
                            if c < 3:
                                chain.add(ins)
                            else:
                                ins.then_inc(combined, 1)

            def dcn_leaky(g):
                for m in range(2):
                    dve.wait_ge(bn2_evac, 2 * g + m + 1)
                    part_h = h2t[:, m, :]
                    dve.scalar_tensor_tensor(part_h, part_h, SLOPE, part_h, ALU.mult, ALU.max).then_inc(h2_ready, 1)

            def moments(chain, src):
                for t, (t0, n) in enumerate(TILES):
                    chain.add(dve.bn_stats(stats[0:n, t, :], src[0:n, t, :]))
                chain.wait()
                dve.sem_inc(dve_turns, 1)
                for t, (t0, n) in enumerate(TILES):
                    chain.add(dve.bn_aggr(mvar[0:n, t, :], stats[0:n, t, :]))
                chain.wait()
                chain.link(dve.tensor_scalar(rs_x[:, :], mvar[:, :, 1], EPS, None, ALU.add))
                rsqrt(chain, rstd[:, :], rs_x[:, :], rs_i[:, :], rs_t[:, :])

            MOMENTS = 7 + RSQRT

            def norm(t, n, dst, src):
                return dve.tensor_scalar(dst[0:n, t, :], src[0:n, t, :], mvar[0:n, t, 0:1], rstd[0:n, t:t + 1],
                                         ALU.subtract, ALU.mult)

            def norm_in(g):
                chain = Chain(dve, ln_chain, g, MOMENTS + 3)
                for t, (t0, n) in enumerate(TILES):
                    dve.wait_ge(t1_mm, 3 * g + t + 1)
                    dve.tensor_copy(h2[0:n, t, :], ps[2 + t][0:n, 0:C2]).then_inc(t1_evac, 1)
                dve.wait_ge(t1_evac, 3 * (g + 1))
                moments(chain, h2)
                for t, (t0, n) in enumerate(TILES):
                    norm(t, n, xn, h2).then_inc(xn_ready, 1)
                dve.wait_ge(xn_ready, 3 * (g + 1))
                for t, (t0, n) in enumerate(TILES):
                    chain.add(dve.tensor_tensor(h2[0:n, t, :], h2[0:n, t, :], beta[0:n, :], ALU.add))
                chain.end()

            def q_copies(g):
                for n in range(6):
                    dve.wait_ge(qk_mm, 6 * g + n + 1)
                    dve.tensor_copy(qk[0:64, n, :], ps[2 + n % 3][0:64, 0:TOK]).then_inc(q_copied, 1)

            def values(g):
                for t, (t0, n) in enumerate(TILES):
                    dve.wait_ge(v_mm, 3 * g + t + 1)
                    for i in range(n // TOK_IMG):
                        dst = mv[0:n, t, i, :].rearrange("t (h c) -> t h c", c=VW)[:, :, 0:DH]
                        ins = dve.tensor_scalar(dst, ps[t % 2][0:n, 0:C2].rearrange("t (h c) -> t h c", c=DH),
                                                own[0:n, i:i + 1], None, ALU.mult)
                    ins.then_inc(v_evac, 1)

            def add_proj_bias(g):
                dve.wait_ge(t2_mm, g + 1)
                for t, (t0, n) in enumerate(TILES):
                    ins = dve.tensor_tensor(xn[0:n, t, :], xn[0:n, t, :], b_proj[0:n, :], ALU.add)
                ins.then_inc(xn_biased, 1)

            def kv_low(g):
                for u in range(6):
                    t, b = u // 2, u % 2
                    ni = TILES[t][1] // TOK_IMG
                    dve.wait_ge(kv_mm, 6 * g + u + 1)
                    src = ps[(4, 0, 1)[u % 3]][0:64, 0:306].rearrange("f (p i c) -> f p i c", p=3, i=3)
                    dve.tensor_copy(kv[0:64, t, 3 * b:3 * b + 3, 0:ni, 0:VW], src[:, :, 0:ni, 0:VW]).then_inc(kv_lo, 1)

            def outputs(g):
                chain = Chain(dve, o_chain, g, 2 * 2 + 6)
                for u in range(6):
                    t, b = u // 2, u % 2
                    n = TILES[t][1]
                    dve.wait_ge(o_first, 6 * g + u + 1)
                    src = ps[2 + b][0:n, 0:306].rearrange("t (p i c) -> t p i c", p=3, i=3)
                    dst = o[0:n, t, 3 * b:3 * b + 3, :]
                    images = n // TOK_IMG
                    for i in range(1, images):
                        ins = dve.scalar_tensor_tensor(dst, src[:, :, i, :], own[0:n, i:i + 1], dst, ALU.mult, ALU.add)
                        if i < images - 1:
                            chain.link(ins)
                    ins.then_inc(o_evac, 1)
                    if b == 1:
                        dve.wait_ge(o_evac, 6 * g + (u + 1))
                        ov = o[0:n, t, :, :].rearrange("t p (h c) -> t (p h) c", c=VW)
                        chain.link(dve.tensor_scalar(den[0:n, t, :], ov[:, :, DH], M * 1e-6, None, ALU.add))
                        chain.link(dve.reciprocal(den[0:n, t, :], den[0:n, t, :]))
                        dve.tensor_tensor(xa[0:n, t, :].rearrange("t (h c) -> t h c", c=DH), ov[:, :, 0:DH],
                                          den[0:n, t, :].unsqueeze(2).to_broadcast([n, HEADS, DH]),
                                          ALU.mult).then_inc(xa_ready, 1)
                chain.end()

            def norms_out(g):
                chain = Chain(dve, ln2_chain, g, 2 * MOMENTS + 12)
                dve.wait_ge(xn_biased, g + 1)
                dve.wait_ge(ln_chain, (MOMENTS + 3) * (g + 1))
                for t, (t0, n) in enumerate(TILES):
                    dve.wait_ge(proj_mm, 3 * g + t + 1)
                    chain.add(dve.tensor_tensor(xn[0:n, t, :], ps[2 + t][0:n, 0:C2], xn[0:n, t, :], ALU.add))
                chain.wait()
                moments(chain, xn)
                done = chain.n
                for t, (t0, n) in enumerate(TILES):
                    chain.add(norm(t, n, h3, xn))
                for t, (t0, n) in enumerate(TILES):
                    chain.wait(done + t + 1)
                    chain.add(dve.tensor_tensor(h3[0:n, t, :], h3[0:n, t, :], gamma[0:n, :], ALU.mult))
                for t, (t0, n) in enumerate(TILES):
                    chain.wait(done + 3 + t + 1)
                    chain.add(dve.tensor_tensor(h3[0:n, t, :], h3[0:n, t, :], h2[0:n, t, :], ALU.add))
                chain.wait()
                moments(chain, h3)
                for t, (t0, n) in enumerate(TILES):
                    norm(t, n, xa, h3).then_inc(xf_ready, 1)
                chain.end()

            def gate_logits(g):
                dve.wait_ge(rt_mm, g + 1)
                for t, (t0, n) in enumerate(TILES):
                    ins = dve.tensor_copy(rt[0:n, t, :], ps[2][0:n, 4 * t:4 * t + 3])
                ins.then_inc(rt_copied, 1)
                chain = Chain(dve, logit_chain, g, 3 + 1)
                dve.wait_ge(logit_mm, g + 1)
                for t, (t0, n) in enumerate(TILES):
                    chain.add(dve.tensor_copy(logit[0:n, t, :], ps[3][0:n, 4 * t:4 * t + 3]))
                chain.wait()
                chain.link(dve.tensor_reduce(rmax[:, :], logit[:, :, :], AX.X, ALU.max))
                dve.tensor_tensor(logit[:, :, :], logit[:, :, :], rmax[:, :].unsqueeze(2).to_broadcast([TT, 3, EXPERTS]),
                                  ALU.subtract).then_inc(logit_ready, 1)
                chain.end()

            def gate(g):
                chain = Chain(dve, gate_chain, g, 9)
                dve.wait_ge(prob_exp, g + 1)
                chain.link(dve.tensor_reduce(rsum[:, :], prob[:, :, :], AX.X, ALU.add))
                chain.link(dve.reciprocal(rsum[:, :], rsum[:, :]))
                chain.link(dve.tensor_tensor(prob[:, :, :], prob[:, :, :], rsum[:, :].unsqueeze(2).to_broadcast([TT, 3, EXPERTS]), ALU.mult))
                chain.link(dve.tensor_reduce(rmax[:, :], prob[:, :, :], AX.X, ALU.max))
                chain.link(dve.tensor_tensor(hot[:, :, :], prob[:, :, :], rmax[:, :].unsqueeze(2).to_broadcast([TT, 3, EXPERTS]), ALU.is_ge))
                chain.link(dve.tensor_tensor(hot[:, :, 1], hot[:, :, 1], hot[:, :, 0], ALU.is_gt))
                chain.link(dve.tensor_tensor(rmax[:, :], hot[:, :, 0], hot[:, :, 1], ALU.add))
                chain.link(dve.tensor_tensor(hot[:, :, 2], hot[:, :, 2], rmax[:, :], ALU.is_gt))
                chain.link(dve.tensor_tensor(gates[:, :, :], prob[:, :, :], hot[:, :, :], ALU.mult))
                chain.end()

            def add_expert(g, e):
                if e == 0:
                    dve.wait_ge(stored, 48 * g + 1)
                for t, (t0, n) in enumerate(TILES):
                    if e > 0:
                        dve.wait_ge(y_added, 9 * g + (3 * e + t - 2))
                    dve.scalar_tensor_tensor(y[0:n, t, :], b_down[0:n, e, :], gates[0:n, t, e:e + 1],
                                             (h3 if e == 0 else y)[0:n, t, :], ALU.mult, ALU.add).then_inc(y_biased, 1)
                for t, (t0, n) in enumerate(TILES):
                    u = 3 * e + t
                    dve.wait_ge(down_mm, 9 * g + u + 1)
                    dve.wait_ge(y_biased, 9 * g + u + 1)
                    dve.scalar_tensor_tensor(y[0:n, t, :], ps[DOWN_BANKS[e][t]][0:n, 0:C2], gates[0:n, t, e:e + 1],
                                             y[0:n, t, :], ALU.mult, ALU.add).then_inc(y_added, 1)

            dve.wait_ge(nat_mm, 1)
            dve.tensor_copy(w_stem[:, :, :], ps[5][0:96, 0:192]).then_inc(nat_evac, 1)
            chain = Chain(dve, bn_chain, 0, 2 + RSQRT + 3)
            chain.link(dve.tensor_copy(bn[:, :, :], ps[5][0:96, 192:207]))
            chain.link(dve.tensor_scalar(bn_tmp[:, 0, :], bn[:, 4, :], EPS, None, ALU.add))
            rsqrt(chain, bn_scale[:, :], bn_tmp[:, 0, :], bn_tmp[:, 1, :].bitcast(I32), bn_bias[:, :])
            chain.link(dve.tensor_tensor(bn_scale[:, :], bn_scale[:, :], bn[:, 1, :], ALU.mult))
            chain.link(dve.tensor_tensor(bn_bias[:, :], bn[:, 0, :], bn[:, 3, :], ALU.subtract))
            chain.link(dve.tensor_tensor(bn_bias[:, :], bn_bias[:, :], bn_scale[:, :], ALU.mult))
            dve.tensor_tensor(bn_bias[:, :], bn_bias[:, :], bn[:, 2, :], ALU.add).then_inc(bn_ready, 1)
            chain.end()
            stem_xt(0, 0)
            stem_xt(0, 1)
            dve.wait_ge(nat_mm, 2)
            dve.tensor_copy(w_off[:, :, :], ps[6][0:C1, 0:512]).then_inc(nat_evac, 1)
            dve.wait_ge(nat_mm, 3)
            dve.wait_ge(ld_small, 16 * 8)
            dve.tensor_copy(w_gate[:, :, :], ps[7][0:96, 0:8].rearrange("p (t e) -> p t e", t=2)[:, :, 0:3])
            dve.tensor_copy(b_up[:, :], ps[7][:, 32:32 + EXPERTS * FCH])
            dve.tensor_tensor(w_feat[0:64, :].rearrange("p (h m) -> p h m", h=4),
                              ps[7][0:64, 64:128].unsqueeze(1).to_broadcast([64, 4, M]),
                              headmask[:, :].rearrange("p (h m) -> p h m", h=4), ALU.mult).then_inc(nat_evac, 1)
            dve.wait_ge(zeroed, 5)
            for s in range(2):
                leaky(0, s)
                stem_ht(0, s)
            part_copy(0)
            dve.wait_ge(ld_offb, 16 * 6)
            dve.tensor_tensor(point[:, :], point[:, :], offb[:, :], ALU.add).then_inc(point_ready, 1)
            dve.wait_ge(point_ready, 1)
            sample_points(0)
            for t in range(3):
                ones = mv[:, t, :, :].rearrange("t i (h c) -> t i h c", c=VW)[:, :, :, DH]
                ins = dve.tensor_copy(ones, own[:, :].unsqueeze(2).to_broadcast([TT, 3, HEADS]))
            ins.then_inc(feat_ready, 1)
            for u in range(8):
                m, k0 = u // 4, 4 * (u % 4)
                dve.wait_ge(nat_mm, u + 4)
                dve.tensor_copy(w_dcn[:, k0:k0 + 4, 96 * m:96 * m + 96],
                                ps[5 + u % 3][0:C1, 0:384].rearrange("c (k o) -> c k o", k=4)).then_inc(nat_evac, 1)

            def step(g, has_last, has_next):
                if has_last:
                    gate_logits(g - 1)
                    combine(g, 2, 6)
                    gate(g - 1)
                    combine(g, 6, 8)
                    add_expert(g - 1, 0)
                    combine(g, 8, BATCHES)
                    add_expert(g - 1, 1)
                else:
                    combine(g, 2, BATCHES)
                dcn_leaky(g)
                if has_next:
                    stem_xt(g + 1, 0)
                if not has_last:
                    dve.wait_ge(ld_attn, 16 * 29)
                norm_in(g)
                if has_next:
                    stem_xt(g + 1, 1)
                    for s in range(2):
                        leaky(g + 1, s)
                        stem_ht(g + 1, s)
                    part_copy(g + 1)
                    sample_points(g + 1)
                add_proj_bias(g)
                q_copies(g)
                values(g)
                kv_low(g)
                outputs(g)
                norms_out(g)
                if has_last:
                    add_expert(g - 1, 2)
                if has_next:
                    combine(g + 1, 0, 2)
                if not has_last:
                    dve.wait_ge(ld_ffn, 16 * 6)

            combine(0, 0, 2)
            steps(dve, step)
            gate_logits(GROUPS - 1)
            gate(GROUPS - 1)
            for e in range(EXPERTS):
                add_expert(GROUPS - 1, e)


_INS = ["x", "L0_tok_stem_w", "L0_tok_stem_b", "L0_tok_bn1_g", "L0_tok_bn1_b", "L0_tok_bn1_m", "L0_tok_bn1_v",
        "L0_tok_off_w", "L0_tok_off_b", "L0_tok_dcn_w", "L0_tok_dcn_b", "L0_tok_bn2_g", "L0_tok_bn2_b", "L0_tok_bn2_m",
        "L0_tok_bn2_v", "L0_attn_W_qkv", "L0_attn_W_proj", "L0_attn_b_proj", "L0_attn_gamma", "L0_attn_beta",
        "L0_attn_random_features", "L0_ffn_Wg", "L0_ffn_W1", "L0_ffn_b1", "L0_ffn_W2", "L0_ffn_b2"]


def kernel(**inputs):
    import numpy as _np
    import concourse.bacc as _bacc
    from concourse import mybir as _mybir
    from concourse.bass_utils import run_bass_kernel_spmd as _run

    nc = _bacc.Bacc("TRN2", target_bir_lowering=False, num_devices=1)
    arrays, aps = {}, {}
    for name in _INS:
        x = _np.ascontiguousarray(inputs[name])
        arrays[f"in_{name}_dram"] = x
        aps[name] = nc.dram_tensor(f"in_{name}_dram", x.shape, _mybir.dt.from_np(x.dtype), kind="ExternalInput").ap()
    for name, x in tables().items():
        arrays[f"table_{name}_dram"] = x
        aps[name] = nc.dram_tensor(f"table_{name}_dram", x.shape, _mybir.dt.from_np(x.dtype), kind="ExternalInput").ap()
    out = nc.dram_tensor("out_0_dram", (IMAGES, TOK_IMG, C2), _mybir.dt.float32, kind="ExternalOutput").ap()
    build(nc, aps, out)
    r = _run(nc, [arrays], core_ids=[0])
    return r.results[0]["out_0_dram"]
```

```python
from contextlib import ExitStack

import numpy as np

import concourse.bass as bass
from concourse import mybir

F32 = mybir.dt.float32
I32 = mybir.dt.int32
ALU = mybir.AluOpType
ACT = mybir.ActivationFunctionType
AX = mybir.AxisListType

IMAGES, CIN, SIDE = 32, 3, 96
STRIDE = 4
C1, C2 = 96, 192
GRID = SIDE // STRIDE
OUT_SIDE = GRID // STRIDE
TOK_IMG = OUT_SIDE * OUT_SIDE
TAPS = STRIDE * STRIDE
GROUP = 8
GROUPS = IMAGES // GROUP
SUB = GROUP // 2
ROWS = SUB * GRID
TOK = GROUP * TOK_IMG
SUBTOK = TOK // 2
COLS = TOK * TAPS // 128
FULL = TOK // 128
REST = TOK - 128 * FULL
BATCH = 3
BATCHES = COLS // BATCH
SLOTS = 6
CELL = 4 * C1
PAD = GRID
HEADS, DH, M = 12, 16, 64
PAIRS = HEADS // 2
VW = DH + 1
EXPERTS, FF = 3, 768
FCH = FF // 128
TILES = ((0, 108), (108, 108), (216, 72))
TT = 108
SLOPE = 0.01
EPS = 1e-5


def tables():
    p = np.arange(128)[:, None]
    col = np.arange(COLS)[None, :]
    full = col < FULL * TAPS
    tok = np.where(full, 128 * (col // TAPS) + p, 128 * FULL + p % 32)
    tap = np.where(full, col % TAPS, 4 * (col - FULL * TAPS) + p // 32)
    py, px = tok % TOK_IMG // OUT_SIDE, tok % OUT_SIDE
    point = np.stack([STRIDE * py + tap // STRIDE, STRIDE * px + tap % STRIDE], 2)
    row = PAD + tok // TOK_IMG * GRID * GRID
    r = np.arange(128)[:, None]
    c = np.arange(4 * M)[None, :]
    same_head = (r % 64) // DH == c // M
    head = np.where(r < 64, 1.0, -0.5) * same_head
    t = np.arange(TT)
    same_img = t[:, None] // TOK_IMG == t[None, :] // TOK_IMG
    f = np.float32
    return {
        "ident": np.eye(128, dtype=f),
        "point": point.reshape(128, 2 * COLS).astype(f),
        "row": row.astype(f),
        "head": head.astype(f),
        "own": (t[:, None] // TOK_IMG == np.arange(3)[None, :]).astype(f),
        "mean": (same_img / TOK_IMG).astype(f),
        "fold": (p % 32 == np.arange(32)[None, :]).astype(f),
    }


def build(nc, a, out):
    a = dict(a)
    w = {n.split("_", 2)[2] if n.startswith("L0_") else n: ap for n, ap in a.items()}
    table = nc.dram_tensor("cells", (PAD + GROUP * GRID * GRID, CELL), F32, kind="Internal").ap()
    out_rows = out.rearrange("b t c -> (b t) c")

    with ExitStack() as ctx:
        def sb(name, shape, dt=F32):
            return ctx.enter_context(nc.sbuf_tensor(name, shape, dt))

        def sem(name):
            return ctx.enter_context(nc.semaphore(name))

        ident = sb("ident_sb", [128, 128])
        point = sb("point_sb", [128, 2 * COLS])
        offb = sb("offb_sb", [128, 2 * COLS])
        rowbase = sb("row_sb", [128, COLS])
        own = sb("own_sb", [TT, 3])
        mean = sb("mean_sb", [TT, TT])
        fold = sb("fold_sb", [128, 32])
        headmask = sb("headmask", [64, 4 * M])
        w_stem = sb("w_stem", [96, 2, C1])
        w_off = sb("w_off", [C1, TAPS, 32])
        w_dcn = sb("w_dcn", [C1, TAPS, C2])
        w_qk = sb("w_qk", [96, 2, 6, 2, 64])
        w_v = sb("w_v", [96, 2, C2])
        w_proj = sb("w_proj", [96, 2, C2])
        w_feat = sb("w_feat", [128, 4 * M])
        w_gate = sb("w_gate", [96, 2, EXPERTS])
        w_up = sb("w_up", [96, 2, EXPERTS, FF])
        w_down = sb("w_down", [128, EXPERTS, FCH, C2])
        b_up = sb("b_up", [128, EXPERTS * FCH])
        b_down = sb("b_down", [TT, EXPERTS, C2])
        gamma = sb("gamma_sb", [TT, C2])
        beta = sb("beta_sb", [TT, C2])
        b_proj = sb("b_proj_sb", [TT, C2])
        bn = sb("bn", [96, 5, 3])
        bn_scale = sb("bn_scale", [96, 3])
        bn_bias = sb("bn_bias", [96, 3])
        bn_tmp = sb("bn_tmp", [96, 2, 3])
        bn_nat = sb("bn_nat", [15, 96])
        gate_nat = sb("gate_nat", [EXPERTS, C2])
        bup_nat = sb("bup_nat", [EXPERTS * FCH, 128])
        feat_nat = sb("feat_nat", [M, 4, DH])

        xs = sb("xs", [ROWS, CIN * STRIDE, SIDE])
        xt = sb("xt", [96, GRID // 2, ROWS])
        h = sb("h", [C1, 2, GRID, ROWS])
        xr = sb("xr", [ROWS, 2, SIDE * CIN * STRIDE])
        part = sb("part", [128, TOK])
        pos = sb("pos", [128, 2 * COLS])
        clipped = sb("clipped", [128, 2 * COLS])
        whole_i = sb("whole_i", [128, 2 * COLS], I32)
        whole = sb("whole", [128, 2 * COLS])
        hat = sb("hat", [128, 2 * COLS, 2])
        above = hat[:, :, 0]
        corner = sb("corner", [128, COLS, 2, 2])
        cell_f = sb("cell_f", [128, COLS])
        cell = sb("cell", [128, COLS], I32)
        ring = sb("ring", [128, SLOTS, BATCH, CELL])
        acc = sb("acc", [128, 3, BATCH, C1])
        shared = sb("shared", [128, TAPS * TOK])
        samp = shared[0:C1, :].rearrange("c (k t) -> c k t", k=TAPS)
        QP_END = 3 * HEADS * M + PAIRS * TOK
        kp = shared[0:TT, 0:3 * HEADS * M].rearrange("t (a f) -> t a f", a=3)
        qp = shared[:, 3 * HEADS * M:3 * HEADS * M + PAIRS * TOK].rearrange("f (p t) -> f p t", p=PAIRS)
        h2t = sb("h2t", [96, 2, TOK])
        h2 = sb("h2", [TT, 3, C2])
        xn = sb("xn", [TT, 3, C2])
        lnT = sb("lnT", [96, 2, TOK])
        qk = sb("qk", [128, 6, TOK])
        mv = sb("mv", [TT, 3, 3, HEADS * VW])
        kv = sb("kv", [128, 3, PAIRS, 3, 2 * VW])
        o = sb("o", [TT, 3, PAIRS, 2 * VW])
        den = sb("den", [TT, 3, HEADS])
        xa = shared[0:TT, QP_END:QP_END + 3 * C2].rearrange("t (a c) -> t a c", a=3)
        h3 = sb("h3", [TT, 3, C2])
        xfT = sb("xfT", [96, 2, TOK])
        stats = sb("stats", [TT, 3, 6])
        mvar = sb("mvar", [TT, 3, 2])
        rs_x = sb("rs_x", [TT, 3])
        rs_i = sb("rs_i", [TT, 3], I32)
        rs_t = sb("rs_t", [TT, 3])
        rstd = sb("rstd", [TT, 3])
        rt = sb("rt", [TT, 3, EXPERTS])
        logit = sb("logit", [TT, 3, EXPERTS])
        rmax = sb("rmax", [TT, 3])
        rsum = sb("rsum", [TT, 3])
        prob = sb("prob", [TT, 3, EXPERTS])
        hot = sb("hot", [TT, 3, EXPERTS])
        gates = sb("gates", [TT, 3, EXPERTS])
        hid = sb("hid", [128, 2, FCH, TOK])
        y = sb("y", [TT, 3, C2])

        flat = ring[:, :, :, :].rearrange("p s b c -> p (s b c)")
        HALF = GRID * C1
        ht = flat[0:ROWS, 0:2 * HALF].rearrange("r (s x c) -> r s x c", s=2, c=C1)
        dcn_nat = hid[0:96, :, :, :].rearrange("p e f t -> p (e f t)")[:, 0:2 * C1 * TAPS].rearrange("o (m k) -> o m k", m=2)
        off_nat = shared[0:32, 2 * C1 * TAPS:3 * C1 * TAPS]
        stem_nat = flat[0:96, 2 * HALF:2 * HALF + 192].rearrange("o (x k) -> o x k", x=2)

        ps = [ctx.enter_context(nc.psum_tensor(f"bank{i}", [128, 512], F32)) for i in range(8)]

        ld_stem, ld_small, ld_dcn, ld_attn, ld_ffn = (sem(n) for n in ("ld_stem", "ld_small", "ld_dcn", "ld_attn", "ld_ffn"))
        ld_bn, ld_offb, ld_nat, point_ready = sem("ld_bn"), sem("ld_offb"), sem("ld_nat"), sem("point_ready")
        xn_biased = sem("xn_biased")
        zeroed = sem("zeroed")
        nat_mm, nat_evac = sem("nat_mm"), sem("nat_evac")
        bn_ready, bn_chain, feat_ready = sem("bn_ready"), sem("bn_chain"), sem("feat_ready")
        x_in, x_ready = sem("x_in"), sem("x_ready")
        xt_mm, xt_evac = sem("xt_mm"), sem("xt_evac")
        stem_mm, bn_evac, h_ready = sem("stem_mm"), sem("bn_evac"), sem("h_ready")
        ht_mm, ht_even, ht_odd, h_stored = sem("ht_mm"), sem("ht_even"), sem("ht_odd"), [sem("h_stored0"), sem("h_stored1")]
        off_mm, part_ready, off_tok = sem("off_mm"), sem("part_ready"), sem("off_tok")
        idx_chain, idx_ready = sem("idx_chain"), sem("idx_ready")
        gathered = [sem(f"gathered{i}") for i in range(SLOTS)]
        first_corner, comb_chain, combined = sem("first_corner"), sem("comb_chain"), sem("combined")
        samp_mm, samp_evac = sem("samp_mm"), sem("samp_evac")
        dcn_mm, bn2_evac, h2_ready = sem("dcn_mm"), sem("bn2_evac"), sem("h2_ready")
        t1_mm, t1_evac, ln_chain, xn_ready = sem("t1_mm"), sem("t1_evac"), sem("ln_chain"), sem("xn_ready")
        t2_mm, t2_evac = sem("t2_mm"), sem("t2_evac")
        qk_mm, q_copied, q_squared = sem("qk_mm"), sem("q_copied"), sem("q_squared")
        v_mm, v_evac = sem("v_mm"), sem("v_evac")
        feat_mm, exp_done = sem("feat_mm"), sem("exp_done")
        kv_mm, kv_lo, kv_hi = sem("kv_mm"), sem("kv_lo"), sem("kv_hi")
        o_first = sem("o_first")
        out_mm, o_chain, o_evac, xa_ready = sem("out_mm"), sem("o_chain"), sem("o_evac"), sem("xa_ready")
        t3_mm, t3_evac = sem("t3_mm"), sem("t3_evac")
        proj_mm, ln2_chain, xf_ready = sem("proj_mm"), sem("ln2_chain"), sem("xf_ready")
        t4_mm, t4_evac = sem("t4_mm"), sem("t4_evac")
        rt_mm, rt_copied, logit_mm = sem("rt_mm"), sem("rt_copied"), sem("logit_mm")
        gate_chain, logit_chain, logit_ready, prob_exp = sem("gate_chain"), sem("logit_chain"), sem("logit_ready"), sem("prob_exp")
        up_mm, gelu_done, down_mm, y_added = sem("up_mm"), sem("gelu_done"), sem("down_mm"), sem("y_added")
        y_biased, stored = sem("y_biased"), sem("stored")
        edges = sem("edges")
        pool_turns, dve_turns = sem("pool_turns"), sem("dve_turns")

        FIRST_UPS = ((2, 1), (3, 1), (4, 2))
        TOKEN_BANKS = (7, 0, 1)
        EARLY = min((SUBTOK // 128) * TAPS // BATCH, HALF // (BATCH * CELL))
        HALF_CELLS = PAD + (SUB * GRID - 1) * GRID
        DOWN_BANKS = ((7, 4, 1), (7, 4, 1), (7, 6, 4))

        def later(g):
            return not isinstance(g, int) or g > 0

        class Chain:

            def __init__(self, eng, s, g, per, n=0):
                self.eng, self.s, self.g, self.per, self.n = eng, s, g, per, n

            def add(self, ins):
                self.n += 1
                ins.then_inc(self.s, 1)
                return self.n

            def wait(self, n=None):
                self.eng.wait_ge(self.s, self.g * self.per + (self.n if n is None else n))

            def link(self, ins):
                self.add(ins)
                self.wait()

            def end(self):
                assert self.n == self.per, (self.n, self.per)

        def steps(eng, step):
            step(0, False, True)
            with eng.Fori(1, GROUPS - 1) as g:
                step(g, True, True)
            step(GROUPS - 1, True, False)

        block = ctx.enter_context(nc.Block())

        @block.sync
        def _(sp):
            def load_images(g, s):
                if s == 1 or later(g):
                    sp.wait_ge(x_ready, 2 * g + s)
                for b in range(SUB):
                    img = w["x"][bass.ds(g * GROUP + (SUB * s + b), 1)]
                    sp.dma_start(xs[GRID * b:GRID * (b + 1), :, :].rearrange("y (c k) x -> y c (k x)", c=CIN),
                                 img.rearrange("n c (y k) x -> (n y) c (k x)", k=STRIDE)).then_inc(x_in, 16)

            def store_cells(g):
                if later(g):
                    for i in range(SLOTS):
                        sp.wait_ge(gathered[i], 96 * g)
                for s in range(2):
                    sp.wait_ge(ht_even, 6 * g + 3 * (s + 1))
                    sp.wait_ge(ht_odd, 6 * g + 3 * (s + 1))
                    for slot in range(2):
                        first = PAD + s * SUB * GRID * GRID - slot * GRID
                        dst = table[first:first + ROWS * GRID, slot * 2 * C1:(slot + 1) * 2 * C1]
                        src = bass.AP(ring, s * HALF, [[SLOTS * BATCH * CELL, ROWS], [C1, GRID - 1], [1, 2 * C1]])
                        sp.dma_start(dst.rearrange("(p x) c -> p x c", p=ROWS)[:, 0:GRID - 1, :], src).then_inc(h_stored[s], 16)

            def store_out(g):
                sp.wait_ge(y_added, 9 * (g + 1))
                for t, (t0, n) in enumerate(TILES):
                    sp.dma_start(out_rows[bass.ds(g * TOK + t0, n), :], y[0:n, t, :]).then_inc(stored, 16)

            sp.sem_inc(stored, 1)
            sp.dma_start(stem_nat[:, 0, 0:48], w["stem_w"].rearrange("o c k l -> o (c k l)")).then_inc(ld_stem, 16)
            sp.dma_start(stem_nat[:, 1, 48:96], w["stem_w"].rearrange("o c k l -> o (c k l)")).then_inc(ld_stem, 16)
            sp.dma_start(ident[:, :], w["ident"]).then_inc(ld_stem, 16)
            load_images(0, 0)
            load_images(0, 1)
            sp.dma_start(off_nat, w["off_w"].rearrange("o c k l -> o (c k l)")).then_inc(ld_small, 16)
            sp.dma_start(point[:, :], w["point"]).then_inc(ld_small, 16)
            sp.dma_start(rowbase[:, :], w["row"]).then_inc(ld_small, 16)
            sp.dma_start(fold[:, :], w["fold"]).then_inc(ld_small, 16)
            sp.dma_start(headmask[:, :], w["head"][0:64, :]).then_inc(ld_small, 16)
            sp.dma_start(w_feat[64:128, :], w["head"][64:128, :]).then_inc(ld_small, 16)
            sp.dma_start(own[:, :], w["own"]).then_inc(ld_small, 16)
            sp.dma_start(mean[:, :], w["mean"]).then_inc(ld_small, 16)
            sp.dma_start(dcn_nat, w["dcn_w"].rearrange("(m o) c k l -> o m (c k l)", m=2)).then_inc(ld_dcn, 16)
            load_images(1, 0)
            load_images(1, 1)
            sp.wait_ge(zeroed, 3)
            zeros = kv[:, :, :, :, :].rearrange("p t q i c -> p (t q i c)")
            last = GROUP * GRID * GRID
            sp.dma_start(table[0:PAD - 1, 0:2 * C1], zeros[0:PAD - 1, 0:2 * C1]).then_inc(edges, 16)
            sp.dma_start(table[last:last + GRID - 1, 2 * C1:], zeros[0:GRID - 1, 0:2 * C1]).then_inc(edges, 16)
            sp.dma_start(table[PAD - 1:PAD, :], zeros[0:1, 0:CELL]).then_inc(edges, 16)
            sp.dma_start(table[PAD:, :].rearrange("(p a x) c -> p a x c", a=2, x=GRID)[:, :, GRID - 1, :],
                         zeros[0:GROUP * GRID // 2, 0:2 * CELL].rearrange("p (a c) -> p a c", a=2)).then_inc(edges, 16)
            store_cells(0)
            for i in range(SLOTS):
                sp.wait_ge(gathered[i], 96)
            for n, kt in ((n, kt) for n in range(6) for kt in range(2)):
                for d in range(2):
                    sp.dma_start(w_qk[:, kt, n, d, :], w["W_qkv"][96 * kt:96 * kt + 96, 64 * n:64 * n + 64]).then_inc(ld_attn, 16)
            sp.dma_start(w_v[:, :, :], w["W_qkv"][:, 2 * C2:].rearrange("(t p) n -> p t n", t=2)).then_inc(ld_attn, 16)
            sp.dma_start(w_proj[:, :, :], w["W_proj"].rearrange("(t p) n -> p t n", t=2)).then_inc(ld_attn, 16)
            for dst, name in ((gamma, "gamma"), (beta, "beta"), (b_proj, "b_proj")):
                sp.dma_start(dst[:, :], w[name].partition_broadcast(TT)).then_inc(ld_attn, 16)
            for kt in range(2):
                sp.dma_start(w_up[:, kt, :, :], w["W1"][:, 96 * kt:96 * kt + 96, :].rearrange("e p f -> p e f")).then_inc(ld_ffn, 16)
            for e in range(EXPERTS):
                sp.dma_start(w_down[:, e, :, :], w["W2"][e].rearrange("(f p) n -> p f n", p=128)).then_inc(ld_ffn, 16)
            sp.dma_start(b_down[:, :, :], w["b2"].rearrange("e n -> (e n)").partition_broadcast(TT)).then_inc(ld_ffn, 16)

            def step(g, has_last, has_next):
                if has_next:
                    if has_last:
                        load_images(g + 1, 0)
                        load_images(g + 1, 1)
                    store_cells(g + 1)
                if has_last:
                    store_out(g - 1)

            steps(sp, step)
            store_out(GROUPS - 1)
            sp.wait_ge(stored, 16 * 3 * GROUPS + 1)

        @block.gpsimd
        def _(pool):
            pool.memset(stem_nat[:, 0, 48:96], 0.0).then_inc(zeroed, 1)
            pool.memset(stem_nat[:, 1, 0:48], 0.0).then_inc(zeroed, 1)
            pool.memset(kv[:, :, :, :, :], 0.0).then_inc(zeroed, 1)
            pool.memset(mvar[:, :, :], 1.0).then_inc(zeroed, 1)
            pool.memset(logit[:, :, :], 0.0).then_inc(zeroed, 1)

            def rearrange_rows(g):
                for s in range(2):
                    if later(g):
                        pool.wait_ge(xt_mm, 6 * g + 3 * s - 3)
                    pool.wait_ge(x_in, 128 * g + 64 * (s + 1))
                    pool.sem_inc(pool_turns, 1)
                    pool.tensor_copy(xr[:, s, :].rearrange("p (x r k) -> p x r k", x=GRID, k=STRIDE),
                                     xs[:, :, :].rearrange("p r (x k) -> p x r k", k=STRIDE)).then_inc(x_ready, 1)

            def gather(g):
                pool.wait_ge(idx_ready, 2 * g + 2)
                pool.wait_ge(h_stored[0], 32 * (g + 1))
                for k in range(BATCHES):
                    if k == EARLY:
                        pool.wait_ge(h_stored[1], 32 * (g + 1))
                    if k >= SLOTS:
                        pool.wait_ge(combined, BATCH * (BATCHES * g + (k - SLOTS + 1)))
                    elif later(g):
                        pool.wait_ge(combined, BATCH * (BATCHES * (g - 1) + (k + SLOTS + 1)))
                    pool.sem_inc(pool_turns, 1)
                    for j in range(BATCH):
                        col = BATCH * k + j
                        pool.indirect_dma_start(
                            ring[:, k % SLOTS, j, :], None, table[0:HALF_CELLS, :] if k < EARLY else table,
                            bass.IndirectOffsetOnAxis(ap=cell[:, col:col + 1], axis=0)).then_inc(gathered[k % SLOTS], 16)

            rearrange_rows(0)
            rearrange_rows(1)
            pool.wait_ge(edges, 64)
            pool.wait_ge(nat_mm, 1)
            gather(0)

            def step(g, has_last, has_next):
                if has_next:
                    if has_last:
                        rearrange_rows(g + 1)
                    gather(g + 1)

            steps(pool, step)

        @block.tensor
        def _(pe):
            def stem_x(g, s, first=0, last=3):
                pe.wait_ge(x_ready, 2 * g + s + 1)
                for j in range(first, last):
                    u = 3 * s + j
                    if u >= 2:
                        pe.wait_ge(xt_evac, 6 * g + (u - 1))
                    for i in range(4):
                        mm = pe.transpose(ps[5 + u % 2][0:96, ROWS * i:ROWS * (i + 1)], xr[:, s, 96 * (4 * j + i):96 * (4 * j + i + 1)],
                                          ident[0:ROWS, 0:ROWS])
                    mm.then_inc(xt_mm, 1)

            def stem_products(g, s, first=0, last=6):
                for i in range(first, last):
                    n = 6 * s + i
                    pe.wait_ge(xt_evac, 6 * g + (3 * s + i // 2 + 1))
                    if n >= 2:
                        pe.wait_ge(bn_evac, 12 * g + (n - 1))
                    pe.matmul(ps[2 + n % 2][0:C1, 0:4 * ROWS], w_stem[:, i % 2, :],
                              xt[:, 4 * (i // 2):4 * (i // 2) + 4, :], start=True, stop=True).then_inc(stem_mm, 1)

            def stem_rows(g):
                for s in range(2):
                    for j in range(6):
                        u = 6 * s + j
                        pe.wait_ge(h_ready, 6 * g + (3 * s + j // 2 + 1))
                        if u < 2:
                            if later(g):
                                pe.wait_ge(t1_evac, 3 * g)
                        else:
                            pe.wait_ge((ht_even, ht_odd)[u % 2], 6 * g + u // 2)
                        for i in range(4):
                            mm = pe.transpose(ps[u % 2][0:ROWS, C1 * i:C1 * (i + 1)], h[:, s, 4 * j + i, :],
                                              ident[0:C1, 0:C1])
                        mm.then_inc(ht_mm, 1)
                    for kw in range(STRIDE):
                        for kh in range(STRIDE):
                            rhs = bass.AP(h, s * GRID * ROWS + kw * ROWS + kh,
                                          [[2 * GRID * ROWS, C1], [STRIDE, SUB * OUT_SIDE], [STRIDE * ROWS, OUT_SIDE]])
                            mm = pe.matmul(ps[4][32 * kh:32 * kh + 32, SUBTOK * s:SUBTOK * (s + 1)],
                                           w_off[:, STRIDE * kh + kw, :], rhs,
                                           start=(kw == 0), stop=(kw == STRIDE - 1), skip_group_check=True)
                    mm.then_inc(off_mm, 1)

            def offsets_by_token(g):
                pe.wait_ge(part_ready, g + 1)
                for t in range(FULL):
                    pe.matmul(ps[4][:, TOK + 32 * t:TOK + 32 * t + 32], part[:, 128 * t:128 * t + 128], fold[:, :],
                              start=True, stop=True, skip_group_check=True)
                for q in range(4):
                    mm = pe.matmul(ps[4][32 * q:32 * q + 32, TOK + 64:TOK + 72], part[:, 128 * FULL:TOK],
                                   fold[:, :].rearrange("p (j q x) -> p j q x", j=4, q=4)[:, :, q, :],
                                   start=True, stop=True, skip_group_check=True)
                mm.then_inc(off_tok, 1)

            def dcn_weights(u):
                m, k0 = u // 4, 4 * (u % 4)
                if u == 0:
                    pe.wait_ge(ld_dcn, 16)
                    pe.wait_ge(xt_evac, 12)
                    pe.wait_ge(nat_evac, 3)
                elif u >= 3:
                    pe.wait_ge(nat_evac, u + 1)
                for i in range(4):
                    mm = pe.transpose(ps[5 + u % 3][0:C1, 96 * i:96 * i + 96],
                                      dcn_nat[:, m, :].rearrange("o (c k) -> o c k", k=TAPS)[:, :, k0 + i], ident[0:96, 0:96])
                mm.then_inc(nat_mm, 1)

            def dcn(g, has_last, has_next):
                for k in range(BATCHES):
                    pe.wait_ge(combined, BATCH * (BATCHES * g + k + 1))
                    if k >= 2:
                        pe.wait_ge(samp_evac, BATCHES * g + (k - 1))
                    elif later(g) and k == 0:
                        pe.wait_ge(rt_copied, g)
                    elif later(g):
                        pe.wait_ge(logit_ready, g)
                    else:
                        pe.wait_ge(bn_evac, 24)
                    for j in range(BATCH):
                        mm = pe.transpose(ps[2 + k % 2][0:C1, 128 * j:128 * (j + 1)], acc[:, k % 3, j, :], ident[:, :])
                    mm.then_inc(samp_mm, 1)
                    if has_last:
                        if k < 3:
                            up(g - 1, 0, *FIRST_UPS[k])
                        elif k < 6:
                            down(g - 1, 0, k - 3)
                        elif k < 9:
                            up(g - 1, 1, 2 * (k - 6), 2)
                        else:
                            down(g - 1, 1, k - 9)
                    elif k < 8:
                        dcn_weights(k)
                if not has_last:
                    pe.wait_ge(nat_evac, 11)
                pe.wait_ge(samp_evac, BATCHES * (g + 1))
                if later(g):
                    pe.wait_ge(t4_evac, 2 * g)
                else:
                    pe.wait_ge(ht_even, 6)
                    pe.wait_ge(ht_odd, 6)
                for m in range(2):
                    if m == 1 and has_last:
                        pe.wait_ge(y_added, 9 * g - 3)
                    for k in range(TAPS):
                        mm = pe.matmul(ps[m][0:96, 0:TOK], w_dcn[:, k, 96 * m:96 * m + 96], samp[:, k, :],
                                       start=(k == 0), stop=(k == TAPS - 1))
                    mm.then_inc(dcn_mm, 1)
                    if has_last and has_next:
                        stem_x(g + 1, 0, 2 * m, 2 + m)

            def tokens(g):
                pe.wait_ge(h2_ready, 2 * (g + 1))
                for t, (t0, n) in enumerate(TILES):
                    for m in range(2):
                        mm = pe.transpose(ps[TOKEN_BANKS[t]][0:n, 96 * m:96 * m + 96], h2t[:, m, t0:t0 + n], ident[0:96, 0:96])
                    mm.then_inc(t1_mm, 1)

            def channels(g, src, ready, s):
                for t, (t0, n) in enumerate(TILES):
                    pe.wait_ge(ready, 3 * g + t + 1)
                    for m in range(2):
                        mm = pe.transpose(ps[m][0:96, t0:t0 + n], src[0:n, t, 96 * m:96 * m + 96], ident[0:n, 0:n])
                mm.then_inc(s, 1)

            def query_key(g, n, has_next):
                if n >= 3:
                    pe.wait_ge(q_copied, 6 * g + (n - 2))
                    pe.wait_ge(q_squared, 6 * g + (n - 2))
                elif has_next and n < 2:
                    pe.wait_ge(bn_evac, 12 * (g + 2))
                elif has_next:
                    pe.wait_ge(idx_ready, 2 * g + 4)
                for kt in range(2):
                    mm = pe.matmul(ps[2 + n % 3][:, 0:TOK], w_qk[:, kt, n, :, :].rearrange("p d c -> p (d c)"),
                                   lnT[:, kt, :], start=(kt == 0), stop=(kt == 1))
                mm.then_inc(qk_mm, 1)

            def value(g, t):
                t0, n = TILES[t]
                if t == 2:
                    pe.wait_ge(v_evac, 3 * g + 1)
                for kt in range(2):
                    mm = pe.matmul(ps[t % 2][0:n, 0:C2], lnT[:, kt, t0:t0 + n], w_v[:, kt, :],
                                   start=(kt == 0), stop=(kt == 1))
                mm.then_inc(v_mm, 1)

            def qkv(g, has_next):
                pe.wait_ge(t2_evac, 2 * (g + 1))
                query_key(g, 0, has_next)
                query_key(g, 1, has_next)
                value(g, 0)
                value(g, 1)
                query_key(g, 2, has_next)
                query_key(g, 3, has_next)
                value(g, 2)
                query_key(g, 4, has_next)
                query_key(g, 5, has_next)

            def features(g):
                pe.wait_ge(v_evac, 3 * (g + 1))
                for u in range(12):
                    if u < 3:
                        pe.wait_ge(q_copied, 6 * g + (5 if u == 0 else 6))
                        pe.wait_ge(q_squared, 6 * g + (5 if u == 0 else 6))
                    if u >= 4:
                        pe.wait_ge(exp_done, 12 * g + (u - 3))
                    bank = ps[u % 4]
                    if u < 6:
                        t0, n = TILES[u // 2]
                        for j in ((0, 1) if u % 2 == 0 else (2,)):
                            mm = pe.matmul(bank[0:n, 256 * (j % 2):256 * (j % 2) + 256], qk[:, 3 + j, t0:t0 + n],
                                           w_feat[:, :], start=True, stop=True)
                    else:
                        p = u - 6
                        mm = pe.matmul(bank[:, 0:TOK], w_feat[:, 128 * (p % 2):128 * (p % 2) + 128], qk[:, p // 2, :],
                                       start=True, stop=True)
                    mm.then_inc(feat_mm, 1)

            def kv_sums(g):
                pe.wait_ge(exp_done, 12 * g + 10)
                for u in range(6):
                    t, b = u // 2, u % 2
                    n = TILES[t][1]
                    ni = n // TOK_IMG
                    if u >= 3:
                        pe.wait_ge(kv_lo, 6 * g + (u - 2))
                        pe.wait_ge(kv_hi, 6 * g + (u - 2))
                    for i in range(3):
                        p = 3 * b + i
                        mm = pe.matmul(ps[(4, 0, 1)[u % 3]][:, 102 * i:102 * i + 34 * ni], kp[0:n, t, 128 * p:128 * p + 128],
                                       mv[0:n, t, 0:ni, 34 * p:34 * p + 34], start=True, stop=True)
                    mm.then_inc(kv_mm, 1)

            def attend(g):
                pe.wait_ge(exp_done, 12 * (g + 1))
                for u in range(6):
                    t, b = u // 2, u % 2
                    t0, n = TILES[t]
                    ni = n // TOK_IMG
                    pe.wait_ge(kv_lo, 6 * g + (u + 1))
                    pe.wait_ge(kv_hi, 6 * g + (u + 1))
                    if u >= 2:
                        pe.wait_ge(o_evac, 6 * g + (u - 1))
                    for i in range(3):
                        p = 3 * b + i
                        mm = pe.matmul(ps[2 + b][0:n, 102 * i:102 * i + 34 * ni], qp[:, p, t0:t0 + n],
                                       kv[:, t, p, 0:ni, :], start=True, stop=True)
                    mm.then_inc(out_mm, 1)

            def project(g):
                pe.wait_ge(t3_evac, 2 * (g + 1))
                for t, (t0, n) in enumerate(TILES):
                    for kt in range(2):
                        mm = pe.matmul(ps[2 + t][0:n, 0:C2], lnT[:, kt, t0:t0 + n], w_proj[:, kt, :],
                                       start=(kt == 0), stop=(kt == 1))
                    mm.then_inc(proj_mm, 1)

            def route(g):
                pe.wait_ge(t4_evac, 2 * (g + 1))
                for t, (t0, n) in enumerate(TILES):
                    for kt in range(2):
                        mm = pe.matmul(ps[2][0:n, 4 * t:4 * t + 3], xfT[:, kt, t0:t0 + n], w_gate[:, kt, :],
                                       start=(kt == 0), stop=(kt == 1))
                mm.then_inc(rt_mm, 1)

            def logits(g):
                pe.wait_ge(rt_copied, g + 1)
                for t, (t0, n) in enumerate(TILES):
                    mm = pe.matmul(ps[3][0:n, 4 * t:4 * t + 3], mean[0:n, 0:n], rt[0:n, t, :], start=True, stop=True)
                mm.then_inc(logit_mm, 1)

            def up(g, e, first=0, count=FCH):
                if e == 0 and first == 0:
                    pe.wait_ge(t4_evac, 2 * (g + 1))
                for f in range(first, first + count):
                    n = FCH * e + f
                    if n >= 2:
                        pe.wait_ge(gelu_done, 18 * g + (n - 1))
                    for kt in range(2):
                        mm = pe.matmul(ps[5 + n % 2][:, 0:TOK], w_up[:, kt, e, 128 * f:128 * f + 128], xfT[:, kt, :],
                                       start=(kt == 0), stop=(kt == 1))
                    mm.then_inc(up_mm, 1)

            def down(g, e, t):
                t0, n = TILES[t]
                pe.wait_ge(gelu_done, 18 * g + 6 * (e + 1))
                if e > 0:
                    pe.wait_ge(y_added, 9 * g + 3 * e)
                for f in range(FCH):
                    mm = pe.matmul(ps[DOWN_BANKS[e][t]][0:n, 0:C2], hid[:, e % 2, f, t0:t0 + n],
                                   w_down[:, e, f, :], start=(f == 0), stop=(f == FCH - 1))
                mm.then_inc(down_mm, 1)

            pe.wait_ge(ld_stem, 48)
            pe.wait_ge(zeroed, 2)
            pe.wait_ge(ld_bn, 16 * 10)
            pe.transpose(ps[5][0:96, 192:207], bn_nat[:, :], ident[0:15, 0:15])
            for i in range(2):
                mm = pe.transpose(ps[5][0:96, 96 * i:96 * i + 96], stem_nat[:, i, :], ident[0:96, 0:96])
            mm.then_inc(nat_mm, 1)
            pe.wait_ge(nat_evac, 1)
            pe.wait_ge(bn_chain, 1)
            for s in range(2):
                stem_x(0, s)
                stem_products(0, s)
            pe.wait_ge(ld_small, 16 * 8)
            pe.wait_ge(xt_evac, 6)
            for k in range(TAPS):
                mm = pe.transpose(ps[6][0:C1, 32 * k:32 * k + 32],
                                  off_nat.rearrange("o (c k) -> o c k", k=TAPS)[:, :, k], ident[0:32, 0:32])
            mm.then_inc(nat_mm, 1)
            pe.wait_ge(ld_nat, 16 * 6)
            for kt in range(2):
                pe.transpose(ps[7][0:96, 4 * kt:4 * kt + 3], gate_nat[:, 96 * kt:96 * kt + 96], ident[0:3, 0:3])
            pe.transpose(ps[7][:, 32:32 + EXPERTS * FCH], bup_nat[:, :], ident[0:18, 0:18])
            pe.transpose(ps[7][0:64, 64:128], feat_nat[:, :, :].rearrange("m h d -> m (h d)"),
                         ident[0:64, 0:64]).then_inc(nat_mm, 1)
            pe.wait_ge(nat_evac, 2)
            stem_rows(0)
            offsets_by_token(0)
            pe.wait_ge(nat_evac, 2)
            for s in range(2):
                stem_x(1, s)
                stem_products(1, s)

            def step(g, has_last, has_next):
                if has_last:
                    logits(g - 1)
                dcn(g, has_last, has_next)
                if has_last and has_next:
                    stem_products(g + 1, 0, 0, 2)
                tokens(g)
                if not has_last:
                    pe.wait_ge(ld_attn, 16 * 29)
                    pe.wait_ge(feat_ready, 1)
                if has_last and has_next:
                    stem_products(g + 1, 0, 2, 6)
                    stem_x(g + 1, 1)
                    stem_products(g + 1, 1)
                if has_next:
                    stem_rows(g + 1)
                    pe.wait_ge(ht_even, 6 * (g + 2))
                    pe.wait_ge(ht_odd, 6 * (g + 2))
                channels(g, xn, xn_ready, t2_mm)
                if has_next:
                    offsets_by_token(g + 1)
                qkv(g, has_next)
                features(g)
                kv_sums(g)
                attend(g)
                if has_last:
                    up(g - 1, 2, 0, 1)
                channels(g, xa, xa_ready, t3_mm)
                if has_last:
                    up(g - 1, 2, 1, 1)
                project(g)
                if has_last:
                    up(g - 1, 2, 2, 4)
                    down(g - 1, 2, 0)
                    down(g - 1, 2, 1)
                channels(g, xa, xf_ready, t4_mm)
                if not has_last:
                    pe.wait_ge(ld_ffn, 16 * 6)
                if has_last:
                    down(g - 1, 2, 2)
                route(g)
                up(g, 0, 0, 1)
                if has_last:
                    pe.wait_ge(y_added, 9 * g)
                up(g, 0, 1, 1)

            steps(pe, step)
            g = GROUPS - 1
            logits(g)
            up(g, 0, 2, 4)
            for e in range(EXPERTS):
                if e + 1 < EXPERTS:
                    up(g, e + 1, 0, 2)
                for t in range(3):
                    down(g, e, t)
                if e + 1 < EXPERTS:
                    up(g, e + 1, 2, 4)

        @block.scalar
        def _(act):
            def stem_xt(g):
                act.wait_ge(stem_mm, 12 * g + 6)
                for j in range(3):
                    act.wait_ge(xt_mm, 6 * g + 3 + j + 1)
                    act.activation(xt[:, 4 * j:4 * j + 4, :], ps[5 + (3 + j) % 2][0:96, 0:4 * ROWS],
                                   ACT.Copy).then_inc(xt_evac, 1)

            def stem_bn(g, s):
                if later(g):
                    act.wait_ge(off_mm, 2 * (g - 1) + (s + 1))
                for i in range(6):
                    n = 6 * s + i
                    act.wait_ge(stem_mm, 12 * g + n + 1)
                    first = 8 * (i // 2) + i % 2
                    act.activation(h[:, s, first:first + 7:2, :], ps[2 + n % 2][0:C1, 0:4 * ROWS], ACT.Identity,
                                   bias=bn_bias[:, 0:1], scale=bn_scale[:, 0:1]).then_inc(bn_evac, 1)

            def stem_ht(g):
                for s in range(2):
                    for j in range(0, 6, 2):
                        act.wait_ge(ht_mm, 12 * g + 6 * s + j + 1)
                        act.activation(ht[:, s, 4 * j:4 * j + 4, :], ps[0][0:ROWS, 0:4 * C1], ACT.Copy).then_inc(ht_even, 1)

            def first_corners(g, k):
                act.wait_ge(gathered[k % SLOTS], 96 * g + 48 * (k // SLOTS + 1))
                if k >= 3:
                    act.wait_ge(samp_mm, BATCHES * g + (k - 2))
                elif later(g):
                    act.wait_ge(samp_mm, BATCHES * g)
                for j in range(BATCH):
                    ins = act.activation(acc[:, k % 3, j, :], ring[:, k % SLOTS, j, 0:C1], ACT.Copy,
                                         scale=corner[:, BATCH * k + j, 0, 0:1])
                ins.then_inc(first_corner, 1)

            def samp_copy(g, k):
                act.wait_ge(samp_mm, BATCHES * g + k + 1)
                bank = ps[2 + k % 2]
                col, pieces = BATCH * k, []
                while col < BATCH * (k + 1):
                    t = col // TAPS
                    run = min(BATCH * (k + 1), TAPS * (t + 1)) - col
                    src = bank[0:C1, 128 * (col - BATCH * k):128 * (col - BATCH * k + run)]
                    if t < FULL:
                        pieces.append((samp[:, col - TAPS * t:col - TAPS * t + run, 128 * t:128 * t + 128],
                                       src.rearrange("c (r t) -> c r t", r=run)))
                    else:
                        k0 = 4 * (col - TAPS * FULL)
                        pieces.append((samp[:, k0:k0 + 4 * run, 128 * FULL:TOK], src.rearrange("c (r t) -> c r t", r=4 * run)))
                    col += run
                for dst, src in pieces:
                    ins = act.activation(dst, src, ACT.Copy)
                ins.then_inc(samp_evac, 1)

            def dcn_weights(u):
                m, k0 = u // 4, 4 * (u % 4)
                act.wait_ge(nat_mm, u + 4)
                act.activation(w_dcn[:, k0:k0 + 4, 96 * m:96 * m + 96],
                               ps[5 + u % 3][0:C1, 0:384].rearrange("c (k o) -> c k o", k=4), ACT.Copy).then_inc(nat_evac, 1)

            def combine_start(g):
                act.wait_ge(idx_ready, 2 * g + 2)
                for k in range(3):
                    first_corners(g, k)

            def combine(g, has_last):
                if later(g):
                    act.wait_ge(out_mm, 6 * g)
                for k in range(BATCHES):
                    if has_last and 1 <= k < 4:
                        gelus(g - 1, 0, *FIRST_UPS[k - 1])
                    if has_last and k == 3:
                        prob_exps(g - 1)
                    if has_last and 7 <= k < 10:
                        gelus(g - 1, 1, 2 * (k - 7), 2)
                    samp_copy(g, k)
                    if k + 3 < BATCHES:
                        first_corners(g, k + 3)
                    if not has_last and k < 8:
                        dcn_weights(k)

            def dcn_bn(g):
                if later(g):
                    act.wait_ge(t1_mm, 3 * g)
                for m in range(2):
                    act.wait_ge(dcn_mm, 2 * g + m + 1)
                    act.activation(h2t[:, m, :], ps[m][0:96, 0:TOK], ACT.Identity,
                                   bias=bn_bias[:, 1 + m:2 + m], scale=bn_scale[:, 1 + m:2 + m]).then_inc(bn2_evac, 1)

            def copy_banks(g, s, dst, done):
                act.wait_ge(s, g + 1)
                for m in range(2):
                    act.activation(dst[:, m, :], ps[m][0:96, 0:TOK], ACT.Copy).then_inc(done, 1)

            def squares(g):
                for n in range(6):
                    act.wait_ge(qk_mm, 6 * g + n + 1)
                    act.activation(qk[64:128, n, :], ps[2 + n % 3][64:128, 0:TOK], ACT.Square).then_inc(q_squared, 1)

            def exps(g):
                for u in range(12):
                    act.wait_ge(feat_mm, 12 * g + u + 1)
                    bank = ps[u % 4]
                    if u < 6:
                        n = TILES[u // 2][1]
                        w0, w1 = (0, 512) if u % 2 == 0 else (512, 768)
                        act.activation(kp[0:n, u // 2, w0:w1], bank[0:n, 0:w1 - w0], ACT.Exp).then_inc(exp_done, 1)
                    else:
                        act.activation(qp[:, u - 6, :], bank[:, 0:TOK], ACT.Exp).then_inc(exp_done, 1)

            def kv_high(g):
                for u in range(6):
                    t, b = u // 2, u % 2
                    ni = TILES[t][1] // TOK_IMG
                    act.wait_ge(kv_mm, 6 * g + u + 1)
                    src = ps[(4, 0, 1)[u % 3]][64:128, 0:306].rearrange("f (p i c) -> f p i c", p=3, i=3)
                    act.activation(kv[64:128, t, 3 * b:3 * b + 3, 0:ni, VW:2 * VW], src[:, :, 0:ni, VW:2 * VW],
                                   ACT.Copy).then_inc(kv_hi, 1)

            def outputs_first(g):
                for u in range(6):
                    t, b = u // 2, u % 2
                    n = TILES[t][1]
                    act.wait_ge(out_mm, 6 * g + u + 1)
                    src = ps[2 + b][0:n, 0:306].rearrange("t (p i c) -> t p i c", p=3, i=3)
                    act.activation(o[0:n, t, 3 * b:3 * b + 3, :], src[:, :, 0, :], ACT.Copy,
                                   scale=own[0:n, 0:1]).then_inc(o_first, 1)

            def gelus(g, e, start=0, count=FCH):
                if e >= 2:
                    act.wait_ge(down_mm, 9 * g + 3 * (e - 1))
                for f in range(start, start + count):
                    n = FCH * e + f
                    act.wait_ge(up_mm, 18 * g + n + 1)
                    act.activation(hid[:, e % 2, f, :], ps[5 + n % 2][:, 0:TOK], ACT.Gelu,
                                   bias=b_up[:, n:n + 1]).then_inc(gelu_done, 1)

            def prob_exps(g):
                act.wait_ge(logit_ready, g + 1)
                act.activation(prob[:, :, :], logit[:, :, :], ACT.Exp).then_inc(prob_exp, 1)

            for i, name in enumerate(("stem_b", "bn1_g", "bn1_b", "bn1_m", "bn1_v")):
                act.dma_start(bn_nat[3 * i:3 * i + 1, :], w[name].rearrange("(m p) -> m p", m=1)).then_inc(ld_bn, 16)
            for i, name in enumerate(("dcn_b", "bn2_g", "bn2_b", "bn2_m", "bn2_v")):
                act.dma_start(bn_nat[3 * i + 1:3 * i + 3, :], w[name].rearrange("(m p) -> m p", m=2)).then_inc(ld_bn, 16)
            for t in range(FULL):
                act.dma_start(offb[:, 32 * t:32 * t + 32], w["off_b"].partition_broadcast(128)).then_inc(ld_offb, 16)
            for q in range(4):
                taps = w["off_b"].rearrange("(j q x) -> j q x", j=4, q=4)[:, q, :]
                act.dma_start(offb[32 * q:32 * q + 32, 64:72].rearrange("p (j x) -> p j x", j=4),
                               taps.partition_broadcast(32)).then_inc(ld_offb, 16)
            act.dma_start(gate_nat[:, :], w["Wg"]).then_inc(ld_nat, 16)
            act.dma_start(bup_nat[:, :], w["b1"].rearrange("e (f p) -> (e f) p", p=128)).then_inc(ld_nat, 16)
            for i in range(4):
                act.dma_start(feat_nat[:, i, :], w["random_features"]).then_inc(ld_nat, 16)

            act.wait_ge(bn_ready, 1)
            stem_bn(0, 0)
            stem_xt(0)
            stem_bn(0, 1)
            stem_ht(0)
            act.wait_ge(zeroed, 5)
            act.wait_ge(feat_ready, 1)
            stem_bn(1, 0)
            stem_xt(1)
            combine_start(0)
            stem_bn(1, 1)

            def step(g, has_last, has_next):
                if has_last:
                    gelus(g - 1, 0, 0, 2)
                combine(g, has_last)
                dcn_bn(g)
                if has_last and has_next:
                    stem_bn(g + 1, 0)
                    stem_xt(g + 1)
                    stem_bn(g + 1, 1)
                if has_next:
                    stem_ht(g + 1)
                copy_banks(g, t2_mm, lnT, t2_evac)
                squares(g)
                exps(g)
                kv_high(g)
                outputs_first(g)
                copy_banks(g, t3_mm, lnT, t3_evac)
                if has_last:
                    gelus(g - 1, 2)
                if has_next:
                    combine_start(g + 1)
                copy_banks(g, t4_mm, xfT, t4_evac)

            steps(act, step)
            gelus(GROUPS - 1, 0)
            prob_exps(GROUPS - 1)
            for e in range(1, EXPERTS):
                gelus(GROUPS - 1, e)

        @block.vector
        def _(dve):
            def rsqrt(chain, dst, x, ti, tt):
                chain.link(dve.tensor_scalar(ti.bitcast(I32) if ti.dtype != I32 else ti, x.bitcast(I32), 1, None, ALU.logical_shift_right))
                chain.link(dve.tensor_scalar(dst.bitcast(I32), ti, -1.0, float(0x5F3759DF), ALU.mult, ALU.add))
                for _ in range(3):
                    chain.link(dve.tensor_tensor(tt, dst, dst, ALU.mult))
                    chain.link(dve.scalar_tensor_tensor(tt, tt, -0.5, x, ALU.mult, ALU.mult))
                    chain.link(dve.scalar_tensor_tensor(dst, tt, 1.5, dst, ALU.add, ALU.mult))

            RSQRT = 11

            def stem_xt(g, first=0, last=3):
                if later(g):
                    dve.wait_ge(stem_mm, 12 * g)
                for j in range(first, last):
                    dve.wait_ge(xt_mm, 6 * g + j + 1)
                    dve.tensor_copy(xt[:, 4 * j:4 * j + 4, :], ps[5 + j % 2][0:96, 0:4 * ROWS]).then_inc(xt_evac, 1)

            def leaky(g, s, first=0, last=3):
                for j in range(first, last):
                    dve.wait_ge(bn_evac, 12 * g + 6 * s + 2 * (j + 1))
                    part_h = h[:, s, 8 * j:8 * j + 8, :]
                    dve.scalar_tensor_tensor(part_h, part_h, SLOPE, part_h, ALU.mult, ALU.max).then_inc(h_ready, 1)

            def stem_ht(g, s, first=1, last=6):
                for j in range(first, last, 2):
                    dve.wait_ge(ht_mm, 12 * g + 6 * s + j + 1)
                    dve.tensor_copy(ht[:, s, 4 * j:4 * j + 4, :], ps[1][0:ROWS, 0:4 * C1]).then_inc(ht_odd, 1)

            def part_copy(g):
                dve.wait_ge(off_mm, 2 * (g + 1))
                dve.tensor_copy(part[:, :], ps[4][:, 0:TOK]).then_inc(part_ready, 1)

            def sample_points(g):
                dve.wait_ge(off_tok, g + 1)
                chain = Chain(dve, idx_chain, g, 11)
                chain.link(dve.tensor_tensor(pos[:, :], ps[4][:, TOK:TOK + 2 * COLS], point[:, :], ALU.add))
                chain.link(dve.tensor_scalar(clipped[:, :], pos[:, :], 0.0, float(GRID - 2), ALU.max, ALU.min))
                chain.link(dve.tensor_copy(whole_i[:, :], clipped[:, :]))
                chain.link(dve.tensor_copy(whole[:, :], whole_i[:, :]))
                chain.link(dve.tensor_tensor(above, whole[:, :], clipped[:, :], ALU.is_gt))
                chain.link(dve.tensor_tensor(whole[:, :], whole[:, :], above, ALU.subtract))
                wh = whole[:, :].rearrange("p (c x) -> p c x", x=2)
                chain.add(dve.scalar_tensor_tensor(cell_f[:, :], wh[:, :, 0], float(GRID), wh[:, :, 1], ALU.mult, ALU.add))
                chain.link(dve.tensor_tensor(hat[:, :, 0], pos[:, :], whole[:, :], ALU.subtract))
                chain.link(dve.tensor_scalar(hat[:, :, 1], hat[:, :, 0], -1.0, None, ALU.add))
                chain.link(dve.scalar_tensor_tensor(hat[:, :, :], hat[:, :, :], -1.0, hat[:, :, :], ALU.mult, ALU.min))
                chain.link(dve.tensor_scalar(hat[:, :, :], hat[:, :, :], 1.0, 0.0, ALU.add, ALU.max))
                hv = hat[:, :, :].rearrange("p (c x) k -> p c x k", x=2)
                hy = hv[:, :, 0, :].unsqueeze(3).to_broadcast([128, COLS, 2, 2])
                hx = hv[:, :, 1, :].unsqueeze(2).to_broadcast([128, COLS, 2, 2])
                dve.tensor_tensor(cell[:, :], cell_f[:, :], rowbase[:, :], ALU.add).then_inc(idx_ready, 1)
                dve.tensor_tensor(corner[:, :, :, :], hy, hx, ALU.mult).then_inc(idx_ready, 1)
                chain.end()

            def combine(g, first, last):
                chain = Chain(dve, comb_chain, g, 2 * BATCH * BATCHES, 2 * BATCH * first)
                for k in range(first, last):
                    dve.wait_ge(first_corner, BATCHES * g + k + 1)
                    for c in range(1, 4):
                        for j in range(BATCH):
                            if c > 1:
                                chain.wait(2 * BATCH * k + BATCH * (c - 2) + j + 1)
                            dst = acc[:, k % 3, j, :]
                            ins = dve.scalar_tensor_tensor(dst, ring[:, k % SLOTS, j, C1 * c:C1 * (c + 1)],
                                                           corner[:, BATCH * k + j, c // 2, c % 2:c % 2 + 1], dst,
                                                           ALU.mult, ALU.add)
                            if c < 3:
                                chain.add(ins)
                            else:
                                ins.then_inc(combined, 1)

            def dcn_leaky(g, m):
                dve.wait_ge(bn2_evac, 2 * g + m + 1)
                part_h = h2t[:, m, :]
                dve.scalar_tensor_tensor(part_h, part_h, SLOPE, part_h, ALU.mult, ALU.max).then_inc(h2_ready, 1)

            def moments(chain, src):
                for t, (t0, n) in enumerate(TILES):
                    chain.add(dve.bn_stats(stats[0:n, t, :], src[0:n, t, :]))
                chain.wait()
                dve.sem_inc(dve_turns, 1)
                for t, (t0, n) in enumerate(TILES):
                    chain.add(dve.bn_aggr(mvar[0:n, t, :], stats[0:n, t, :]))
                chain.wait()
                chain.link(dve.tensor_scalar(rs_x[:, :], mvar[:, :, 1], EPS, None, ALU.add))
                rsqrt(chain, rstd[:, :], rs_x[:, :], rs_i[:, :], rs_t[:, :])

            MOMENTS = 7 + RSQRT

            def norm(t, n, dst, src):
                return dve.tensor_scalar(dst[0:n, t, :], src[0:n, t, :], mvar[0:n, t, 0:1], rstd[0:n, t:t + 1],
                                         ALU.subtract, ALU.mult)

            def token_copies(g):
                for t, (t0, n) in enumerate(TILES):
                    dve.wait_ge(t1_mm, 3 * g + t + 1)
                    dve.tensor_copy(h2[0:n, t, :], ps[TOKEN_BANKS[t]][0:n, 0:C2]).then_inc(t1_evac, 1)

            def norm_in(g):
                chain = Chain(dve, ln_chain, g, MOMENTS)
                dve.wait_ge(t1_evac, 3 * (g + 1))
                moments(chain, h2)
                for t, (t0, n) in enumerate(TILES):
                    norm(t, n, xn, h2).then_inc(xn_ready, 1)
                dve.wait_ge(xn_ready, 3 * (g + 1))
                chain.end()

            def q_copies(g, first, last):
                for n in range(first, last):
                    dve.wait_ge(qk_mm, 6 * g + n + 1)
                    dve.tensor_copy(qk[0:64, n, :], ps[2 + n % 3][0:64, 0:TOK]).then_inc(q_copied, 1)

            def values(g, first, last):
                for t in range(first, last):
                    n = TILES[t][1]
                    dve.wait_ge(v_mm, 3 * g + t + 1)
                    for i in range(n // TOK_IMG):
                        dst = mv[0:n, t, i, :].rearrange("t (h c) -> t h c", c=VW)[:, :, 0:DH]
                        ins = dve.tensor_scalar(dst, ps[t % 2][0:n, 0:C2].rearrange("t (h c) -> t h c", c=DH),
                                                own[0:n, i:i + 1], None, ALU.mult)
                    ins.then_inc(v_evac, 1)

            def add_biases(g):
                dve.wait_ge(t2_mm, g + 1)
                for t, (t0, n) in enumerate(TILES):
                    dve.tensor_tensor(h2[0:n, t, :], h2[0:n, t, :], beta[0:n, :], ALU.add)
                for t, (t0, n) in enumerate(TILES):
                    ins = dve.tensor_tensor(xn[0:n, t, :], xn[0:n, t, :], b_proj[0:n, :], ALU.add)
                ins.then_inc(xn_biased, 1)

            def kv_low(g):
                for u in range(6):
                    t, b = u // 2, u % 2
                    ni = TILES[t][1] // TOK_IMG
                    dve.wait_ge(kv_mm, 6 * g + u + 1)
                    src = ps[(4, 0, 1)[u % 3]][0:64, 0:306].rearrange("f (p i c) -> f p i c", p=3, i=3)
                    dve.tensor_copy(kv[0:64, t, 3 * b:3 * b + 3, 0:ni, 0:VW], src[:, :, 0:ni, 0:VW]).then_inc(kv_lo, 1)

            def outputs(g):
                chain = Chain(dve, o_chain, g, 2 * 2 + 6)
                for u in range(6):
                    t, b = u // 2, u % 2
                    n = TILES[t][1]
                    dve.wait_ge(o_first, 6 * g + u + 1)
                    src = ps[2 + b][0:n, 0:306].rearrange("t (p i c) -> t p i c", p=3, i=3)
                    dst = o[0:n, t, 3 * b:3 * b + 3, :]
                    images = n // TOK_IMG
                    for i in range(1, images):
                        ins = dve.scalar_tensor_tensor(dst, src[:, :, i, :], own[0:n, i:i + 1], dst, ALU.mult, ALU.add)
                        if i < images - 1:
                            chain.link(ins)
                    ins.then_inc(o_evac, 1)
                    if b == 1:
                        dve.wait_ge(o_evac, 6 * g + (u + 1))
                        ov = o[0:n, t, :, :].rearrange("t p (h c) -> t (p h) c", c=VW)
                        chain.link(dve.tensor_scalar(den[0:n, t, :], ov[:, :, DH], M * 1e-6, None, ALU.add))
                        chain.link(dve.reciprocal(den[0:n, t, :], den[0:n, t, :]))
                        dve.tensor_tensor(xa[0:n, t, :].rearrange("t (h c) -> t h c", c=DH), ov[:, :, 0:DH],
                                          den[0:n, t, :].unsqueeze(2).to_broadcast([n, HEADS, DH]),
                                          ALU.mult).then_inc(xa_ready, 1)
                chain.end()

            def norms_out(g):
                chain = Chain(dve, ln2_chain, g, 2 * MOMENTS + 9)
                dve.wait_ge(xn_biased, g + 1)
                for t, (t0, n) in enumerate(TILES):
                    dve.wait_ge(proj_mm, 3 * g + t + 1)
                    chain.add(dve.tensor_tensor(xn[0:n, t, :], ps[2 + t][0:n, 0:C2], xn[0:n, t, :], ALU.add))
                chain.wait()
                moments(chain, xn)
                done = chain.n
                for t, (t0, n) in enumerate(TILES):
                    chain.add(dve.scalar_tensor_tensor(h3[0:n, t, :], xn[0:n, t, :], mvar[0:n, t, 0:1], gamma[0:n, :],
                                                       ALU.subtract, ALU.mult))
                for t, (t0, n) in enumerate(TILES):
                    chain.wait(done + t + 1)
                    chain.add(dve.scalar_tensor_tensor(h3[0:n, t, :], h3[0:n, t, :], rstd[0:n, t:t + 1], h2[0:n, t, :],
                                                       ALU.mult, ALU.add))
                chain.wait()
                moments(chain, h3)
                for t, (t0, n) in enumerate(TILES):
                    norm(t, n, xa, h3).then_inc(xf_ready, 1)
                chain.end()

            def gate_copy(g):
                dve.wait_ge(rt_mm, g + 1)
                for t, (t0, n) in enumerate(TILES):
                    ins = dve.tensor_copy(rt[0:n, t, :], ps[2][0:n, 4 * t:4 * t + 3])
                ins.then_inc(rt_copied, 1)

            def gate_logits(g):
                chain = Chain(dve, logit_chain, g, 3 + 1)
                dve.wait_ge(logit_mm, g + 1)
                for t, (t0, n) in enumerate(TILES):
                    chain.add(dve.tensor_copy(logit[0:n, t, :], ps[3][0:n, 4 * t:4 * t + 3]))
                chain.wait()
                chain.link(dve.tensor_reduce(rmax[:, :], logit[:, :, :], AX.X, ALU.max))
                dve.tensor_tensor(logit[:, :, :], logit[:, :, :], rmax[:, :].unsqueeze(2).to_broadcast([TT, 3, EXPERTS]),
                                  ALU.subtract).then_inc(logit_ready, 1)
                chain.end()

            def gate(g):
                chain = Chain(dve, gate_chain, g, 9)
                dve.wait_ge(prob_exp, g + 1)
                chain.link(dve.tensor_reduce(rsum[:, :], prob[:, :, :], AX.X, ALU.add))
                chain.link(dve.reciprocal(rsum[:, :], rsum[:, :]))
                chain.link(dve.tensor_tensor(prob[:, :, :], prob[:, :, :], rsum[:, :].unsqueeze(2).to_broadcast([TT, 3, EXPERTS]), ALU.mult))
                chain.link(dve.tensor_reduce(rmax[:, :], prob[:, :, :], AX.X, ALU.max))
                chain.link(dve.tensor_tensor(hot[:, :, :], prob[:, :, :], rmax[:, :].unsqueeze(2).to_broadcast([TT, 3, EXPERTS]), ALU.is_ge))
                chain.link(dve.tensor_tensor(hot[:, :, 1], hot[:, :, 1], hot[:, :, 0], ALU.is_gt))
                chain.link(dve.tensor_tensor(rmax[:, :], hot[:, :, 0], hot[:, :, 1], ALU.add))
                chain.link(dve.tensor_tensor(hot[:, :, 2], hot[:, :, 2], rmax[:, :], ALU.is_gt))
                chain.link(dve.tensor_tensor(gates[:, :, :], prob[:, :, :], hot[:, :, :], ALU.mult))
                chain.end()

            def add_expert(g, e):
                if e == 0:
                    dve.wait_ge(stored, 48 * g + 1)
                for t, (t0, n) in enumerate(TILES):
                    if e > 0:
                        dve.wait_ge(y_added, 9 * g + (3 * e + t - 2))
                    dve.scalar_tensor_tensor(y[0:n, t, :], b_down[0:n, e, :], gates[0:n, t, e:e + 1],
                                             (h3 if e == 0 else y)[0:n, t, :], ALU.mult, ALU.add).then_inc(y_biased, 1)
                for t, (t0, n) in enumerate(TILES):
                    u = 3 * e + t
                    dve.wait_ge(down_mm, 9 * g + u + 1)
                    dve.wait_ge(y_biased, 9 * g + u + 1)
                    dve.scalar_tensor_tensor(y[0:n, t, :], ps[DOWN_BANKS[e][t]][0:n, 0:C2], gates[0:n, t, e:e + 1],
                                             y[0:n, t, :], ALU.mult, ALU.add).then_inc(y_added, 1)

            dve.wait_ge(nat_mm, 1)
            dve.tensor_copy(w_stem[:, :, :], ps[5][0:96, 0:192]).then_inc(nat_evac, 1)
            chain = Chain(dve, bn_chain, 0, 2 + RSQRT + 3)
            chain.link(dve.tensor_copy(bn[:, :, :], ps[5][0:96, 192:207]))
            chain.link(dve.tensor_scalar(bn_tmp[:, 0, :], bn[:, 4, :], EPS, None, ALU.add))
            rsqrt(chain, bn_scale[:, :], bn_tmp[:, 0, :], bn_tmp[:, 1, :].bitcast(I32), bn_bias[:, :])
            chain.link(dve.tensor_tensor(bn_scale[:, :], bn_scale[:, :], bn[:, 1, :], ALU.mult))
            chain.link(dve.tensor_tensor(bn_bias[:, :], bn[:, 0, :], bn[:, 3, :], ALU.subtract))
            chain.link(dve.tensor_tensor(bn_bias[:, :], bn_bias[:, :], bn_scale[:, :], ALU.mult))
            dve.tensor_tensor(bn_bias[:, :], bn_bias[:, :], bn[:, 2, :], ALU.add).then_inc(bn_ready, 1)
            chain.end()
            stem_xt(0)
            dve.wait_ge(nat_mm, 2)
            dve.tensor_copy(w_off[:, :, :], ps[6][0:C1, 0:512]).then_inc(nat_evac, 1)
            dve.wait_ge(nat_mm, 3)
            dve.wait_ge(ld_small, 16 * 8)
            dve.tensor_copy(w_gate[:, :, :], ps[7][0:96, 0:8].rearrange("p (t e) -> p t e", t=2)[:, :, 0:3])
            dve.tensor_copy(b_up[:, :], ps[7][:, 32:32 + EXPERTS * FCH])
            dve.tensor_tensor(w_feat[0:64, :].rearrange("p (h m) -> p h m", h=4),
                              ps[7][0:64, 64:128].unsqueeze(1).to_broadcast([64, 4, M]),
                              headmask[:, :].rearrange("p (h m) -> p h m", h=4), ALU.mult).then_inc(nat_evac, 1)
            dve.wait_ge(zeroed, 5)
            for s in range(2):
                leaky(0, s)
                stem_ht(0, s)
            part_copy(0)
            dve.wait_ge(ld_offb, 16 * 6)
            dve.tensor_tensor(point[:, :], point[:, :], offb[:, :], ALU.add).then_inc(point_ready, 1)
            dve.wait_ge(point_ready, 1)
            sample_points(0)
            for t in range(3):
                ones = mv[:, t, :, :].rearrange("t i (h c) -> t i h c", c=VW)[:, :, :, DH]
                ins = dve.tensor_copy(ones, own[:, :].unsqueeze(2).to_broadcast([TT, 3, HEADS]))
            ins.then_inc(feat_ready, 1)

            def step(g, has_last, has_next):
                if has_last:
                    gate_logits(g - 1)
                    combine(g, 2, 6)
                    gate(g - 1)
                    combine(g, 6, 8)
                    add_expert(g - 1, 0)
                    combine(g, 8, BATCHES)
                    add_expert(g - 1, 1)
                else:
                    combine(g, 2, BATCHES)
                    leaky(g + 1, 0)
                    leaky(g + 1, 1)
                dcn_leaky(g, 0)
                if has_last and has_next:
                    stem_xt(g + 1, 0, 2)
                dcn_leaky(g, 1)
                if has_last and has_next:
                    stem_xt(g + 1, 2, 3)
                if not has_last:
                    dve.wait_ge(ld_attn, 16 * 29)
                token_copies(g)
                if not has_last:
                    stem_ht(g + 1, 0)
                norm_in(g)
                if has_last and has_next:
                    leaky(g + 1, 0)
                    for j in range(3):
                        leaky(g + 1, 1, j, j + 1)
                        stem_ht(g + 1, 0, 2 * j + 1, 2 * j + 2)
                if has_next:
                    stem_ht(g + 1, 1)
                    part_copy(g + 1)
                    sample_points(g + 1)
                add_biases(g)
                q_copies(g, 0, 2)
                values(g, 0, 2)
                q_copies(g, 2, 4)
                values(g, 2, 3)
                q_copies(g, 4, 6)
                kv_low(g)
                outputs(g)
                norms_out(g)
                if has_next:
                    combine(g + 1, 0, 1)
                if has_last:
                    add_expert(g - 1, 2)
                gate_copy(g)
                if has_next:
                    combine(g + 1, 1, 2)
                if not has_last:
                    dve.wait_ge(ld_ffn, 16 * 6)

            stem_xt(1)
            combine(0, 0, 2)
            steps(dve, step)
            gate_logits(GROUPS - 1)
            gate(GROUPS - 1)
            for e in range(EXPERTS):
                add_expert(GROUPS - 1, e)


_INS = ["x", "L0_tok_stem_w", "L0_tok_stem_b", "L0_tok_bn1_g", "L0_tok_bn1_b", "L0_tok_bn1_m", "L0_tok_bn1_v",
        "L0_tok_off_w", "L0_tok_off_b", "L0_tok_dcn_w", "L0_tok_dcn_b", "L0_tok_bn2_g", "L0_tok_bn2_b", "L0_tok_bn2_m",
        "L0_tok_bn2_v", "L0_attn_W_qkv", "L0_attn_W_proj", "L0_attn_b_proj", "L0_attn_gamma", "L0_attn_beta",
        "L0_attn_random_features", "L0_ffn_Wg", "L0_ffn_W1", "L0_ffn_b1", "L0_ffn_W2", "L0_ffn_b2"]


def kernel(**inputs):
    import numpy as _np
    import concourse.bacc as _bacc
    from concourse import mybir as _mybir
    from concourse.bass_utils import run_bass_kernel_spmd as _run

    nc = _bacc.Bacc("TRN2", target_bir_lowering=False, num_devices=1)
    arrays, aps = {}, {}
    for name in _INS:
        x = _np.ascontiguousarray(inputs[name])
        arrays[f"in_{name}_dram"] = x
        aps[name] = nc.dram_tensor(f"in_{name}_dram", x.shape, _mybir.dt.from_np(x.dtype), kind="ExternalInput").ap()
    for name, x in tables().items():
        arrays[f"table_{name}_dram"] = x
        aps[name] = nc.dram_tensor(f"table_{name}_dram", x.shape, _mybir.dt.from_np(x.dtype), kind="ExternalInput").ap()
    out = nc.dram_tensor("out_0_dram", (IMAGES, TOK_IMG, C2), _mybir.dt.float32, kind="ExternalOutput").ap()
    build(nc, aps, out)
    r = _run(nc, [arrays], core_ids=[0])
    return r.results[0]["out_0_dram"]
```
